# Optimizing a Trainium2 kernel written in Bass

```python
import numpy as np
import jax
import jax.numpy as jnp

def _softmax(x, axis=-1):
    return jax.nn.softmax(x, axis=axis)

def _gelu(x):
    return jax.nn.gelu(x, approximate=True)

def _silu(x):
    return jax.nn.silu(x)

def _sigmoid(x):
    return jax.nn.sigmoid(x)

def _layernorm(x, axis=-1, eps=1e-05):
    m = jnp.mean(x, axis=axis, keepdims=True)
    v = jnp.var(x, axis=axis, keepdims=True)
    return (x - m) / jnp.sqrt(v + eps)

def _scatter_add(tgt, idx, src, axis=0):
    return tgt.at[idx].add(src)

def _segment_sum(src, seg, n):
    return jax.ops.segment_sum(src, seg, n)
kernel_name = 'mk_seq_preln_d2_jaxref_r8_85c4ad'

def setup_inputs(seed: int=0):
    np.random.seed(seed)
    _w = jnp.asarray

    def _L0_attn_setup():
        import jax, jax.numpy as jnp
        import numpy as np
        B, L, D = (2, 256, 128)
        H = 16
        HD = D // H
        TOP_FRAC = 0.2
        key = jax.random.key(seed)
        ks = jax.random.split(key, 9)
        s = 1.0 / np.sqrt(D)
        return {'x': jax.random.normal(ks[0], (B, L, D), dtype=jnp.float32), 'Wq': jax.random.normal(ks[1], (D, D), dtype=jnp.float32) * s, 'bq': jnp.zeros((D,), jnp.float32), 'Wk': jax.random.normal(ks[2], (D, D), dtype=jnp.float32) * s, 'bk': jnp.zeros((D,), jnp.float32), 'Wv': jax.random.normal(ks[3], (D, D), dtype=jnp.float32) * s, 'bv': jnp.zeros((D,), jnp.float32), 'Wo': jax.random.normal(ks[4], (D, D), dtype=jnp.float32) * s, 'bo': jnp.zeros((D,), jnp.float32)}
    _L0_attn_in = _L0_attn_setup()

    def _L0_ffn_setup():
        import jax, jax.numpy as jnp
        import numpy as np
        D_MODEL = 128
        D1, D2 = (32, 32)
        F1, F2 = (64, 64)
        E = 64
        TOP_K = 2

        def kmoe(x_flat, W_router, A, B, scale, bias, d_in1, d_in2, d_out1, d_out2, top_k):
            logits = x_flat @ W_router.T
            vals, idx = jax.lax.top_k(logits, top_k)
            probs = jax.nn.softmax(vals, axis=-1)
            xs = x_flat.reshape(-1, d_in1, d_in2)
            Ag = A[idx]
            Bg = B[idx]
            Y = jnp.einsum('nkoi,nij,nkpj->nkop', Ag, xs, Bg)
            out = jnp.einsum('nkop,nk->nop', Y, probs).reshape(-1, d_out1 * d_out2)
            return out * scale + bias
        key = jax.random.key(seed)
        ks = jax.random.split(key, 12)
        s = 0.02
        return {'x': jax.random.normal(ks[0], (4, 256, D_MODEL), dtype=jnp.float32), 'W_up': jax.random.normal(ks[1], (E, D1 * D2), dtype=jnp.float32) * s, 'A_up': jax.random.normal(ks[2], (E, F1, D1), dtype=jnp.float32) * s, 'B_up': jax.random.normal(ks[3], (E, F2, D2), dtype=jnp.float32) * s, 'scale_up': jnp.ones((1,), dtype=jnp.float32), 'bias_up': jnp.zeros((F1 * F2,), dtype=jnp.float32), 'W_down': jax.random.normal(ks[4], (E, F1 * F2), dtype=jnp.float32) * s, 'A_down': jax.random.normal(ks[5], (E, D1, F1), dtype=jnp.float32) * s, 'B_down': jax.random.normal(ks[6], (E, D2, F2), dtype=jnp.float32) * s, 'scale_down': jnp.ones((1,), dtype=jnp.float32), 'bias_down': jnp.zeros((D1 * D2,), dtype=jnp.float32)}
    _L0_ffn_in = _L0_ffn_setup()

    def _L1_attn_setup():
        import jax, jax.numpy as jnp
        import numpy as np
        import math
        B, L, D, H = (4, 512, 128, 16)
        d = D // H

        def _stp_forward(x, Wqkv_w, Wqkv_b, out_w, out_b, W_static, Lambda_raw, Gamma):
            b, l, dm = x.shape
            scale = 1.0 / math.sqrt(d)
            qkv = x @ Wqkv_w.T + Wqkv_b
            qkv = qkv.reshape(b, l, 3, H, d)
            qkv = jnp.transpose(qkv, (2, 0, 3, 1, 4))
            q, k, v = (qkv[0], qkv[1], qkv[2])
            k = k * scale
            retention = 1.0 - jax.nn.sigmoid(Lambda_raw)
            qs = jnp.moveaxis(q, 2, 0)
            ks_ = jnp.moveaxis(k, 2, 0)
            vs = jnp.moveaxis(v, 2, 0)

            def step(state, qkv_t):
                q_t, k_t, v_t = qkv_t
                hebbian = jnp.einsum('bhi,bhj->bhij', v_t, k_t)
                state = retention[None] * state + Gamma[None] * hebbian
                y_t = jnp.einsum('bhij,bhj->bhi', W_static[None] + state, q_t)
                return (state, y_t)
            state0 = jnp.zeros((b, H, d, d), dtype=x.dtype)
            _, ys = jax.lax.scan(step, state0, (qs, ks_, vs))
            y = jnp.transpose(ys, (1, 0, 2, 3)).reshape(b, l, dm)
            return y @ out_w.T + out_b
        key = jax.random.key(seed)
        ks = jax.random.split(key, 8)
        s = 0.02
        x = jax.random.normal(ks[0], (B, L, D), dtype=jnp.float32)
        Wqkv_w = jax.random.normal(ks[1], (3 * D, D), dtype=jnp.float32) * s
        Wqkv_b = jnp.zeros((3 * D,), dtype=jnp.float32)
        out_w = jax.random.normal(ks[2], (D, D), dtype=jnp.float32) * s
        out_b = jnp.zeros((D,), dtype=jnp.float32)
        W_static = jax.random.normal(ks[3], (H, d, d), dtype=jnp.float32) * s
        Lambda_raw = jax.random.uniform(ks[4], (H, d, d), dtype=jnp.float32, minval=-3.0, maxval=3.0)
        g = 0.5 / math.sqrt(d)
        Gamma = jax.random.uniform(ks[5], (H, d, d), dtype=jnp.float32, minval=-g, maxval=g)
        return {'x': x, 'Wqkv_w': Wqkv_w, 'Wqkv_b': Wqkv_b, 'out_w': out_w, 'out_b': out_b, 'W_static': W_static, 'Lambda_raw': Lambda_raw, 'Gamma': Gamma}
    _L1_attn_in = _L1_attn_setup()

    def _L1_ffn_setup():
        import jax, jax.numpy as jnp
        import numpy as np
        DIM = 128
        HIDDEN = 384
        SCALE = 1.0 / 127.0

        def _dequant(w_int, dtype):
            return w_int.astype(dtype) * jnp.asarray(SCALE, dtype)
        key = jax.random.key(seed)
        k_x, k_g, k_u, k_d = jax.random.split(key, 4)
        x = jax.random.normal(k_x, (4, 256, DIM), dtype=jnp.float32)
        w_gate = jax.random.randint(k_g, (HIDDEN, DIM), -127, 128, dtype=jnp.int32)
        w_up = jax.random.randint(k_u, (HIDDEN, DIM), -127, 128, dtype=jnp.int32)
        w_down = jax.random.randint(k_d, (DIM, HIDDEN), -127, 128, dtype=jnp.int32)
        return {'x': x, 'w_gate': w_gate, 'w_up': w_up, 'w_down': w_down}
    _L1_ffn_in = _L1_ffn_setup()
    _d = {'L0_attn_x': _L0_attn_in['x'], 'L0_attn_Wq': _L0_attn_in['Wq'], 'L0_attn_bq': _L0_attn_in['bq'], 'L0_attn_Wk': _L0_attn_in['Wk'], 'L0_attn_bk': _L0_attn_in['bk'], 'L0_attn_Wv': _L0_attn_in['Wv'], 'L0_attn_bv': _L0_attn_in['bv'], 'L0_attn_Wo': _L0_attn_in['Wo'], 'L0_attn_bo': _L0_attn_in['bo'], 'L0_ffn_W_up': _L0_ffn_in['W_up'], 'L0_ffn_A_up': _L0_ffn_in['A_up'], 'L0_ffn_B_up': _L0_ffn_in['B_up'], 'L0_ffn_scale_up': _L0_ffn_in['scale_up'], 'L0_ffn_bias_up': _L0_ffn_in['bias_up'], 'L0_ffn_W_down': _L0_ffn_in['W_down'], 'L0_ffn_A_down': _L0_ffn_in['A_down'], 'L0_ffn_B_down': _L0_ffn_in['B_down'], 'L0_ffn_scale_down': _L0_ffn_in['scale_down'], 'L0_ffn_bias_down': _L0_ffn_in['bias_down'], 'L1_attn_Wqkv_w': _L1_attn_in['Wqkv_w'], 'L1_attn_Wqkv_b': _L1_attn_in['Wqkv_b'], 'L1_attn_out_w': _L1_attn_in['out_w'], 'L1_attn_out_b': _L1_attn_in['out_b'], 'L1_attn_W_static': _L1_attn_in['W_static'], 'L1_attn_Lambda_raw': _L1_attn_in['Lambda_raw'], 'L1_attn_Gamma': _L1_attn_in['Gamma'], 'L1_ffn_w_gate': _L1_ffn_in['w_gate'], 'L1_ffn_w_up': _L1_ffn_in['w_up'], 'L1_ffn_w_down': _L1_ffn_in['w_down']}
    _x0 = _d['L0_attn_x']
    _d['L0_attn_x'] = jax.random.normal(jax.random.fold_in(jax.random.key(seed), 1), (8, 512, 128), dtype=_x0.dtype)
    del _x0
    return _d

def reference(L0_attn_x, L0_attn_Wq, L0_attn_bq, L0_attn_Wk, L0_attn_bk, L0_attn_Wv, L0_attn_bv, L0_attn_Wo, L0_attn_bo, L0_ffn_W_up, L0_ffn_A_up, L0_ffn_B_up, L0_ffn_scale_up, L0_ffn_bias_up, L0_ffn_W_down, L0_ffn_A_down, L0_ffn_B_down, L0_ffn_scale_down, L0_ffn_bias_down, L1_attn_Wqkv_w, L1_attn_Wqkv_b, L1_attn_out_w, L1_attn_out_b, L1_attn_W_static, L1_attn_Lambda_raw, L1_attn_Gamma, L1_ffn_w_gate, L1_ffn_w_up, L1_ffn_w_down):

    def _L0_attn_ref(x, Wq, bq, Wk, bk, Wv, bv, Wo, bo):
        import jax, jax.numpy as jnp
        import numpy as np
        B, L, D = (2, 256, 128)
        H = 16
        HD = D // H
        TOP_FRAC = 0.2
        b, l, d = x.shape
        scale = HD ** (-0.5)
        k_top = max(1, int(l * TOP_FRAC))

        def split_heads(t):
            return t.reshape(b, l, H, HD).transpose(0, 2, 1, 3)
        q = split_heads(x @ Wq.T + bq)
        k = split_heads(x @ Wk.T + bk)
        v = split_heads(x @ Wv.T + bv)
        q_norm = jnp.sum(q * q, axis=-1)
        _, topk_idx = jax.lax.top_k(q_norm, k_top)
        bi = jnp.arange(b)[:, None, None]
        hi = jnp.arange(H)[None, :, None]
        mask = jnp.zeros((b, H, l), dtype=bool).at[bi, hi, topk_idx].set(True)
        q = q * mask[..., None]
        scores = jnp.einsum('bhqd,bhkd->bhqk', q, k) * scale
        probs = jax.nn.softmax(scores, axis=-1)
        out = jnp.einsum('bhqk,bhkd->bhqd', probs, v)
        out = out.transpose(0, 2, 1, 3).reshape(b, l, d)
        return out @ Wo.T + bo

    def _L0_ffn_ref(x, W_up, A_up, B_up, scale_up, bias_up, W_down, A_down, B_down, scale_down, bias_down):
        import jax, jax.numpy as jnp
        import numpy as np
        D_MODEL = 128
        D1, D2 = (32, 32)
        F1, F2 = (64, 64)
        E = 64
        TOP_K = 2

        def kmoe(x_flat, W_router, A, B, scale, bias, d_in1, d_in2, d_out1, d_out2, top_k):
            logits = x_flat @ W_router.T
            vals, idx = jax.lax.top_k(logits, top_k)
            probs = jax.nn.softmax(vals, axis=-1)
            xs = x_flat.reshape(-1, d_in1, d_in2)
            Ag = A[idx]
            Bg = B[idx]
            Y = jnp.einsum('nkoi,nij,nkpj->nkop', Ag, xs, Bg)
            out = jnp.einsum('nkop,nk->nop', Y, probs).reshape(-1, d_out1 * d_out2)
            return out * scale + bias
        orig_shape = x.shape
        x_flat = x.reshape(-1, D1 * D2)
        h = kmoe(x_flat, W_up, A_up, B_up, scale_up, bias_up, D1, D2, F1, F2, TOP_K)
        h = jax.nn.gelu(h, approximate=False)
        y = kmoe(h, W_down, A_down, B_down, scale_down, bias_down, F1, F2, D1, D2, TOP_K)
        return y.reshape(*orig_shape[:-1], D_MODEL)

    def _L1_attn_ref(x, Wqkv_w, Wqkv_b, out_w, out_b, W_static, Lambda_raw, Gamma):
        import jax, jax.numpy as jnp
        import numpy as np
        import math
        B, L, D, H = (4, 512, 128, 16)
        d = D // H

        def _stp_forward(x, Wqkv_w, Wqkv_b, out_w, out_b, W_static, Lambda_raw, Gamma):
            b, l, dm = x.shape
            scale = 1.0 / math.sqrt(d)
            qkv = x @ Wqkv_w.T + Wqkv_b
            qkv = qkv.reshape(b, l, 3, H, d)
            qkv = jnp.transpose(qkv, (2, 0, 3, 1, 4))
            q, k, v = (qkv[0], qkv[1], qkv[2])
            k = k * scale
            retention = 1.0 - jax.nn.sigmoid(Lambda_raw)
            qs = jnp.moveaxis(q, 2, 0)
            ks_ = jnp.moveaxis(k, 2, 0)
            vs = jnp.moveaxis(v, 2, 0)

            def step(state, qkv_t):
                q_t, k_t, v_t = qkv_t
                hebbian = jnp.einsum('bhi,bhj->bhij', v_t, k_t)
                state = retention[None] * state + Gamma[None] * hebbian
                y_t = jnp.einsum('bhij,bhj->bhi', W_static[None] + state, q_t)
                return (state, y_t)
            state0 = jnp.zeros((b, H, d, d), dtype=x.dtype)
            _, ys = jax.lax.scan(step, state0, (qs, ks_, vs))
            y = jnp.transpose(ys, (1, 0, 2, 3)).reshape(b, l, dm)
            return y @ out_w.T + out_b
        return _stp_forward(x, Wqkv_w, Wqkv_b, out_w, out_b, W_static, Lambda_raw, Gamma)

    def _L1_ffn_ref(x, w_gate, w_up, w_down):
        import jax, jax.numpy as jnp
        import numpy as np
        DIM = 128
        HIDDEN = 384
        SCALE = 1.0 / 127.0

        def _dequant(w_int, dtype):
            return w_int.astype(dtype) * jnp.asarray(SCALE, dtype)
        wg = _dequant(w_gate, x.dtype)
        wu = _dequant(w_up, x.dtype)
        wd = _dequant(w_down, x.dtype)
        gate = jnp.einsum('bsd,hd->bsh', x, wg)
        up = jnp.einsum('bsd,hd->bsh', x, wu)
        h = jax.nn.silu(gate) * up
        return jnp.einsum('bsh,dh->bsd', h, wd)
    x = L0_attn_x
    x = x + _L0_attn_ref(_layernorm(x, axis=-1), L0_attn_Wq, L0_attn_bq, L0_attn_Wk, L0_attn_bk, L0_attn_Wv, L0_attn_bv, L0_attn_Wo, L0_attn_bo)
    x = x + _L0_ffn_ref(_layernorm(x, axis=-1), L0_ffn_W_up, L0_ffn_A_up, L0_ffn_B_up, L0_ffn_scale_up, L0_ffn_bias_up, L0_ffn_W_down, L0_ffn_A_down, L0_ffn_B_down, L0_ffn_scale_down, L0_ffn_bias_down)
    x = x + _L1_attn_ref(_layernorm(x, axis=-1), L1_attn_Wqkv_w, L1_attn_Wqkv_b, L1_attn_out_w, L1_attn_out_b, L1_attn_W_static, L1_attn_Lambda_raw, L1_attn_Gamma)
    x = x + _L1_ffn_ref(_layernorm(x, axis=-1), L1_ffn_w_gate, L1_ffn_w_up, L1_ffn_w_down)
    return x

_drawn_inputs = setup_inputs


def setup_inputs(seed=0):
    import zlib

    import numpy as np

    out = dict(_drawn_inputs(seed))
    spreads = {'L0_attn_bq': (0.0, 0.1),
     'L0_attn_bk': (0.0, 2.0),
     'L0_attn_bv': (0.0, 0.1),
     'L0_attn_bo': (0.0, 0.1),
     'L0_ffn_bias_up': (0.0, 0.8),
     'L0_ffn_bias_down': (0.0, 0.1),
     'L1_attn_Wqkv_b': (0.0, 0.8),
     'L1_attn_out_b': (0.0, 0.8)}
    factors = {'L0_ffn_W_up': 8.0,
     'L0_ffn_A_up': 8.0,
     'L0_ffn_B_up': 8.0,
     'L0_ffn_W_down': 8.0,
     'L0_ffn_A_down': 8.0,
     'L0_ffn_B_down': 8.0,
     'L1_attn_Wqkv_w': 8.0,
     'L1_attn_out_w': 8.0,
     'L1_attn_W_static': 34.369,
     'L1_attn_Lambda_raw': 8.0,
     'L1_attn_Gamma': 8.0}
    for name, (base, spread) in spreads.items():
        noise = np.random.default_rng([zlib.crc32(name.encode()), seed]).standard_normal(out[name].shape)
        drawn = base * np.exp(spread * noise) if base else spread * noise
        out[name] = jnp.asarray(drawn.astype(out[name].dtype))
    for name, factor in factors.items():
        out[name] = (out[name] * factor).astype(out[name].dtype)
    return out
```

```python
import concourse.bass as bass
from concourse import mybir
from concourse.bass import ds
from contextlib import ExitStack

P = 128
B, L = 8, 512
N = B * L
TPS = L // P
NT = N // P
H, HD = 16, 8
KTOP = int(L * 0.2)
ROUNDS = -(-KTOP // 8)
LAST = KTOP - 8 * (ROUNDS - 1)
QPART = [0, 0, 0, 1, 1, 2]
KPART = [0, 1, 2, 0, 1, 0]
NPROD = len(QPART)
KROWS = NPROD * HD
QSCALE = float(HD) ** -0.5
NEXP, TOPK = 64, 2
ROWTOK = 8
SROWS = 128
STOK = SROWS * ROWTOK
TPU = STOK // P
NS = N // STOK
G4 = 4
NG = SROWS // G4
NQ = NG // 4
HM = 3
EPS = 1e-5

F32 = mybir.dt.float32
BF16 = mybir.dt.bfloat16
I32 = mybir.dt.int32
U32 = mybir.dt.uint32
ALU = mybir.AluOpType
ACT = mybir.ActivationFunctionType
AX = mybir.AxisListType


class Sig:

    def __init__(self, sem, per=1, given=True):
        self.sem, self.per, self.given = sem, per, given

    def seed(self, eng):
        if self.given:
            eng.sem_inc(self.sem, self.per)

    def at(self, turn, k=None):
        return (turn + self.given) * self.per + (self.per if k is None else k)

    def before(self, turn, k=None):
        assert self.given
        return turn * self.per + (self.per if k is None else k)


class Room:

    def __init__(self, nc, ctx, name):
        self.nc, self.ctx, self.name = nc, ctx, name
        self.sigs, self.sems = [], []

    def sb(self, name, shape, dt=F32):
        return self.ctx.enter_context(self.nc.sbuf_tensor(self.name + name, shape, dt))

    def ps(self, name, shape, dt=F32):
        return self.ctx.enter_context(self.nc.psum_tensor(self.name + name, shape, dt))

    def sem(self, name):
        self.sems.append(self.ctx.enter_context(self.nc.semaphore(self.name + name)))
        return self.sems[-1]

    def clear(self):
        self.nc.gpsimd.drain()
        for s in self.sems:
            self.nc.gpsimd.sem_clear(s)
        self.nc.all_engine_barrier()

    def sig(self, name, per=1, given=True):
        self.sigs.append(Sig(self.sem(name), per, given))
        return self.sigs[-1]

    def seed(self, eng):
        for s in self.sigs:
            s.seed(eng)


def one(ap):
    if len(ap.shape) == 3:
        return ap.rearrange("p o c -> p (o c)")
    return ap.rearrange("p o t c -> p (o t) c")


def load(nc, c, a):
    with ExitStack() as ctx:
        r = Room(nc, ctx, "ld_")
        s_in, s_int = r.sem("in"), r.sem("int")
        ints = r.sb("ints", [P, 3 * HM * P], I32)
        ctx.callback(r.clear)
        block = ctx.enter_context(nc.Block())
        loads = [
            (c.X[:, :, :], a["x"].rearrange("(t p) c -> p t c", p=P)),
            (c.consts[:, :], a["consts"]),
            (c.W[:, 0, :], a["WqT"]), (c.W[:, 1, :], a["WkT"]), (c.W[:, 2, :], a["WvT"]), (c.W[:, 3, :], a["WoT"]),
            (c.rows[:, 0, :], a["bq"].partition_broadcast(P)), (c.rows[:, 1, :], a["bv"].partition_broadcast(P)),
            (c.rows[:, 2, :], a["bo"].partition_broadcast(P)), (c.rows[:, 3, :], a["out_b"].partition_broadcast(P)),
            (c.cols[:, 0:1], a["bk"]),
            (ints[:, 0:HM * P], a["w_gateT"]), (ints[:, HM * P:2 * HM * P], a["w_upT"]),
            (ints[:, 2 * HM * P:].rearrange("p (m c) -> p m c", m=HM), a["w_downT"].rearrange("(m p) c -> p m c", p=P)),
            (c.WupR[:, :], a["WupR"]), (c.WdR[:, :], a["WdR"]),
            (c.scales[:, 0:1], a["scale_up"].partition_broadcast(P)),
            (c.scales[:, 1:2], a["scale_down"].partition_broadcast(P)),
            (c.Wqkv[:, :], a["WqkvT"]), (c.outW[:, :], a["out_wT"]), (c.bqkv[:, :], a["bqkv"]),
            (c.stp[:, :], a["stp"]),
        ] + [(c.bup[32 * i:32 * i + 32, :], a["bias_up"]) for i in range(4)] \
          + [(c.bdn[32 * i:32 * i + 32, :], a["bias_down"]) for i in range(4)]

        @block.sync
        def _(sp):
            for dst, src in loads:
                sp.dma_start(dst, src).then_inc(s_in, 16)

        @block.vector
        def _(dve):
            nc.vector.memset(c.mean_ones[:, :], 1.0 / L)
            nc.vector.memset(c.ones[:, :], 1.0)
            nc.vector.memset(c.eps[:, :], EPS)
            dve.wait_ge(s_in, 16 * len(loads))
            nc.vector.tensor_copy(c.Wint[:, :], ints[:, :]).then_inc(s_int, 1)
            nc.vector.tensor_copy(c.iota1[:, :], c.consts[:, P:2 * P])
            dve.wait_ge(s_int, 1)
            nc.vector.tensor_scalar(c.Wint[:, :], c.Wint[:, :], 1.0 / 127.0, None, ALU.mult).then_inc(s_int, 1)
            dve.wait_ge(s_int, 2)


def attention_projections(nc, c, kd, qd):
    with ExitStack() as ctx:
        r = Room(nc, ctx, "a1_")
        stats, mv = r.sb("stats", [P, NT, 6]), r.sb("mv", [P, NT, 2])
        std, rstd = r.sb("std", [P, NT]), r.sb("rstd", [P, NT])
        xn = r.sb("xn", [P, TPS, P])
        xnT = r.sb("xnT", [P, L])
        q, q2, qs = r.sb("q", [P, L]), r.sb("q2", [P, L]), r.sb("qs", [P, L])
        qp = r.sb("qp", [P, 3, L], BF16)
        qres = r.sb("qres", [P, L])
        kres = r.sb("kres", [P, L])
        k3 = r.sb("k3", [P, 3, L], BF16)
        vcur = r.sb("vcur", [P, L])
        q6 = r.sb("q6", [P, TPS * H * KROWS], BF16)
        q_stored = r.sig("q6st", 16)
        psT, psK, psQ, psV = (r.ps(n, [P, L]) for n in ("psT", "psK", "psQ", "psV"))
        psM = r.ps("psM", [P, 512])
        s_stats, s_var, s_std, s_rstd = (r.sem(n) for n in ("stats", "var", "std", "rstd"))
        xn_ready, t_done, xnT_ready = r.sig("xn"), r.sig("t"), r.sig("xnT")
        k_done, q_done, v_done, m_done = r.sig("k"), r.sig("q"), r.sig("v"), r.sig("m")
        khi, kres_ready, kmid, klo = r.sig("khi"), r.sig("kres"), r.sig("kmid"), r.sig("klo")
        k_stored = r.sig("kst", 16)
        q_ready, q2_ready, qs_ready, qn_ready = r.sig("qf"), r.sig("q2"), r.sig("qs"), r.sig("qn")
        qhi, qres_ready, qmid, qlo, q_copied = r.sig("qhi"), r.sig("qres"), r.sig("qmid"), r.sig("qlo"), r.sig("qcp")
        v_ready, v_stored, mean_ready = r.sig("vf"), r.sig("vst", 16), r.sig("mean")
        bq_row = c.rows[:, 0, :].unsqueeze(1).to_broadcast([P, TPS, P])
        bv_row = c.rows[:, 1, :].unsqueeze(1).to_broadcast([P, TPS, P])
        gate = r.sb("gate", [P, 1])
        ctx.callback(r.clear)
        block = ctx.enter_context(nc.Block())

        def tiles(ap):
            return ap.rearrange("p (t c) -> p t c", c=P)

        @block.sync
        def _(sp):
            with sp.Fori(0, B) as b:
                sp.wait_ge(klo.sem, klo.at(b))
                sp.dma_start(kd[ds(b, 1), :, :, :].rearrange("o p c t -> (o p) c t"),
                             k3[:, :, :]).then_inc(k_stored.sem, 16)
                sp.wait_ge(v_ready.sem, v_ready.at(b))
                sp.dma_start(one(c.V[:, ds(b, 1), :]), vcur[:, :]).then_inc(v_stored.sem, 16)
                sp.wait_ge(q_copied.sem, q_copied.at(b))
                sp.dma_start(one(qd[ds(b, 1), :, :].rearrange("o p n -> p o n")), q6[:, :]).then_inc(q_stored.sem, 16)
            sp.wait_ge(k_stored.sem, k_stored.at(B - 1))
            sp.wait_ge(q_stored.sem, q_stored.at(B - 1))
            sp.wait_ge(v_stored.sem, v_stored.at(B - 1))

        @block.tensor
        def _(pe):
            with pe.Fori(0, B) as b:
                pe.wait_ge(xn_ready.sem, xn_ready.at(b))
                pe.wait_ge(xnT_ready.sem, xnT_ready.before(b))
                for t in range(TPS):
                    last = nc.tensor.transpose(psT[:, t * P:(t + 1) * P], xn[:, t, :], c.ident)
                last.then_inc(t_done.sem, 1)
                pe.wait_ge(xnT_ready.sem, xnT_ready.at(b))
                pe.wait_ge(kres_ready.sem, kres_ready.before(b))
                nc.tensor.matmul(psK[:, :], c.W[:, 1, :], xnT[:, :], start=True, stop=True).then_inc(k_done.sem, 1)
                pe.wait_ge(q_ready.sem, q_ready.before(b))
                for t in range(TPS):
                    last = nc.tensor.matmul(psQ[:, t * P:(t + 1) * P], xnT[:, t * P:(t + 1) * P], c.W[:, 0, :],
                                            start=True, stop=True)
                last.then_inc(q_done.sem, 1)
                pe.wait_ge(v_ready.sem, v_ready.before(b))
                for t in range(TPS):
                    last = nc.tensor.matmul(psV[:, t * P:(t + 1) * P], xnT[:, t * P:(t + 1) * P], c.W[:, 2, :],
                                            start=True, stop=True)
                last.then_inc(v_done.sem, 1)
                pe.wait_ge(v_ready.sem, v_ready.at(b))
                pe.wait_ge(mean_ready.sem, mean_ready.before(b))
                for t in range(TPS):
                    last = nc.tensor.matmul(psM[:, 0:P], c.mean_ones[:, :], vcur[:, t * P:(t + 1) * P],
                                            start=(t == 0), stop=(t == TPS - 1))
                last.then_inc(m_done.sem, 1)

        @block.scalar
        def _(act):
            act.wait_ge(s_var, 1)
            nc.scalar.activation(std[:, :], mv[:, :, 1], ACT.Sqrt, bias=c.eps[:, :], scale=1.0).then_inc(s_std, 1)
            with act.Fori(0, B) as b:
                act.wait_ge(t_done.sem, t_done.at(b))
                act.wait_ge(m_done.sem, m_done.before(b))
                nc.scalar.activation(xnT[:, :], psT[:, :], ACT.Copy).then_inc(xnT_ready.sem, 1)
                act.wait_ge(k_done.sem, k_done.at(b))
                act.wait_ge(k_stored.sem, k_stored.before(b))
                nc.scalar.activation(k3[:, 0, :], psK[:, :], ACT.Identity, bias=c.cols[:, 0:1]).then_inc(khi.sem, 1)
                act.wait_ge(q_ready.sem, q_ready.at(b))
                act.wait_ge(qn_ready.sem, qn_ready.before(b))
                nc.scalar.activation(q2[:, :], q[:, :], ACT.Square).then_inc(q2_ready.sem, 1)
                act.wait_ge(kres_ready.sem, kres_ready.at(b))
                nc.scalar.activation(k3[:, 1, :], kres[:, :], ACT.Copy).then_inc(kmid.sem, 1)
                act.wait_ge(qs_ready.sem, qs_ready.at(b))
                act.wait_ge(q_copied.sem, q_copied.before(b))
                nc.scalar.activation(qp[:, 0, :], qs[:, :], ACT.Copy).then_inc(qhi.sem, 1)
                act.wait_ge(qres_ready.sem, qres_ready.at(b))
                nc.scalar.activation(qp[:, 1, :], qres[:, :], ACT.Copy).then_inc(qmid.sem, 1)
                act.wait_ge(m_done.sem, m_done.at(b))
                nc.scalar.activation(one(c.VM[:, ds(b, 1), :]), psM[:, 0:P], ACT.Copy).then_inc(mean_ready.sem, 1)

        @block.gpsimd
        def _(pool):
            r.seed(pool)
            with pool.Fori(0, B) as b:
                pool.wait_ge(kmid.sem, kmid.at(b))
                nc.gpsimd.tensor_tensor(k3[:, 2, :], kres[:, :], k3[:, 1, :], ALU.subtract).then_inc(klo.sem, 1)
                pool.wait_ge(qlo.sem, qlo.at(b))
                pool.wait_ge(q_stored.sem, q_stored.before(b))
                nc.gpsimd.tensor_tensor(gate[:, :], c.ones[:, :], c.ones[:, :], ALU.mult)
                rows = q6[:, :].rearrange("p (a c d) -> p a c d", c=NPROD, d=HD)
                for n in range(NPROD):
                    last = nc.gpsimd.tensor_copy(rows[:, :, n, :],
                                                 qp[:, QPART[n], :].rearrange("p (a d) -> p a d", d=HD))
                last.then_inc(q_copied.sem, 1)

        @block.vector
        def _(dve):
            for t in range(NT):
                last = nc.vector.bn_stats(stats[:, t, :], c.X[:, t, :])
            last.then_inc(s_stats, 1)
            dve.wait_ge(s_stats, 1)
            for t in range(NT):
                last = nc.vector.bn_aggr(mv[:, t, :], stats[:, t, :])
            last.then_inc(s_var, 1)
            dve.wait_ge(s_std, 1)
            nc.vector.reciprocal(rstd[:, :], std[:, :]).then_inc(s_rstd, 1)
            dve.wait_ge(s_rstd, 1)
            with dve.Fori(0, B) as b:
                dve.wait_ge(t_done.sem, t_done.before(b))
                for t in range(TPS):
                    j = b * TPS + t
                    last = nc.vector.tensor_scalar(xn[:, t, :], one(c.X[:, ds(j, 1), :]), one(mv[:, ds(j, 1), 0:1]),
                                                   rstd[:, ds(j, 1)], ALU.subtract, ALU.mult)
                last.then_inc(xn_ready.sem, 1)
                dve.wait_ge(khi.sem, khi.at(b))
                dve.wait_ge(klo.sem, klo.before(b))
                nc.vector.scalar_tensor_tensor(kres[:, :], psK[:, :], c.cols[:, 0:1], k3[:, 0, :],
                                               ALU.add, ALU.subtract).then_inc(kres_ready.sem, 1)
                dve.wait_ge(q_done.sem, q_done.at(b))
                dve.wait_ge(q2_ready.sem, q2_ready.before(b))
                nc.vector.tensor_tensor(tiles(q[:, :]), tiles(psQ[:, :]), bq_row, ALU.add).then_inc(q_ready.sem, 1)
                dve.wait_ge(v_done.sem, v_done.at(b))
                dve.wait_ge(v_stored.sem, v_stored.before(b))
                dve.wait_ge(m_done.sem, m_done.before(b))
                nc.vector.tensor_tensor(tiles(vcur[:, :]), tiles(psV[:, :]), bv_row, ALU.add).then_inc(v_ready.sem, 1)
                dve.wait_ge(q_ready.sem, q_ready.at(b))
                dve.wait_ge(qres_ready.sem, qres_ready.before(b))
                nc.vector.tensor_scalar(qs[:, :], q[:, :], QSCALE, None, ALU.mult).then_inc(qs_ready.sem, 1)
                dve.wait_ge(q2_ready.sem, q2_ready.at(b))
                nc.vector.tensor_reduce(c.QN[:, :, ds(b * H, H)], q2[:, :].rearrange("p (t h d) -> p t h d", h=H, d=HD),
                                        AX.X, ALU.add).then_inc(qn_ready.sem, 1)
                dve.wait_ge(qhi.sem, qhi.at(b))
                dve.wait_ge(qlo.sem, qlo.before(b))
                nc.vector.tensor_tensor(qres[:, :], qs[:, :], qp[:, 0, :], ALU.subtract).then_inc(qres_ready.sem, 1)
                dve.wait_ge(qmid.sem, qmid.at(b))
                nc.vector.tensor_tensor(qp[:, 2, :], qres[:, :], qp[:, 1, :], ALU.subtract).then_inc(qlo.sem, 1)


def top_queries(nc, c, posd):
    REPLACED = -1000.0
    FILL = 8 - LAST
    with ExitStack() as ctx:
        r = Room(nc, ctx, "tk_")
        w = r.sb("w", [P, L + 8])
        m8 = r.sb("m8", [P, 8])
        mask, cum, pos = r.sb("mask", [P, L]), r.sb("cum", [P, L]), r.sb("pos", [P, L])
        posb = r.sb("posb", [P, L], BF16)
        psN, psP = r.ps("psN", [P, L]), r.ps("psP", [P, L])
        s_n, s_pos, s_posb, s_t, s_posT, s_store, s_dve = (
            r.sem(n) for n in ("n", "pos", "posb", "t", "posT", "store", "dve"))
        ctx.callback(r.clear)
        block = ctx.enter_context(nc.Block())

        @block.tensor
        def _(pe):
            for t in range(TPS):
                last = nc.tensor.transpose(psN[:, t * P:(t + 1) * P], c.QN[:, t, :], c.ident)
            last.then_inc(s_n, 1)
            pe.wait_ge(s_pos, 1)
            for t in range(TPS):
                last = nc.tensor.transpose(psP[:, t * P:(t + 1) * P], pos[:, t * P:(t + 1) * P], c.ident)
            last.then_inc(s_t, 1)

        @block.sync
        def _(sp):
            sp.wait_ge(s_posb, 1)
            sp.dma_start(posd, posb[:, :]).then_inc(s_store, 16)
            sp.wait_ge(s_store, 16)

        @block.scalar
        def _(act):
            act.wait_ge(s_pos, 1)
            nc.scalar.activation(posb[:, :], pos[:, :], ACT.Copy).then_inc(s_posb, 1)

        @block.vector
        def _(dve):
            for i in range(8):
                last = nc.vector.memset(w[:, L + i:L + i + 1], -1.0 - i)
            last.then_inc(s_dve, 1)
            dve.wait_ge(s_n, 1)
            nc.vector.tensor_copy(w[:, 0:L], psN[:, :]).then_inc(s_dve, 1)
            for i in range(ROUNDS - 1):
                dve.wait_ge(s_dve, i * 2 + 2)
                nc.vector.max(m8[:, :], w[:, :]).then_inc(s_dve, 1)
                dve.wait_ge(s_dve, i * 2 + 3)
                nc.vector.match_replace(w[:, :], m8[:, :], w[:, :], REPLACED).then_inc(s_dve, 1)
            n = 2 * ROUNDS
            dve.wait_ge(s_dve, n)
            nc.vector.max(m8[:, :], w[:, :]).then_inc(s_dve, 1)
            dve.wait_ge(s_dve, n + 1)
            nc.vector.tensor_copy(m8[:, LAST:8], w[:, L:L + FILL]).then_inc(s_dve, 1)
            dve.wait_ge(s_dve, n + 2)
            nc.vector.match_replace(w[:, :], m8[:, :], w[:, :], REPLACED).then_inc(s_dve, 1)
            dve.wait_ge(s_dve, n + 3)
            nc.vector.tensor_scalar(mask[:, :], w[:, 0:L], REPLACED, None, ALU.is_equal).then_inc(s_dve, 1)
            dve.wait_ge(s_dve, n + 4)
            nc.vector.tensor_tensor_scan(cum[:, :], c.ones[:, 0:1].to_broadcast([P, L]), mask[:, :], 0.0,
                                         ALU.mult, ALU.add).then_inc(s_dve, 1)
            dve.wait_ge(s_dve, n + 5)
            nc.vector.tensor_tensor(pos[:, :], cum[:, :], mask[:, :], ALU.mult).then_inc(s_pos, 1)
            dve.wait_ge(s_t, 1)
            nc.vector.tensor_copy(c.posT[:, :, :].rearrange("p t n -> p (t n)"), psP[:, :]).then_inc(s_posT, 1)
            dve.wait_ge(s_posT, 1)


def attention(nc, c, kd, qd, posd):
    NH = 2 * H
    with ExitStack() as ctx:
        r = Room(nc, ctx, "a2_")
        q6 = r.sb("q6", [P, 2, TPS * H * KROWS + P], BF16)
        k6T = r.sb("k6T", [KROWS, 2, H, L], BF16)
        posrow = r.sb("posrow", [P, 2, H * L], BF16)
        vcur = r.sb("vcur", [P, 2, L])
        pick = r.sb("pick", [P, 2, TPS, P], BF16)
        place = r.sb("place", [P, 2, H, L], BF16)
        qsel = r.sb("qsel", [KROWS, 2, P], BF16)
        nmax = r.sb("nmax", [P, 2])
        rsum = r.sb("rsum", [P, 2, H])
        prob, probT = r.sb("prob", [P, 2, L]), r.sb("probT", [P, 2, L])
        rinv, o, ores = r.sb("rinv", [P, H]), r.sb("o", [P, P]), r.sb("ores", [P, P])
        o3 = r.sb("o3", [P, H, 3, HD], BF16)
        others, omean = r.sb("others", [P, TPS, H]), r.sb("omean", [P, L])
        vmean = r.sb("vmean", [P, 2, P])
        ssum, attn, attnT, xb = (r.sb(n, [P, L]) for n in ("ssum", "attn", "attnT", "xb"))
        psG, psC = r.ps("psG", [P, L]), r.ps("psC", [P, L])
        psS, psE, psO = r.ps("psS", [P, 2, L]), r.ps("psE", [P, 2, L]), r.ps("psO", [P, 2, L])

        k_in, q_in, pos_in, v_in, vm_in = ([r.sig(f"{n}{u}", 16 * m) for u in range(2)] for n, m in
                                           (("kin", NPROD), ("qin", 1), ("pin", 1), ("vin", 1), ("vmin", 1)))
        picked, placed = r.sig("pick", NH), r.sig("place", NH)
        g_done, qsel_ready, s_done, max_ready = r.sig("g", NH), r.sig("qsel", NH), r.sig("s", NH), r.sig("max", NH)
        prob_ready, e_done, probT_ready, o_done = r.sig("prob", NH), r.sig("e", NH), r.sig("probT", NH), r.sig("o", NH)
        rinv_ready, o_ready, ohi, ores_ready, omid, olo = (r.sig(n, 2) for n in ("ri", "of", "ohi", "ores", "omid", "olo"))
        c_done, ssum_ready = r.sig("c", 2 * TPS), r.sig("ssum", 2 * TPS)
        others_ready, omean_ready, attn_ready = r.sig("oth", 2), r.sig("om", 2), r.sig("attn", 2)
        a_done, attnT_ready, w_done, xb_ready, x_ready = (r.sig(n, 2) for n in ("a", "attnT", "w", "xb", "x"))
        pad_set = r.sem("pad")
        block = ctx.enter_context(nc.Block())

        @block.sync
        def _(sp):
            with sp.Fori(0, B // 2) as it:
                for u in range(2):
                    b = it * 2 + u
                    sp.wait_ge(s_done.sem, s_done.at(it, (u - 1) * H))
                    for n in range(NPROD):
                        sp.dma_start(k6T[n * HD:(n + 1) * HD, u, :, :],
                                     kd[ds(b, 1), :, KPART[n], :].rearrange("o (h d) t -> (o d) h t", h=H)
                                     ).then_inc(k_in[u].sem, 16)
                    sp.wait_ge(g_done.sem, g_done.at(it, (u - 1) * H))
                    sp.dma_start(q6[:, u, 0:TPS * H * KROWS], qd[ds(b, 1), :, :].rearrange("o p n -> (o p) n")
                                 ).then_inc(q_in[u].sem, 16)
                    sp.wait_ge(placed.sem, placed.at(it, (u - 1) * H))
                    sp.dma_start(posrow[:, u, :], posd[ds(b * H, H), :].rearrange("h t -> (h t)")
                                 .partition_broadcast(P)).then_inc(pos_in[u].sem, 16)
                    sp.wait_ge(o_done.sem, o_done.at(it, (u - 1) * H))
                    sp.dma_start(vcur[:, u, :], one(c.V[:, ds(b, 1), :])).then_inc(v_in[u].sem, 16)
                    sp.wait_ge(omean_ready.sem, omean_ready.at(it, u - 1))
                    sp.dma_start(vmean[:, u, :], one(c.VM[:, ds(b, 1), :])).then_inc(vm_in[u].sem, 16)

        @block.tensor
        def _(pe):
            def gather(it, h):
                u, hh = divmod(h, H)
                if hh == 0:
                    pe.wait_ge(q_in[u].sem, q_in[u].at(it))
                pe.wait_ge(picked.sem, picked.at(it, h + 1))
                pe.wait_ge(qsel_ready.sem, qsel_ready.at(it, h))
                for t in range(TPS):
                    at = t * H * KROWS + hh * KROWS
                    last = nc.tensor.matmul(psG[:, 0:P], q6[:, u, at:at + P], pick[:, h % 2, t, :],
                                            start=(t == 0), stop=(t == TPS - 1))
                last.then_inc(g_done.sem, 1)

            def scores(it, h):
                u, hh = divmod(h, H)
                if hh == 0:
                    pe.wait_ge(k_in[u].sem, k_in[u].at(it))
                pe.wait_ge(qsel_ready.sem, qsel_ready.at(it, h + 1))
                pe.wait_ge(prob_ready.sem, prob_ready.at(it, h - 1))
                nc.tensor.matmul(psS[:, h % 2, :], qsel[:, h % 2, :], k6T[:, u, hh, :],
                                 start=True, stop=True).then_inc(s_done.sem, 1)

            def turn(it, h):
                pe.wait_ge(prob_ready.sem, prob_ready.at(it, h + 1))
                pe.wait_ge(probT_ready.sem, probT_ready.at(it, h - 1))
                for t in range(TPS):
                    last = nc.tensor.transpose(psE[:, h % 2, t * P:(t + 1) * P], prob[:, h % 2, t * P:(t + 1) * P],
                                               c.ident)
                last.then_inc(e_done.sem, 1)

            def weigh(it, h):
                u, hh = divmod(h, H)
                if hh == 0:
                    pe.wait_ge(v_in[u].sem, v_in[u].at(it))
                    pe.wait_ge(o_ready.sem, o_ready.at(it, u - 1))
                pe.wait_ge(probT_ready.sem, probT_ready.at(it, h + 1))
                for t in range(TPS):
                    at = t * P + hh * HD
                    last = nc.tensor.matmul(psO[:, u, hh * HD:(hh + 1) * HD], probT[:, h % 2, t * P:(t + 1) * P],
                                            vcur[:, u, at:at + HD], start=(t == 0), stop=(t == TPS - 1))
                last.then_inc(o_done.sem, 1)

            def put_back(it, u, t):
                if t == 0:
                    pe.wait_ge(olo.sem, olo.at(it, u + 1))
                    pe.wait_ge(x_ready.sem, x_ready.at(it, u))
                pe.wait_ge(ssum_ready.sem, ssum_ready.at(it, u * TPS + t))
                for h in range(H):
                    last = nc.tensor.matmul(psC[:, h * 3 * HD:(h + 1) * 3 * HD], place[:, u, h, t * P:(t + 1) * P],
                                            o3[:, h, :, :].rearrange("p s d -> p (s d)"), start=True, stop=True)
                last.then_inc(c_done.sem, 1)

            def turn_outputs(it, u):
                pe.wait_ge(attn_ready.sem, attn_ready.at(it, u + 1))
                for t in range(TPS):
                    last = nc.tensor.transpose(psC[:, t * P:(t + 1) * P], attn[:, t * P:(t + 1) * P], c.ident)
                last.then_inc(a_done.sem, 1)

            def project(it, u):
                pe.wait_ge(attnT_ready.sem, attnT_ready.at(it, u + 1))
                for t in range(TPS):
                    last = nc.tensor.matmul(psC[:, t * P:(t + 1) * P], attnT[:, t * P:(t + 1) * P], c.W[:, 3, :],
                                            start=True, stop=True)
                last.then_inc(w_done.sem, 1)

            pe.wait_ge(pad_set, 1)
            with pe.Fori(0, B // 2) as it:
                for h in range(NH + 3):
                    if h < NH:
                        gather(it, h)
                    if 1 <= h < NH + 1:
                        scores(it, h - 1)
                    if 2 <= h < NH + 2:
                        turn(it, h - 2)
                    if 3 <= h:
                        weigh(it, h - 3)
                    if 9 <= h - H < 9 + TPS:
                        put_back(it, 0, h - H - 9)
                    if h == H + 14:
                        turn_outputs(it, 0)
                    if h == H + 15:
                        project(it, 0)
                for t in range(TPS):
                    put_back(it, 1, t)
                turn_outputs(it, 1)
                project(it, 1)

        @block.scalar
        def _(act):
            def exponents(it, h):
                u, hh = divmod(h, H)
                act.wait_ge(max_ready.sem, max_ready.at(it, h + 1))
                act.wait_ge(e_done.sem, e_done.at(it, h - 1))
                if hh == 0:
                    act.wait_ge(rinv_ready.sem, rinv_ready.at(it, u - 1))
                nc.scalar.activation(prob[:, h % 2, :], psS[:, h % 2, :], ACT.Exp, bias=nmax[:, h % 2:h % 2 + 1],
                                     accum_out=rsum[:, u, hh:hh + 1]).then_inc(prob_ready.sem, 1)

            def turned(it, h):
                act.wait_ge(e_done.sem, e_done.at(it, h + 1))
                act.wait_ge(o_done.sem, o_done.at(it, h - 1))
                nc.scalar.activation(probT[:, h % 2, :], psE[:, h % 2, :], ACT.Copy).then_inc(probT_ready.sem, 1)

            def output_high(it, u):
                act.wait_ge(o_ready.sem, o_ready.at(it, u + 1))
                act.wait_ge(c_done.sem, c_done.at(it, u * TPS))
                nc.scalar.activation(o3[:, :, 0, :], o[:, :].rearrange("p (h d) -> p h d", d=HD),
                                     ACT.Copy).then_inc(ohi.sem, 1)

            def output_middle(it, u):
                act.wait_ge(ores_ready.sem, ores_ready.at(it, u + 1))
                nc.scalar.activation(o3[:, :, 1, :], ores[:, :].rearrange("p (h d) -> p h d", d=HD),
                                     ACT.Copy).then_inc(omid.sem, 1)

            def outputs_turned(it, u):
                act.wait_ge(a_done.sem, a_done.at(it, u + 1))
                act.wait_ge(w_done.sem, w_done.at(it, u))
                nc.scalar.activation(attnT[:, :], psC[:, :], ACT.Copy).then_inc(attnT_ready.sem, 1)

            with act.Fori(0, B // 2) as it:
                for h in range(NH + 3):
                    if 1 <= h < NH + 1:
                        exponents(it, h - 1)
                    if 2 <= h < NH + 2:
                        turned(it, h - 2)
                    for slot, step in ((5, output_high), (7, output_middle), (15, outputs_turned)):
                        if h == H + slot:
                            step(it, 0)
                for step in (output_high, output_middle, outputs_turned):
                    step(it, 1)

        @block.gpsimd
        def _(pool):
            nc.gpsimd.memset(q6[:, :, TPS * H * KROWS:], 0.0).then_inc(pad_set, 1)
            r.seed(pool)
            with pool.Fori(0, B // 2) as it:
                for u in range(2):
                    b = it * 2 + u
                    pool.wait_ge(x_ready.sem, x_ready.at(it, u))
                    nc.gpsimd.tensor_tensor(xb[:, :].rearrange("p (t c) -> p t c", c=P), c.X[:, ds(b * TPS, TPS), :],
                                            c.rows[:, 2, :].unsqueeze(1).to_broadcast([P, TPS, P]),
                                            ALU.add).then_inc(xb_ready.sem, 1)
                    pool.wait_ge(others_ready.sem, others_ready.at(it, u + 1))
                    pool.wait_ge(vm_in[u].sem, vm_in[u].at(it))
                    pool.wait_ge(attn_ready.sem, attn_ready.at(it, u))
                    nc.gpsimd.tensor_tensor(
                        omean[:, :].rearrange("p (t h d) -> p t h d", h=H, d=HD),
                        others[:, :, :].unsqueeze(3).to_broadcast([P, TPS, H, HD]),
                        vmean[:, u, :].rearrange("p (h d) -> p h d", d=HD).unsqueeze(1).to_broadcast([P, TPS, H, HD]),
                        ALU.mult).then_inc(omean_ready.sem, 1)

        @block.vector
        def _(dve):
            def one_hots(it, h):
                u, hh = divmod(h, H)
                dve.wait_ge(g_done.sem, g_done.at(it, h - 1))
                for t in range(TPS):
                    last = nc.vector.tensor_scalar(pick[:, h % 2, t, :], c.iota1[:, :],
                                                   c.posT[:, t, ds(it * NH + h, 1)], None, ALU.is_equal)
                last.then_inc(picked.sem, 1)
                if hh == 0:
                    dve.wait_ge(pos_in[u].sem, pos_in[u].at(it))
                    dve.wait_ge(c_done.sem, c_done.at(it, (u - 1) * TPS))
                nc.vector.tensor_scalar(place[:, u, hh, :], posrow[:, u, hh * L:(hh + 1) * L], c.slot1, None,
                                        ALU.is_equal).then_inc(placed.sem, 1)

            def queries(it, h):
                dve.wait_ge(g_done.sem, g_done.at(it, h + 1))
                dve.wait_ge(s_done.sem, s_done.at(it, h - 1))
                nc.vector.tensor_copy(qsel[:, h % 2, :], psG[0:KROWS, 0:P]).then_inc(qsel_ready.sem, 1)

            def maximum(it, h):
                dve.wait_ge(s_done.sem, s_done.at(it, h + 1))
                dve.wait_ge(prob_ready.sem, prob_ready.at(it, h - 1))
                nc.vector.tensor_reduce(nmax[:, h % 2:h % 2 + 1], psS[:, h % 2, :], AX.X, ALU.max,
                                        negate=True).then_inc(max_ready.sem, 1)

            def divide(it, u):
                dve.wait_ge(prob_ready.sem, prob_ready.at(it, (u + 1) * H))
                nc.vector.reciprocal(rinv[:, :], rsum[:, u, :]).then_inc(rinv_ready.sem, 1)
                dve.wait_ge(omean_ready.sem, omean_ready.at(it, u))
                nc.vector.tensor_scalar(others[:, :, :], c.posT[:, :, ds((it * 2 + u) * H, H)], 0.0, None,
                                        ALU.is_equal).then_inc(others_ready.sem, 1)
                dve.wait_ge(rinv_ready.sem, rinv_ready.at(it, u + 1))
                dve.wait_ge(o_done.sem, o_done.at(it, (u + 1) * H))
                nc.vector.tensor_tensor(o[:, :].rearrange("p (h d) -> p h d", d=HD),
                                        psO[:, u, 0:P].rearrange("p (h d) -> p h d", d=HD),
                                        rinv[:, :].unsqueeze(2).to_broadcast([P, H, HD]), ALU.mult
                                        ).then_inc(o_ready.sem, 1)

            def output_rest(it, u):
                dve.wait_ge(ohi.sem, ohi.at(it, u + 1))
                nc.vector.tensor_tensor(ores[:, :].rearrange("p (h d) -> p h d", d=HD),
                                        o[:, :].rearrange("p (h d) -> p h d", d=HD), o3[:, :, 0, :],
                                        ALU.subtract).then_inc(ores_ready.sem, 1)

            def output_low(it, u):
                dve.wait_ge(omid.sem, omid.at(it, u + 1))
                nc.vector.tensor_tensor(o3[:, :, 2, :], ores[:, :].rearrange("p (h d) -> p h d", d=HD), o3[:, :, 1, :],
                                        ALU.subtract).then_inc(olo.sem, 1)

            def sum_parts(it, u, t):
                dve.wait_ge(c_done.sem, c_done.at(it, u * TPS + t + 1))
                nc.vector.tensor_reduce(ssum[:, t * P:(t + 1) * P].rearrange("p (h d) -> p h d", d=HD),
                                        psC[:, 0:H * 3 * HD].rearrange("p (h s d) -> p h d s", s=3, d=HD),
                                        AX.X, ALU.add).then_inc(ssum_ready.sem, 1)

            def add_means(it, u):
                dve.wait_ge(ssum_ready.sem, ssum_ready.at(it, (u + 1) * TPS))
                dve.wait_ge(omean_ready.sem, omean_ready.at(it, u + 1))
                dve.wait_ge(a_done.sem, a_done.at(it, u))
                nc.vector.tensor_tensor(attn[:, :], ssum[:, :], omean[:, :], ALU.add).then_inc(attn_ready.sem, 1)

            def residual(it, u):
                b = it * 2 + u
                dve.wait_ge(w_done.sem, w_done.at(it, u + 1))
                dve.wait_ge(xb_ready.sem, xb_ready.at(it, u + 1))
                nc.vector.tensor_tensor(c.X[:, ds(b * TPS, TPS), :], psC[:, :].rearrange("p (t c) -> p t c", c=P),
                                        xb[:, :].rearrange("p (t c) -> p t c", c=P), ALU.add).then_inc(x_ready.sem, 1)

            with dve.Fori(0, B // 2) as it:
                for h in range(NH + 3):
                    for slot, step in ((4, divide), (6, output_rest), (8, output_low), (16, residual)):
                        if h == H + slot:
                            step(it, 0)
                    if 10 <= h - H < 10 + TPS:
                        sum_parts(it, 0, h - H - 10)
                    if h == H + 9 + TPS:
                        add_means(it, 0)
                    if h == 0:
                        one_hots(it, 0)
                    if h < NH:
                        queries(it, h)
                    if h + 1 < NH:
                        one_hots(it, h + 1)
                    if 1 <= h < NH + 1:
                        maximum(it, h - 1)
                for step in (divide, output_rest, output_low):
                    step(it, 1)
                for t in range(TPS):
                    sum_parts(it, 1, t)
                add_means(it, 1)
                residual(it, 1)
            dve.wait_ge(x_ready.sem, x_ready.at(B // 2 - 1))


def experts(nc, c, a, xnd, yd):
    R32 = 32
    BANKG = 4
    with ExitStack() as ctx:
        r = Room(nc, ctx, "e_")
        stats, mv = r.sb("stats", [P, TPU, 6]), r.sb("mv", [P, TPU, 2])
        std, rstd = r.sb("std", [P, TPU]), r.sb("rstd", [P, TPU])
        xn, xnT = r.sb("xn", [P, TPU, P]), r.sb("xnT", [P, STOK])
        xbd = r.sb("xbd", [P, NG, P])
        m8, i8 = r.sb("m8", [P, 8]), r.sb("i8", [P, 8], U32)
        vals, dif = r.sb("vals", [P, 4]), r.sb("dif", [P, 3])
        spread = r.sb("spread", [P, NG, 4])
        idx = r.sb("idx", [P, 2, NG * TOPK], U32)
        wts = r.sb("wts", [P, 2, NG * TOPK])
        tab = r.sb("tab", [P, 2, NG, TOPK, P])
        tbd = r.sb("tbd", [P, 2, 16, P])
        hbd = r.sb("hbd", [P, 2, 16, P])
        hpre = r.sb("hpre", [P, 2, BANKG, P])
        hid = r.sb("hid", [P, NG, P])
        hidT = r.sb("hidT", [P, NG, P])
        y, ytok = r.sb("y", [P, NG, R32]), r.sb("ytok", [P, TPU, P])
        psT = r.ps("psT", [P, 2, 512])
        psL, psY = r.ps("psL", [P, 512]), r.ps("psY", [P, 512])
        ps1, ps2 = r.ps("ps1", [P, 2, 512]), r.ps("ps2", [P, 2, 512])

        stat_ready, var_ready, std_ready, rstd_ready = r.sig("stat"), r.sig("var"), r.sig("std"), r.sig("rstd")
        xn_ready, xn_stored, xbd_loaded = r.sig("xn"), r.sig("xst", 16), r.sig("xld", 64)
        t_done, xnT_ready = r.sig("t", 2 + NQ), r.sig("xT", 2)
        logits, spread_done = r.sig("lg", 2), r.sig("sd", 2)
        m8_ready, i8_ready, dif_ready, exp_ready, den_ready, inv_ready, vals_ready, spread_ready = (
            r.sig(n, 2) for n in ("m8", "i8", "dif", "exp", "den", "inv", "vals", "spr"))
        idx_ready, wts_ready = r.sig("idx", 2), r.sig("wts", 2)
        gathered = [[r.sig(f"g{w}{q}", BANKG * TOPK * 16, given=False) for q in range(NQ)] for w in range(2)]
        weighted = r.sig("wgt", 2 * NQ)
        first_done, tbd_act, tbd_dve, second_done = (r.sig(n, 2 * NQ) for n in ("f", "ta", "td", "s"))
        hpre_ready, hid_ready, hidT_ready, hbd_act, hbd_dve = (r.sig(n, NQ) for n in ("hp", "h", "hT", "ha", "hd"))
        y_ready, y_stored, y_loaded, x_ready = r.sig("y", 2), r.sig("yst", 16), r.sig("yld", 16), r.sig("x")
        zeroed = r.sem("zero")
        block = ctx.enter_context(nc.Block())

        def alone(eng):
            eng.sem_inc(c.passed, 1)

        def layout(flat, s):
            return flat[ds(s * (STOK * P), STOK * P)].rearrange("(g p j) -> p g j", p=P, j=R32)

        def tokens(flat, s):
            return flat[ds(s * (STOK * P), STOK * P)].rearrange("(t p c) -> p t c", p=P, c=P)

        @block.sync
        def _(sp):
            sp.wait_ge(zeroed, 1)
            with sp.Fori(0, NS) as s:
                sp.wait_ge(xn_ready.sem, xn_ready.at(s))
                alone(sp)
                sp.dma_start(tokens(xnd, s), xn[:, :, :]).then_inc(xn_stored.sem, 16)
                sp.wait_ge(xn_stored.sem, xn_stored.at(s))
                alone(sp)
                sp.wait_ge(first_done.sem, first_done.at(s, NQ - 2 * NQ))
                alone(sp)
                for g in range(4):
                    sp.dma_start(xbd[R32 * g:R32 * g + R32, :, R32 * g:R32 * g + R32],
                                 layout(xnd, s)[R32 * g:R32 * g + R32, :, :]).then_inc(xbd_loaded.sem, 16)
                sp.wait_ge(y_ready.sem, y_ready.at(s))
                alone(sp)
                sp.dma_start(layout(yd, s), y[:, :, :]).then_inc(y_stored.sem, 16)
                sp.wait_ge(y_stored.sem, y_stored.at(s))
                alone(sp)
                sp.wait_ge(x_ready.sem, x_ready.before(s))
                alone(sp)
                sp.dma_start(ytok[:, :, :], tokens(yd, s)).then_inc(y_loaded.sem, 16)
            sp.wait_ge(y_stored.sem, y_stored.at(NS - 1))
            sp.wait_ge(xn_stored.sem, xn_stored.at(NS - 1))

        @block.gpsimd
        def _(pool):
            for buf in (xbd, tbd, hbd):
                last = nc.gpsimd.memset(buf[:, :, :] if buf is xbd else buf[:, :, :, :], 0.0)
            last.then_inc(zeroed, 1)
            r.seed(pool)
            with pool.Fori(0, NS) as s:
                for w, table in enumerate((a["tab_up"], a["tab_down"])):
                    for q in range(NQ):
                        if q == 0:
                            pool.wait_ge(idx_ready.sem, idx_ready.at(s, w + 1))
                        pool.wait_ge(second_done.sem, second_done.at(s, (w - 2) * NQ + q + 1))
                        alone(pool)
                        for n in range(q * BANKG * TOPK, (q + 1) * BANKG * TOPK):
                            nc.gpsimd.indirect_dma_start(
                                tab[:, w, n // TOPK, n % TOPK, :], None, table,
                                bass.IndirectOffsetOnAxis(ap=idx[:, w, n:n + 1], axis=0)
                            ).then_inc(gathered[w][q].sem, 16)

        @block.tensor
        def _(pe):
            def spread_out(s, w):
                pe.wait_ge(spread_ready.sem, spread_ready.at(s, w + 1))
                nc.tensor.matmul(psL[:, 0:NG * 4], c.sel4, spread[:, :, :].rearrange("p a b -> p (a b)"),
                                 start=True, stop=True).then_inc(spread_done.sem, 1)

            def first(s, w, q):
                u = w * NQ + q
                pe.wait_ge(weighted.sem, weighted.at(s, u + 1))
                pe.wait_ge(tbd_act.sem, tbd_act.at(s, u - 1))
                pe.wait_ge(tbd_dve.sem, tbd_dve.at(s, u - 1))
                if w == 0 and q == 0:
                    pe.wait_ge(xbd_loaded.sem, xbd_loaded.at(s))
                if w == 1:
                    pe.wait_ge(hbd_act.sem, hbd_act.at(s, q + 1))
                    pe.wait_ge(hbd_dve.sem, hbd_dve.at(s, q + 1))
                for i in range(BANKG):
                    n = q * BANKG + i
                    if w == 0:
                        last = nc.tensor.matmul(ps1[:, u % 2, i * P:(i + 1) * P], xbd[:, n, :],
                                                tab[:, 0, n, :, 0:64], start=True, stop=True)
                    else:
                        for jh in range(2):
                            for ih in range(2):
                                last = nc.tensor.matmul(
                                    ps1[:, u % 2, i * P + jh * 64:i * P + jh * 64 + 64],
                                    hbd[:, q % 2, i * 4 + ih * 2 + jh, :],
                                    tab[:, 1, n, :, ih * R32:(ih + 1) * R32], start=(ih == 0), stop=(ih == 1))
                last.then_inc(first_done.sem, 1)

            def second(s, w, q):
                u = w * NQ + q
                pe.wait_ge(tbd_act.sem, tbd_act.at(s, u + 1))
                pe.wait_ge(tbd_dve.sem, tbd_dve.at(s, u + 1))
                if w == 0:
                    pe.wait_ge(hpre_ready.sem, hpre_ready.at(s, q - 1))
                elif q % 4 == 0:
                    pe.wait_ge(y_ready.sem, y_ready.at(s, q // 4))
                for i in range(BANKG):
                    n = q * BANKG + i
                    if w == 0:
                        for h in range(2):
                            for k in range(TOPK):
                                last = nc.tensor.matmul(
                                    ps2[:, q % 2, i * P + h * 64:i * P + h * 64 + 64],
                                    tbd[:, u % 2, i * 4 + k * 2 + h, :], tab[:, 0, n, k, 64:P],
                                    start=(k == 0), stop=(k == TOPK - 1))
                    else:
                        for m in range(4):
                            jh, k = divmod(m, 2)
                            at = (n % 16) * R32
                            last = nc.tensor.matmul(
                                psY[:, at:at + R32], tbd[:, u % 2, i * 4 + jh * 2 + k, :],
                                tab[:, 1, n, k, 64 + jh * R32:64 + (jh + 1) * R32], start=(m == 0), stop=(m == 3))
                last.then_inc(second_done.sem, 1)

            def turn_hidden(s, q):
                pe.wait_ge(hid_ready.sem, hid_ready.at(s, q + 1))
                pe.wait_ge(hidT_ready.sem, hidT_ready.at(s, q - 1))
                for i in range(BANKG):
                    last = nc.tensor.transpose(psT[:, q % 2, i * P:(i + 1) * P], hid[:, q * BANKG + i, :], c.ident)
                last.then_inc(t_done.sem, 1)

            pe.wait_ge(zeroed, 1)
            with pe.Fori(0, NS) as s:
                pe.wait_ge(xn_ready.sem, xn_ready.at(s))
                pe.wait_ge(hidT_ready.sem, hidT_ready.before(s))
                for i in range(2):
                    for t in range(4):
                        last = nc.tensor.transpose(psT[:, i, t * P:(t + 1) * P], xn[:, i * 4 + t, :], c.ident)
                    last.then_inc(t_done.sem, 1)
                pe.wait_ge(xnT_ready.sem, xnT_ready.at(s))
                pe.wait_ge(wts_ready.sem, wts_ready.before(s))
                for t in range(ROWTOK):
                    last = nc.tensor.matmul(psL[:, 0:NEXP], xnT[:, :].rearrange("p (n t) -> p t n", t=ROWTOK)[:, t, :],
                                            c.WupR[:, t * NEXP:(t + 1) * NEXP], start=(t == 0), stop=(t == ROWTOK - 1))
                last.then_inc(logits.sem, 1)
                spread_out(s, 0)
                for q in range(NQ + 2):
                    if q < NQ:
                        first(s, 0, q)
                    if 1 <= q < NQ + 1:
                        second(s, 0, q - 1)
                    if q >= 2:
                        turn_hidden(s, q - 2)
                pe.wait_ge(hidT_ready.sem, hidT_ready.at(s))
                pe.wait_ge(wts_ready.sem, wts_ready.at(s, 1))
                byrow = hidT[:, :, :].rearrange("p n (g o) -> p o (n g)", o=R32)
                for o in range(R32):
                    last = nc.tensor.matmul(psL[:, 0:NEXP], byrow[:, o, :], c.WdR[:, o * NEXP:(o + 1) * NEXP],
                                            start=(o == 0), stop=(o == R32 - 1))
                last.then_inc(logits.sem, 1)
                spread_out(s, 1)
                for q in range(NQ + 1):
                    if q < NQ:
                        first(s, 1, q)
                    if q >= 1:
                        second(s, 1, q - 1)

        def diagonal(copy, dst, src, g):
            return copy(dst[R32 * g:R32 * g + R32, :, R32 * g:R32 * g + R32],
                        src[R32 * g:R32 * g + R32, :].rearrange("p (a b) -> p a b", b=R32))

        @block.scalar
        def _(act):
            def copy(dst, src):
                return nc.scalar.activation(dst, src, ACT.Copy)

            def exponent(s, w):
                act.wait_ge(dif_ready.sem, dif_ready.at(s, w + 1))
                act.wait_ge(vals_ready.sem, vals_ready.at(s, w))
                nc.scalar.activation(dif[:, 1:2], dif[:, 0:1], ACT.Exp).then_inc(exp_ready.sem, 1)

            def first_to_diagonal(s, w, q):
                u = w * NQ + q
                act.wait_ge(first_done.sem, first_done.at(s, u + 1))
                act.wait_ge(second_done.sem, second_done.at(s, u - 1))
                for g in (0, 1):
                    last = diagonal(copy, tbd[:, u % 2, :, :], ps1[:, u % 2, :], g)
                last.then_inc(tbd_act.sem, 1)

            def hidden_to_diagonal(s, q):
                act.wait_ge(first_done.sem, first_done.at(s, NQ + q - 1))
                for g in (0, 1):
                    last = diagonal(copy, hbd[:, q % 2, :, :],
                                    hid[:, q * BANKG:(q + 1) * BANKG, :].rearrange("p a b -> p (a b)"), g)
                last.then_inc(hbd_act.sem, 1)

            act.wait_ge(zeroed, 1)
            with act.Fori(0, NS) as s:
                act.wait_ge(var_ready.sem, var_ready.at(s))
                act.wait_ge(rstd_ready.sem, rstd_ready.before(s))
                nc.scalar.activation(std[:, :], mv[:, :, 1], ACT.Sqrt, bias=c.eps[:, :], scale=1.0).then_inc(std_ready.sem, 1)
                act.wait_ge(logits.sem, logits.before(s))
                for i in range(2):
                    act.wait_ge(t_done.sem, t_done.at(s, i + 1))
                    nc.scalar.activation(xnT[:, i * 512:(i + 1) * 512], psT[:, i, :], ACT.Copy).then_inc(xnT_ready.sem, 1)
                exponent(s, 0)
                for q in range(NQ + 1):
                    if q < NQ:
                        first_to_diagonal(s, 0, q)
                    if q >= 1:
                        act.wait_ge(hpre_ready.sem, hpre_ready.at(s, q))
                        act.wait_ge(hbd_act.sem, hbd_act.before(s))
                        act.wait_ge(hbd_dve.sem, hbd_dve.before(s))
                        nc.scalar.activation(hid[:, (q - 1) * BANKG:q * BANKG, :], hpre[:, (q - 1) % 2, :, :],
                                             ACT.Gelu).then_inc(hid_ready.sem, 1)
                exponent(s, 1)
                act.wait_ge(hid_ready.sem, hid_ready.at(s))
                for q in range(NQ):
                    hidden_to_diagonal(s, q)
                    first_to_diagonal(s, 1, q)

        @block.vector
        def _(dve):
            def route(s, w):
                dve.wait_ge(logits.sem, logits.at(s, w + 1))
                dve.wait_ge(vals_ready.sem, vals_ready.at(s, w))
                alone(dve)
                nc.vector.max(m8[:, :], psL[:, 0:NEXP]).then_inc(m8_ready.sem, 1)
                dve.wait_ge(m8_ready.sem, m8_ready.at(s, w + 1))
                nc.vector.tensor_tensor(dif[:, 0:1], m8[:, 1:2], m8[:, 0:1], ALU.subtract).then_inc(dif_ready.sem, 1)
                nc.vector.max_index(i8[:, :], m8[:, :], psL[:, 0:NEXP]).then_inc(i8_ready.sem, 1)
                dve.wait_ge(exp_ready.sem, exp_ready.at(s, w + 1))
                nc.vector.tensor_scalar(dif[:, 2:3], dif[:, 1:2], 1.0, None, ALU.add).then_inc(den_ready.sem, 1)
                dve.wait_ge(den_ready.sem, den_ready.at(s, w + 1))
                dve.wait_ge(spread_ready.sem, spread_ready.at(s, w))
                nc.vector.reciprocal(vals[:, 2:3], dif[:, 2:3]).then_inc(inv_ready.sem, 1)
                dve.wait_ge(i8_ready.sem, i8_ready.at(s, w + 1))
                nc.vector.tensor_copy(vals[:, 0:2], i8[:, 0:2])
                dve.wait_ge(inv_ready.sem, inv_ready.at(s, w + 1))
                nc.vector.tensor_tensor(vals[:, 3:4], dif[:, 1:2], vals[:, 2:3], ALU.mult).then_inc(vals_ready.sem, 1)
                dve.wait_ge(vals_ready.sem, vals_ready.at(s, w + 1))
                dve.wait_ge(spread_done.sem, spread_done.at(s, w))
                nc.vector.tensor_tensor(spread[:, :, :], c.grp.unsqueeze(2).to_broadcast([P, NG, 4]),
                                        vals[:, :].unsqueeze(1).to_broadcast([P, NG, 4]), ALU.mult
                                        ).then_inc(spread_ready.sem, 1)
                dve.wait_ge(spread_done.sem, spread_done.at(s, w + 1))
                both = psL[:, 0:NG * 4].rearrange("p (n v) -> p n v", v=4)
                nc.vector.tensor_scalar(idx[:, w, :].rearrange("p (n k) -> p n k", k=TOPK), both[:, :, 0:2], float(R32),
                                        c.row32, ALU.mult, ALU.add).then_inc(idx_ready.sem, 1)
                nc.vector.tensor_copy(wts[:, w, :].rearrange("p (n k) -> p n k", k=TOPK), both[:, :, 2:4]
                                      ).then_inc(wts_ready.sem, 1)
                dve.wait_ge(wts_ready.sem, wts_ready.at(s, w + 1))

            def weigh(s, w, q):
                dve.wait_ge(gathered[w][q].sem, gathered[w][q].at(s))
                part = tab[:, w, q * BANKG:(q + 1) * BANKG, :, 0:64].rearrange("p n k o -> p (n k) o")
                wt = wts[:, w, q * BANKG * TOPK:(q + 1) * BANKG * TOPK].unsqueeze(2).to_broadcast([P, BANKG * TOPK, 64])
                nc.vector.tensor_tensor(part, part, wt, ALU.mult).then_inc(weighted.sem, 1)

            def first_to_diagonal(s, w, q):
                u = w * NQ + q
                dve.wait_ge(first_done.sem, first_done.at(s, u + 1))
                dve.wait_ge(second_done.sem, second_done.at(s, u - 1))
                for g in (2, 3):
                    last = diagonal(nc.vector.tensor_copy, tbd[:, u % 2, :, :], ps1[:, u % 2, :], g)
                last.then_inc(tbd_dve.sem, 1)

            def hidden_to_diagonal(s, q):
                dve.wait_ge(first_done.sem, first_done.at(s, NQ + q - 1))
                for g in (2, 3):
                    last = diagonal(nc.vector.tensor_copy, hbd[:, q % 2, :, :],
                                    hid[:, q * BANKG:(q + 1) * BANKG, :].rearrange("p a b -> p (a b)"), g)
                last.then_inc(hbd_dve.sem, 1)

            dve.wait_ge(zeroed, 1)
            with dve.Fori(0, NS) as s:
                for t in range(TPU):
                    last = nc.vector.bn_stats(stats[:, t, :], one(c.X[:, ds(s * TPU + t, 1), :]))
                last.then_inc(stat_ready.sem, 1)
                dve.wait_ge(stat_ready.sem, stat_ready.at(s))
                alone(dve)
                for t in range(TPU):
                    last = nc.vector.bn_aggr(mv[:, t, :], stats[:, t, :])
                last.then_inc(var_ready.sem, 1)
                dve.wait_ge(std_ready.sem, std_ready.at(s))
                nc.vector.reciprocal(rstd[:, :], std[:, :]).then_inc(rstd_ready.sem, 1)
                dve.wait_ge(rstd_ready.sem, rstd_ready.at(s))
                dve.wait_ge(xn_stored.sem, xn_stored.before(s))
                dve.wait_ge(t_done.sem, t_done.before(s))
                for t in range(TPU):
                    last = nc.vector.tensor_scalar(xn[:, t, :], one(c.X[:, ds(s * TPU + t, 1), :]), mv[:, t, 0:1],
                                                   rstd[:, t:t + 1], ALU.subtract, ALU.mult)
                last.then_inc(xn_ready.sem, 1)
                route(s, 0)
                for q in range(NQ + 2):
                    if q < NQ:
                        weigh(s, 0, q)
                        first_to_diagonal(s, 0, q)
                    if 1 <= q < NQ + 1:
                        n = q - 1
                        dve.wait_ge(second_done.sem, second_done.at(s, n + 1))
                        dve.wait_ge(hid_ready.sem, hid_ready.at(s, n - 1))
                        nc.vector.scalar_tensor_tensor(
                            hpre[:, n % 2, :, :], ps2[:, n % 2, :].rearrange("p (a b) -> p a b", b=P),
                            c.scales[:, 0:1], c.bup[:, :].unsqueeze(1).to_broadcast([P, BANKG, P]),
                            ALU.mult, ALU.add).then_inc(hpre_ready.sem, 1)
                    if q >= 2:
                        n = q - 2
                        dve.wait_ge(t_done.sem, t_done.at(s, 2 + n + 1))
                        dve.wait_ge(logits.sem, logits.before(s))
                        nc.vector.tensor_copy(hidT[:, n * BANKG:(n + 1) * BANKG, :].rearrange("p a b -> p (a b)"),
                                              psT[:, n % 2, :]).then_inc(hidT_ready.sem, 1)
                route(s, 1)
                for q in range(NQ + 1):
                    if q < NQ:
                        hidden_to_diagonal(s, q)
                        weigh(s, 1, q)
                        first_to_diagonal(s, 1, q)
                    if q == 4 or q == NQ:
                        n = q // 4 - 1
                        dve.wait_ge(second_done.sem, second_done.at(s, NQ + 4 * (n + 1)))
                        dve.wait_ge(y_stored.sem, y_stored.before(s))
                        nc.vector.scalar_tensor_tensor(
                            y[:, n * 16:(n + 1) * 16, :], psY[:, :].rearrange("p (a b) -> p a b", b=R32),
                            c.scales[:, 1:2], c.bdn[:, :].unsqueeze(1).to_broadcast([P, 16, R32]),
                            ALU.mult, ALU.add).then_inc(y_ready.sem, 1)
                dve.wait_ge(y_loaded.sem, y_loaded.at(s))
                nc.vector.tensor_tensor(c.X[:, ds(s * TPU, TPU), :], c.X[:, ds(s * TPU, TPU), :], ytok[:, :, :],
                                        ALU.add).then_inc(x_ready.sem, 1)
            dve.wait_ge(x_ready.sem, x_ready.at(NS - 1))


class Norm:

    def __init__(self, nc, c, r):
        self.nc, self.c = nc, c
        self.stats, self.mv = r.sb("stats", [P, TPS, 6]), r.sb("mv", [P, TPS, 2])
        self.std, self.rstd = r.sb("std", [P, TPS]), r.sb("rstd", [P, TPS])
        self.xn, self.xnT, self.psT = r.sb("xn", [P, TPS, P]), r.sb("xnT", [P, L]), r.ps("psT", [P, L])
        self.stat_ready, self.var_ready, self.std_ready, self.rstd_ready, self.xn_ready, self.t_done, self.ready = (
            r.sig(n) for n in ("stat", "var", "std", "rstd", "xn", "t", "xnT"))


    def statistics(self, dve, b):
        for t in range(TPS):
            last = self.nc.vector.bn_stats(self.stats[:, t, :], one(self.c.X[:, ds(b * TPS + t, 1), :]))
        last.then_inc(self.stat_ready.sem, 1)
        dve.wait_ge(self.stat_ready.sem, self.stat_ready.at(b))
        dve.sem_inc(self.c.passed, 1)
        for t in range(TPS):
            last = self.nc.vector.bn_aggr(self.mv[:, t, :], self.stats[:, t, :])
        last.then_inc(self.var_ready.sem, 1)

    def root(self, act, b):
        act.wait_ge(self.var_ready.sem, self.var_ready.at(b))
        self.nc.scalar.activation(self.std[:, :], self.mv[:, :, 1], ACT.Sqrt, bias=self.c.eps[:, :],
                                  scale=1.0).then_inc(self.std_ready.sem, 1)

    def apply(self, dve, b):
        dve.wait_ge(self.std_ready.sem, self.std_ready.at(b))
        self.nc.vector.reciprocal(self.rstd[:, :], self.std[:, :]).then_inc(self.rstd_ready.sem, 1)
        dve.wait_ge(self.t_done.sem, self.t_done.before(b))
        dve.wait_ge(self.rstd_ready.sem, self.rstd_ready.at(b))
        for t in range(TPS):
            last = self.nc.vector.tensor_scalar(self.xn[:, t, :], one(self.c.X[:, ds(b * TPS + t, 1), :]),
                                                self.mv[:, t, 0:1], self.rstd[:, t:t + 1], ALU.subtract, ALU.mult)
        last.then_inc(self.xn_ready.sem, 1)

    def turn(self, pe, b):
        pe.wait_ge(self.xn_ready.sem, self.xn_ready.at(b))
        pe.wait_ge(self.ready.sem, self.ready.before(b))
        for t in range(TPS):
            last = self.nc.tensor.transpose(self.psT[:, t * P:(t + 1) * P], self.xn[:, t, :], self.c.ident)
        last.then_inc(self.t_done.sem, 1)

    def turned(self, act, b, used):
        act.wait_ge(self.t_done.sem, self.t_done.at(b))
        act.wait_ge(used.sem, used.before(b))
        self.nc.scalar.activation(self.xnT[:, :], self.psT[:, :], ACT.Copy).then_inc(self.ready.sem, 1)


def plastic_attention(nc, c):
    with ExitStack() as ctx:
        r = Room(nc, ctx, "s_")
        norm = Norm(nc, c, r)
        wq, wk = r.sb("wq", [P, HD, P]), r.sb("wk", [P, HD, P])
        keep, gain = r.sb("keep", [P, HD]), r.sb("gain", [P, HD])
        v = r.sb("v", [P, L])
        heb, state, syn, z = (r.sb(n, [P, 2, L]) for n in ("heb", "state", "syn", "z"))
        xb = r.sb("xb", [P, TPS, P])
        psV, psO = r.ps("psV", [P, L]), r.ps("psO", [P, L])
        psK, psQ = r.ps("psK", [P, 2, L]), r.ps("psQ", [P, 2, L])
        v_done, v_ready, k_done, q_done = r.sig("vd"), r.sig("v"), r.sig("kd", HD), r.sig("qd", HD)
        heb_ready, state_ready, syn_ready, z_ready, o_done = (r.sig(n, HD) for n in ("heb", "st", "syn", "z", "o"))
        used, xb_ready, x_ready = r.sig("used"), r.sig("xb"), r.sig("x")
        w_ready, sig_ready, set_up = r.sem("w"), r.sem("sg"), r.sem("setup")
        static, lam, gamma = (c.stp[:, n * HD:(n + 1) * HD] for n in range(3))
        block = ctx.enter_context(nc.Block())

        @block.tensor
        def _(pe):
            pe.wait_ge(w_ready, 2)
            norm.turn(pe, 0)

            def sequence(b, more):
                pe.wait_ge(norm.ready.sem, norm.ready.at(b))
                pe.wait_ge(v_ready.sem, v_ready.before(b))
                nc.tensor.matmul(psV[:, :], c.Wqkv[:, 2 * P:3 * P], norm.xnT[:, :], start=True, stop=True
                                 ).then_inc(v_done.sem, 1)
                for j in range(HD + 2):
                    if j < HD:
                        pe.wait_ge(heb_ready.sem, heb_ready.at(b, j - 1))
                        nc.tensor.matmul(psK[:, j % 2, :], wk[:, j, :], norm.xnT[:, :], start=True, stop=True
                                         ).then_inc(k_done.sem, 1)
                        pe.wait_ge(z_ready.sem, z_ready.at(b, j - 1))
                        last = nc.tensor.matmul(psQ[:, j % 2, :], wq[:, j, :], norm.xnT[:, :], start=True, stop=True)
                        last.then_inc(q_done.sem, 1)
                    if j == HD - 1:
                        pe.drain().then_inc(used.sem, 1)
                    if j == HD and more:
                        norm.turn(pe, b + 1)
                    if j >= 2:
                        n = j - 2
                        pe.wait_ge(z_ready.sem, z_ready.at(b, n + 1))
                        if n == 0:
                            pe.wait_ge(x_ready.sem, x_ready.before(b))
                        for t in range(TPS):
                            last = nc.tensor.matmul(psO[:, t * P:(t + 1) * P], z[:, n % 2, t * P:(t + 1) * P],
                                                    c.outW[:, :], start=(n == 0 and t == 0), stop=(n == HD - 1),
                                                    skip_group_check=True)
                        last.then_inc(o_done.sem, 1)

            with pe.Fori(0, B - 1) as b:
                sequence(b, True)
            sequence(B - 1, False)

        @block.scalar
        def _(act):
            nc.scalar.activation(keep[:, :], lam, ACT.Sigmoid).then_inc(sig_ready, 1)
            norm.root(act, 0)
            norm.turned(act, 0, used)

            def sequence(b, more):
                act.wait_ge(v_done.sem, v_done.at(b))
                act.wait_ge(heb_ready.sem, heb_ready.before(b))
                nc.scalar.activation(v[:, :], psV[:, :], ACT.Identity, bias=c.bqkv[:, 0:1]).then_inc(v_ready.sem, 1)
                for j in range(HD):
                    act.wait_ge(state_ready.sem, state_ready.at(b, j + 1))
                    act.wait_ge(z_ready.sem, z_ready.at(b, j - 1))
                    nc.scalar.activation(syn[:, j % 2, :], state[:, j % 2, :], ACT.Identity, bias=static[:, j:j + 1],
                                         scale=gain[:, j:j + 1]).then_inc(syn_ready.sem, 1)
                    if j == 4 and more:
                        norm.root(act, b + 1)
                if more:
                    norm.turned(act, b + 1, used)

            act.wait_ge(set_up, 2)
            with act.Fori(0, B - 1) as b:
                sequence(b, True)
            sequence(B - 1, False)

        @block.gpsimd
        def _(pool):
            r.seed(pool)

            def sequence(b):
                pool.wait_ge(x_ready.sem, x_ready.before(b))
                nc.gpsimd.tensor_tensor(xb[:, :, :], c.X[:, ds(b * TPS, TPS), :],
                                        c.rows[:, 3, :].unsqueeze(1).to_broadcast([P, TPS, P]),
                                        ALU.add).then_inc(xb_ready.sem, 1)

            with pool.Fori(0, B) as b:
                sequence(b)

        @block.vector
        def _(dve):
            for dst, at in ((wq, 0), (wk, P)):
                nc.vector.tensor_copy(
                    dst[:, :, :].rearrange("p j (h i) -> p j h i", h=H),
                    c.Wqkv[:, at:at + P].rearrange("p (h j) -> p j h", h=H).unsqueeze(3).to_broadcast([P, HD, H, HD])
                ).then_inc(w_ready, 1)
            nc.vector.tensor_scalar(gain[:, :], gamma, QSCALE, None, ALU.mult).then_inc(set_up, 1)
            dve.wait_ge(sig_ready, 1)
            nc.vector.tensor_scalar(keep[:, :], keep[:, :], -1.0, 1.0, ALU.mult, ALU.add).then_inc(set_up, 1)
            dve.wait_ge(set_up, 2)
            norm.statistics(dve, 0)
            norm.apply(dve, 0)

            def sequence(b, more):
                for j in range(HD + 2):
                    if j < HD:
                        dve.wait_ge(k_done.sem, k_done.at(b, j + 1))
                        if j == 0:
                            dve.wait_ge(v_ready.sem, v_ready.at(b))
                        dve.wait_ge(state_ready.sem, state_ready.at(b, j - 1))
                        nc.vector.scalar_tensor_tensor(heb[:, j % 2, :], psK[:, j % 2, :],
                                                       c.bqkv[:, 2 + HD + j:3 + HD + j], v[:, :], ALU.add, ALU.mult
                                                       ).then_inc(heb_ready.sem, 1)
                    if j >= 2:
                        n = j - 2
                        dve.wait_ge(syn_ready.sem, syn_ready.at(b, n + 1))
                        dve.wait_ge(q_done.sem, q_done.at(b, n + 1))
                        dve.wait_ge(o_done.sem, o_done.at(b, n - 1))
                        nc.vector.scalar_tensor_tensor(z[:, n % 2, :], psQ[:, n % 2, :], c.bqkv[:, 2 + n:3 + n],
                                                       syn[:, n % 2, :], ALU.add, ALU.mult).then_inc(z_ready.sem, 1)
                    if j < HD:
                        dve.wait_ge(heb_ready.sem, heb_ready.at(b, j + 1))
                        dve.wait_ge(syn_ready.sem, syn_ready.at(b, j - 1))
                        nc.vector.tensor_tensor_scan(state[:, j % 2, :], keep[:, j:j + 1].to_broadcast([P, L]),
                                                     heb[:, j % 2, :], 0.0, ALU.mult, ALU.add
                                                     ).then_inc(state_ready.sem, 1)
                    if j == 3 and more:
                        norm.statistics(dve, b + 1)
                    if j == 6 and more:
                        norm.apply(dve, b + 1)
                dve.wait_ge(o_done.sem, o_done.at(b))
                dve.wait_ge(xb_ready.sem, xb_ready.at(b))
                nc.vector.tensor_tensor(c.X[:, ds(b * TPS, TPS), :], psO[:, :].rearrange("p (t c) -> p t c", c=P),
                                        xb[:, :, :], ALU.add).then_inc(x_ready.sem, 1)

            with dve.Fori(0, B - 1) as b:
                sequence(b, True)
            sequence(B - 1, False)
            dve.wait_ge(x_ready.sem, x_ready.at(B - 1))


def gated_feed_forward(nc, c, out):
    with ExitStack() as ctx:
        r = Room(nc, ctx, "f_")
        norm = Norm(nc, c, r)
        gated, hidden = r.sb("gated", [P, 2, L]), r.sb("hidden", [P, HM, L])
        res = r.sb("res", [P, 2, L])
        psG, psU, psO = r.ps("psG", [P, 2, L]), r.ps("psU", [P, 2, L]), r.ps("psO", [P, L])
        g_done, u_done, gated_ready, hidden_ready = (r.sig(n, HM) for n in ("g", "u", "gt", "h"))
        used, o_done, x_ready, stored = r.sig("used"), r.sig("o"), r.sig("x"), r.sig("out", 16)

        block = ctx.enter_context(nc.Block())

        @block.sync
        def _(sp):
            with sp.Fori(0, B) as b:
                sp.wait_ge(x_ready.sem, x_ready.at(b))
                sp.sem_inc(c.passed, 1)
                sp.dma_start(out[ds(b * L, L), :].rearrange("(t p) c -> p t c", p=P),
                             c.X[:, ds(b * TPS, TPS), :]).then_inc(stored.sem, 16)
            sp.wait_ge(stored.sem, stored.at(B - 1))

        @block.tensor
        def _(pe):
            norm.turn(pe, 0)

            def sequence(b, more):
                pe.wait_ge(norm.ready.sem, norm.ready.at(b))
                for m in range(HM):
                    pe.wait_ge(gated_ready.sem, gated_ready.at(b, m - 1))
                    nc.tensor.matmul(psG[:, m % 2, :], c.Wint[:, m * P:(m + 1) * P], norm.xnT[:, :],
                                     start=True, stop=True).then_inc(g_done.sem, 1)
                    pe.wait_ge(hidden_ready.sem, hidden_ready.at(b, m - 1))
                    last = nc.tensor.matmul(psU[:, m % 2, :], c.Wint[:, (HM + m) * P:(HM + m + 1) * P],
                                            norm.xnT[:, :], start=True, stop=True)
                    last.then_inc(u_done.sem, 1)
                pe.drain().then_inc(used.sem, 1)
                if more:
                    norm.turn(pe, b + 1)
                pe.wait_ge(hidden_ready.sem, hidden_ready.at(b))
                pe.wait_ge(x_ready.sem, x_ready.before(b))
                for t in range(TPS):
                    for m in range(HM):
                        last = nc.tensor.matmul(psO[:, t * P:(t + 1) * P], hidden[:, m, t * P:(t + 1) * P],
                                                c.Wint[:, (2 * HM + m) * P:(2 * HM + m + 1) * P],
                                                start=(m == 0), stop=(m == HM - 1))
                last.then_inc(o_done.sem, 1)

            with pe.Fori(0, B - 1) as b:
                sequence(b, True)
            sequence(B - 1, False)

        @block.scalar
        def _(act):
            norm.root(act, 0)
            norm.turned(act, 0, used)

            def sequence(b, more):
                if more:
                    norm.root(act, b + 1)
                for m in range(HM):
                    act.wait_ge(g_done.sem, g_done.at(b, m + 1))
                    act.wait_ge(hidden_ready.sem, hidden_ready.at(b, m - 1))
                    nc.scalar.activation(gated[:, m % 2, :], psG[:, m % 2, :], ACT.Silu).then_inc(gated_ready.sem, 1)
                if more:
                    norm.turned(act, b + 1, used)

            with act.Fori(0, B - 1) as b:
                sequence(b, True)
            sequence(B - 1, False)

        @block.gpsimd
        def _(pool):
            r.seed(pool)

        @block.vector
        def _(dve):
            norm.statistics(dve, 0)
            norm.apply(dve, 0)

            def sequence(b, more):
                if more:
                    norm.statistics(dve, b + 1)
                    norm.apply(dve, b + 1)
                for m in range(HM):
                    dve.wait_ge(gated_ready.sem, gated_ready.at(b, m + 1))
                    dve.wait_ge(u_done.sem, u_done.at(b, m + 1))
                    dve.wait_ge(o_done.sem, o_done.before(b))
                    nc.vector.tensor_tensor(hidden[:, m, :], psU[:, m % 2, :], gated[:, m % 2, :], ALU.mult
                                            ).then_inc(hidden_ready.sem, 1)
                dve.wait_ge(o_done.sem, o_done.at(b))
                nc.vector.tensor_tensor(c.X[:, ds(b * TPS, TPS), :], psO[:, :].rearrange("p (t c) -> p t c", c=P),
                                        c.X[:, ds(b * TPS, TPS), :], ALU.add).then_inc(x_ready.sem, 1)

            with dve.Fori(0, B - 1) as b:
                sequence(b, True)
            sequence(B - 1, False)


def build(nc, a, out):
    scratch = {
        "kd": ((B, P, 3, L), BF16),
        "qd": ((B, P, TPS * H * KROWS), BF16),
        "posd": ((P, L), BF16),
        "xnd": ((N * P,), F32),
        "yd": ((N * P,), F32),
    }
    kd, qd, posd, xnd, yd = (nc.dram_tensor(n, s, d).ap() for n, (s, d) in scratch.items())
    with ExitStack() as ctx:
        c = Room(nc, ctx, "c_")
        c.passed = c.sem("passed")
        c.X = c.sb("X", [P, NT, P])
        c.consts = c.sb("consts", [P, 3 * P + NG + 2])
        c.ident = c.consts[:, 0:P]
        c.sel4 = c.consts[:, 2 * P:3 * P]
        c.grp = c.consts[:, 3 * P:3 * P + NG]
        c.slot1 = c.consts[:, 3 * P + NG:3 * P + NG + 1]
        c.row32 = c.consts[:, 3 * P + NG + 1:3 * P + NG + 2]
        c.iota1 = c.sb("iota1", [P, P], BF16)
        c.ones, c.eps, c.mean_ones = c.sb("ones", [P, 1]), c.sb("eps", [P, 1]), c.sb("mean_ones", [P, P])
        c.W, c.rows, c.cols = c.sb("W", [P, 4, P]), c.sb("rows", [P, 4, P]), c.sb("cols", [P, 1])
        c.Wint = c.sb("Wint", [P, 3 * HM * P])
        c.WupR, c.WdR = c.sb("WupR", [P, ROWTOK * NEXP]), c.sb("WdR", [P, 32 * NEXP])
        c.scales, c.bup, c.bdn = c.sb("scales", [P, 2]), c.sb("bup", [P, P]), c.sb("bdn", [P, 32])
        c.Wqkv, c.outW, c.bqkv, c.stp = (c.sb("Wqkv", [P, 3 * P]), c.sb("outW", [P, P]),
                                         c.sb("bqkv", [P, 2 + 2 * HD]), c.sb("stp", [P, 3 * HD]))
        load(nc, c, a)
        with ExitStack() as att:
            t = Room(nc, att, "c0_")
            c.V, c.VM, c.QN, c.posT = (t.sb("V", [P, B, L]), t.sb("VM", [P, B, P]), t.sb("QN", [P, TPS, P]),
                                       t.sb("posT", [P, TPS, P]))
            attention_projections(nc, c, kd, qd)
            top_queries(nc, c, posd)
            attention(nc, c, kd, qd, posd)
        experts(nc, c, a, xnd, yd)
        plastic_attention(nc, c)
        gated_feed_forward(nc, c, out)


def kernel(**inputs):
    import numpy as _np
    import concourse.bacc as _bacc
    from concourse import mybir as _mybir
    from concourse.bass_utils import run_bass_kernel_spmd as _run

    def turned(name):
        return inputs[name].T

    i = {k: _np.asarray(v) for k, v in inputs.items()}
    n = _np.arange(P)
    consts = _np.concatenate([
        _np.eye(P), _np.tile(n + 1.0, (P, 1)), n[:, None] % G4 == n[None, :] // 32,
        n[:, None] // G4 == _np.arange(NG)[None, :], n[:, None] + 1.0, n[:, None] % 32,
    ], axis=1).astype(_np.float32)
    arrays = {
        "x": i["L0_attn_x"].reshape(N, P), "consts": consts,
        "WqT": i["L0_attn_Wq"].T, "WkT": i["L0_attn_Wk"].T, "WvT": i["L0_attn_Wv"].T, "WoT": i["L0_attn_Wo"].T,
        "bq": i["L0_attn_bq"], "bk": i["L0_attn_bk"].reshape(P, 1), "bv": i["L0_attn_bv"], "bo": i["L0_attn_bo"],
        "WupR": i["L0_ffn_W_up"].reshape(NEXP, ROWTOK, P).transpose(2, 1, 0).reshape(P, -1),
        "tab_up": _np.concatenate([i["L0_ffn_A_up"].transpose(0, 2, 1), i["L0_ffn_B_up"].transpose(0, 2, 1)],
                                  axis=2).reshape(NEXP * 32, P),
        "tab_down": _np.concatenate([
            i[f"L0_ffn_{m}_down"].transpose(0, 2, 1).reshape(NEXP, 2, 32, 32).transpose(0, 2, 1, 3).reshape(NEXP, 32, 64)
            for m in "AB"], axis=2).reshape(NEXP * 32, P),
        "bias_up": i["L0_ffn_bias_up"].reshape(2, 32, 64).transpose(1, 0, 2).reshape(32, P),
        "bias_down": i["L0_ffn_bias_down"].reshape(32, 32),
        "scale_up": i["L0_ffn_scale_up"], "scale_down": i["L0_ffn_scale_down"],
        "WdR": i["L0_ffn_W_down"].reshape(NEXP, 2, 32, 64).transpose(1, 3, 2, 0).reshape(P, -1),
        "WqkvT": i["L1_attn_Wqkv_w"].T, "out_wT": i["L1_attn_out_w"].T, "out_b": i["L1_attn_out_b"],
        "bqkv": _np.concatenate([
            i["L1_attn_Wqkv_b"][2 * P:].reshape(P, 1), i["L1_attn_Wqkv_b"][2 * P:].reshape(P, 1),
            _np.repeat(i["L1_attn_Wqkv_b"][:P].reshape(H, HD), HD, axis=0),
            _np.repeat(i["L1_attn_Wqkv_b"][P:2 * P].reshape(H, HD), HD, axis=0)], axis=1),
        "stp": _np.concatenate([i[f"L1_attn_{m}"].reshape(P, HD) for m in ("W_static", "Lambda_raw", "Gamma")], axis=1),
        "w_gateT": i["L1_ffn_w_gate"].T, "w_upT": i["L1_ffn_w_up"].T, "w_downT": i["L1_ffn_w_down"].T,
    }
    arrays = {f"in_{k}": _np.ascontiguousarray(v) for k, v in arrays.items()}
    nc = _bacc.Bacc("TRN2", target_bir_lowering=False, num_devices=1)
    a = {k[3:]: nc.dram_tensor(k, v.shape, _mybir.dt.from_np(v.dtype), kind="ExternalInput").ap()
         for k, v in arrays.items()}
    out = nc.dram_tensor("out_x", (N, P), F32, kind="ExternalOutput").ap()
    build(nc, a, out)
    r = _run(nc, [arrays], core_ids=[0])
    return r.results[0]["out_x"].reshape(B, L, P)
```

```python
import concourse.bass as bass
from concourse import mybir
from concourse.bass import ds
from contextlib import ExitStack

P = 128
B, L = 8, 512
N = B * L
TPS = L // P
NT = N // P
H, HD = 16, 8
KTOP = int(L * 0.2)
ROUNDS = -(-KTOP // 8)
LAST = KTOP - 8 * (ROUNDS - 1)
QPART = [0, 0, 0, 1, 1, 2]
KPART = [0, 1, 2, 0, 1, 0]
NPROD = len(QPART)
KROWS = NPROD * HD
QSCALE = float(HD) ** -0.5
NEXP, TOPK = 64, 2
ROWTOK = 8
SROWS = 128
STOK = SROWS * ROWTOK
TPU = STOK // P
NS = N // STOK
G4 = 4
NG = SROWS // G4
NQ = NG // 4
HM = 3
EPS = 1e-5
WARM = 5

F32 = mybir.dt.float32
BF16 = mybir.dt.bfloat16
I32 = mybir.dt.int32
U32 = mybir.dt.uint32
ALU = mybir.AluOpType
ACT = mybir.ActivationFunctionType
AX = mybir.AxisListType


class Sig:

    def __init__(self, sem, per=1, given=True):
        self.sem, self.per, self.given = sem, per, given

    def seed(self, eng):
        if self.given:
            eng.sem_inc(self.sem, self.per)

    def at(self, turn, k=None):
        return (turn + self.given) * self.per + (self.per if k is None else k)

    def before(self, turn, k=None):
        assert self.given
        return turn * self.per + (self.per if k is None else k)


class Room:

    def __init__(self, nc, ctx, name):
        self.nc, self.ctx, self.name = nc, ctx, name
        self.sigs, self.sems = [], []

    def sb(self, name, shape, dt=F32):
        return self.ctx.enter_context(self.nc.sbuf_tensor(self.name + name, shape, dt))

    def ps(self, name, shape, dt=F32):
        return self.ctx.enter_context(self.nc.psum_tensor(self.name + name, shape, dt))

    def sem(self, name):
        self.sems.append(self.ctx.enter_context(self.nc.semaphore(self.name + name)))
        return self.sems[-1]

    def clear(self):
        self.nc.gpsimd.drain()
        for s in self.sems:
            self.nc.gpsimd.sem_clear(s)
        self.nc.all_engine_barrier()

    def sig(self, name, per=1, given=True):
        self.sigs.append(Sig(self.sem(name), per, given))
        return self.sigs[-1]

    def seed(self, eng):
        for s in self.sigs:
            s.seed(eng)


def one(ap):
    if len(ap.shape) == 3:
        return ap.rearrange("p o c -> p (o c)")
    return ap.rearrange("p o t c -> p (o t) c")


def warm_up(nc, c, ps):
    for _ in range(WARM):
        nc.tensor.matmul(ps, c.ident, c.Wint[:, 0:512], start=True, stop=True)


def load(nc, c, a):
    with ExitStack() as ctx:
        r = Room(nc, ctx, "ld_")
        s_in, s_int = r.sem("in"), r.sem("int")
        ints = r.sb("ints", [P, 3 * HM * P], I32)
        ctx.callback(r.clear)
        block = ctx.enter_context(nc.Block())
        loads = [
            (c.X[:, :, :], a["x"].rearrange("(t p) c -> p t c", p=P)),
            (c.consts[:, :], a["consts"]),
            (c.W[:, 0, :], a["WqT"]), (c.W[:, 1, :], a["WkT"]), (c.W[:, 2, :], a["WvT"]), (c.W[:, 3, :], a["WoT"]),
            (c.rows[:, 0, :], a["bq"].partition_broadcast(P)), (c.rows[:, 1, :], a["bv"].partition_broadcast(P)),
            (c.rows[:, 2, :], a["bo"].partition_broadcast(P)), (c.rows[:, 3, :], a["out_b"].partition_broadcast(P)),
            (c.cols[:, 0:1], a["bk"]),
            (ints[:, 0:HM * P], a["w_gateT"]), (ints[:, HM * P:2 * HM * P], a["w_upT"]),
            (ints[:, 2 * HM * P:].rearrange("p (m c) -> p m c", m=HM), a["w_downT"].rearrange("(m p) c -> p m c", p=P)),
            (c.WupR[:, :], a["WupR"]), (c.WdR[:, :], a["WdR"]),
            (c.scales[:, 0:1], a["scale_up"].partition_broadcast(P)),
            (c.scales[:, 1:2], a["scale_down"].partition_broadcast(P)),
            (c.Wqkv[:, :], a["WqkvT"]), (c.outW[:, :], a["out_wT"]), (c.bqkv[:, :], a["bqkv"]),
            (c.stp[:, :], a["stp"]),
            (c.bup[:, :], a["bias_up"]),
        ] + [(c.bdn[32 * i:32 * i + 32, :], a["bias_down"]) for i in range(4)]

        @block.sync
        def _(sp):
            for dst, src in loads:
                sp.dma_start(dst, src).then_inc(s_in, 16)

        @block.vector
        def _(dve):
            nc.vector.memset(c.mean_ones[:, :], 1.0 / L)
            nc.vector.memset(c.ones[:, :], 1.0)
            nc.vector.memset(c.eps[:, :], EPS)
            dve.wait_ge(s_in, 16 * len(loads))
            nc.vector.tensor_copy(c.Wint[:, :], ints[:, :]).then_inc(s_int, 1)
            nc.vector.tensor_copy(c.iota1[:, :], c.consts[:, P:2 * P])
            dve.wait_ge(s_int, 1)
            nc.vector.tensor_scalar(c.Wint[:, :], c.Wint[:, :], 1.0 / 127.0, None, ALU.mult).then_inc(s_int, 1)
            dve.wait_ge(s_int, 2)


def attention_projections(nc, c, kd, qd):
    with ExitStack() as ctx:
        r = Room(nc, ctx, "a1_")
        stats, mv = r.sb("stats", [P, NT, 6]), r.sb("mv", [P, NT, 2])
        std, rstd = r.sb("std", [P, NT]), r.sb("rstd", [P, NT])
        xn = r.sb("xn", [P, TPS, P])
        xnT = r.sb("xnT", [P, L])
        q, q2, qs = r.sb("q", [P, L]), r.sb("q2", [P, L]), r.sb("qs", [P, L])
        qres = r.sb("qres", [P, L])
        kres = r.sb("kres", [P, L])
        k3 = r.sb("k3", [P, 3, L], BF16)
        vcur = r.sb("vcur", [P, L])
        q6 = r.sb("q6", [P, TPS * H * KROWS], BF16)
        parts = q6[:, :].rearrange("p (a c d) -> p a c d", c=NPROD, d=HD)
        q_stored = r.sig("q6st", 16)
        psT, psK, psQ, psV = (r.ps(n, [P, L]) for n in ("psT", "psK", "psQ", "psV"))
        psM = r.ps("psM", [P, 512])
        s_stats, s_var, s_std, s_rstd = (r.sem(n) for n in ("stats", "var", "std", "rstd"))
        xn_ready, t_done, xnT_ready = r.sig("xn"), r.sig("t"), r.sig("xnT")
        k_done, q_done, v_done, m_done = r.sig("k"), r.sig("q"), r.sig("v"), r.sig("m")
        khi, kres_ready, kmid, klo = r.sig("khi"), r.sig("kres"), r.sig("kmid"), r.sig("klo")
        k_stored = r.sig("kst", 16)
        q_ready, q2_ready, qs_ready, qn_ready = r.sig("qf"), r.sig("q2"), r.sig("qs"), r.sig("qn")
        qhi, qres_ready, qmid, qlo = r.sig("qhi"), r.sig("qres"), r.sig("qmid"), r.sig("qlo")
        v_ready, v_stored, mean_ready = r.sig("vf"), r.sig("vst", 16), r.sig("mean")
        bq_row = c.rows[:, 0, :].unsqueeze(1).to_broadcast([P, TPS, P])
        bv_row = c.rows[:, 1, :].unsqueeze(1).to_broadcast([P, TPS, P])
        ctx.callback(r.clear)
        block = ctx.enter_context(nc.Block())

        def tiles(ap):
            return ap.rearrange("p (t c) -> p t c", c=P)

        def heads(buf):
            return buf[:, :].rearrange("p (a d) -> p a d", d=HD)

        @block.sync
        def _(sp):
            with sp.Fori(0, B) as b:
                sp.wait_ge(klo.sem, klo.at(b))
                sp.dma_start(kd[ds(b, 1), :, :, :].rearrange("o p c t -> (o p) c t"),
                             k3[:, :, :]).then_inc(k_stored.sem, 16)
                sp.wait_ge(v_ready.sem, v_ready.at(b))
                sp.dma_start(one(c.V[:, ds(b, 1), :]), vcur[:, :]).then_inc(v_stored.sem, 16)
                sp.wait_ge(qlo.sem, qlo.at(b))
                sp.dma_start(one(qd[ds(b, 1), :, :].rearrange("o p n -> p o n")), q6[:, :]).then_inc(q_stored.sem, 16)
            sp.wait_ge(k_stored.sem, k_stored.at(B - 1))
            sp.wait_ge(q_stored.sem, q_stored.at(B - 1))
            sp.wait_ge(v_stored.sem, v_stored.at(B - 1))

        @block.tensor
        def _(pe):
            def turn(b):
                pe.wait_ge(xn_ready.sem, xn_ready.at(b))
                pe.wait_ge(xnT_ready.sem, xnT_ready.before(b))
                for t in range(TPS):
                    last = nc.tensor.transpose(psT[:, t * P:(t + 1) * P], xn[:, t, :], c.ident)
                last.then_inc(t_done.sem, 1)

            def sequence(b, more):
                pe.wait_ge(xnT_ready.sem, xnT_ready.at(b))
                pe.wait_ge(kres_ready.sem, kres_ready.before(b))
                nc.tensor.matmul(psK[:, :], c.W[:, 1, :], xnT[:, :], start=True, stop=True).then_inc(k_done.sem, 1)
                pe.wait_ge(q_ready.sem, q_ready.before(b))
                for t in range(TPS):
                    last = nc.tensor.matmul(psQ[:, t * P:(t + 1) * P], xnT[:, t * P:(t + 1) * P], c.W[:, 0, :],
                                            start=True, stop=True)
                last.then_inc(q_done.sem, 1)
                pe.wait_ge(v_ready.sem, v_ready.before(b))
                for t in range(TPS):
                    last = nc.tensor.matmul(psV[:, t * P:(t + 1) * P], xnT[:, t * P:(t + 1) * P], c.W[:, 2, :],
                                            start=True, stop=True)
                last.then_inc(v_done.sem, 1)
                if more:
                    turn(b + 1)
                pe.wait_ge(v_ready.sem, v_ready.at(b))
                pe.wait_ge(mean_ready.sem, mean_ready.before(b))
                for t in range(TPS):
                    last = nc.tensor.matmul(psM[:, 0:P], c.mean_ones[:, :], vcur[:, t * P:(t + 1) * P],
                                            start=(t == 0), stop=(t == TPS - 1))
                last.then_inc(m_done.sem, 1)

            turn(0)
            with pe.Fori(0, B - 1) as b:
                sequence(b, True)
            sequence(B - 1, False)

        @block.scalar
        def _(act):
            act.wait_ge(s_var, 1)
            nc.scalar.activation(std[:, :], mv[:, :, 1], ACT.Sqrt, bias=c.eps[:, :], scale=1.0).then_inc(s_std, 1)

            def turned(b):
                act.wait_ge(t_done.sem, t_done.at(b))
                act.wait_ge(v_done.sem, v_done.before(b))
                nc.scalar.activation(xnT[:, :], psT[:, :], ACT.Copy).then_inc(xnT_ready.sem, 1)

            def sequence(b, more):
                act.wait_ge(k_done.sem, k_done.at(b))
                act.wait_ge(k_stored.sem, k_stored.before(b))
                nc.scalar.activation(k3[:, 0, :], psK[:, :], ACT.Identity, bias=c.cols[:, 0:1]).then_inc(khi.sem, 1)
                act.wait_ge(q_ready.sem, q_ready.at(b))
                act.wait_ge(qn_ready.sem, qn_ready.before(b))
                nc.scalar.activation(q2[:, :], q[:, :], ACT.Square).then_inc(q2_ready.sem, 1)
                act.wait_ge(kres_ready.sem, kres_ready.at(b))
                nc.scalar.activation(k3[:, 1, :], kres[:, :], ACT.Copy).then_inc(kmid.sem, 1)
                if more:
                    turned(b + 1)
                act.wait_ge(qs_ready.sem, qs_ready.at(b))
                act.wait_ge(q_stored.sem, q_stored.before(b))
                nc.scalar.activation(parts[:, :, 0:3, :], heads(qs).unsqueeze(2).to_broadcast([P, TPS * H, 3, HD]),
                                     ACT.Copy).then_inc(qhi.sem, 1)
                act.wait_ge(qres_ready.sem, qres_ready.at(b))
                nc.scalar.activation(parts[:, :, 3:5, :], heads(qres).unsqueeze(2).to_broadcast([P, TPS * H, 2, HD]),
                                     ACT.Copy).then_inc(qmid.sem, 1)
                act.wait_ge(m_done.sem, m_done.at(b))
                nc.scalar.activation(one(c.VM[:, ds(b, 1), :]), psM[:, 0:P], ACT.Copy).then_inc(mean_ready.sem, 1)

            turned(0)
            with act.Fori(0, B - 1) as b:
                sequence(b, True)
            sequence(B - 1, False)

        @block.gpsimd
        def _(pool):
            r.seed(pool)
            with pool.Fori(0, B) as b:
                pool.wait_ge(kmid.sem, kmid.at(b))
                nc.gpsimd.tensor_tensor(k3[:, 2, :], kres[:, :], k3[:, 1, :], ALU.subtract).then_inc(klo.sem, 1)

        @block.vector
        def _(dve):
            for t in range(NT):
                last = nc.vector.bn_stats(stats[:, t, :], c.X[:, t, :])
            last.then_inc(s_stats, 1)
            dve.wait_ge(s_stats, 1)
            for t in range(NT):
                last = nc.vector.bn_aggr(mv[:, t, :], stats[:, t, :])
            last.then_inc(s_var, 1)
            dve.wait_ge(s_std, 1)
            nc.vector.reciprocal(rstd[:, :], std[:, :]).then_inc(s_rstd, 1)
            dve.wait_ge(s_rstd, 1)

            def normalise(b):
                dve.wait_ge(t_done.sem, t_done.before(b))
                for t in range(TPS):
                    j = b * TPS + t
                    last = nc.vector.tensor_scalar(xn[:, t, :], one(c.X[:, ds(j, 1), :]), one(mv[:, ds(j, 1), 0:1]),
                                                   rstd[:, ds(j, 1)], ALU.subtract, ALU.mult)
                last.then_inc(xn_ready.sem, 1)

            def sequence(b, more):
                dve.wait_ge(khi.sem, khi.at(b))
                dve.wait_ge(klo.sem, klo.before(b))
                nc.vector.scalar_tensor_tensor(kres[:, :], psK[:, :], c.cols[:, 0:1], k3[:, 0, :],
                                               ALU.add, ALU.subtract).then_inc(kres_ready.sem, 1)
                dve.wait_ge(q_done.sem, q_done.at(b))
                dve.wait_ge(q2_ready.sem, q2_ready.before(b))
                nc.vector.tensor_tensor(tiles(q[:, :]), tiles(psQ[:, :]), bq_row, ALU.add).then_inc(q_ready.sem, 1)
                dve.wait_ge(v_done.sem, v_done.at(b))
                dve.wait_ge(v_stored.sem, v_stored.before(b))
                dve.wait_ge(m_done.sem, m_done.before(b))
                nc.vector.tensor_tensor(tiles(vcur[:, :]), tiles(psV[:, :]), bv_row, ALU.add).then_inc(v_ready.sem, 1)
                if more:
                    normalise(b + 1)
                dve.wait_ge(q_ready.sem, q_ready.at(b))
                dve.wait_ge(qres_ready.sem, qres_ready.before(b))
                nc.vector.tensor_scalar(qs[:, :], q[:, :], QSCALE, None, ALU.mult).then_inc(qs_ready.sem, 1)
                dve.wait_ge(q2_ready.sem, q2_ready.at(b))
                nc.vector.tensor_reduce(c.QN[:, :, ds(b * H, H)], q2[:, :].rearrange("p (t h d) -> p t h d", h=H, d=HD),
                                        AX.X, ALU.add).then_inc(qn_ready.sem, 1)
                dve.wait_ge(qhi.sem, qhi.at(b))
                dve.wait_ge(qlo.sem, qlo.before(b))
                nc.vector.tensor_tensor(heads(qres), heads(qs), parts[:, :, 0, :], ALU.subtract
                                        ).then_inc(qres_ready.sem, 1)
                dve.wait_ge(qmid.sem, qmid.at(b))
                nc.vector.tensor_tensor(parts[:, :, 5, :], heads(qres), parts[:, :, 3, :], ALU.subtract
                                        ).then_inc(qlo.sem, 1)

            normalise(0)
            with dve.Fori(0, B - 1) as b:
                sequence(b, True)
            sequence(B - 1, False)


def top_queries(nc, c, posd):
    REPLACED = -1000.0
    FILL = 8 - LAST
    with ExitStack() as ctx:
        r = Room(nc, ctx, "tk_")
        w = r.sb("w", [P, L + 8])
        m8 = r.sb("m8", [P, 8])
        mask, cum, pos = r.sb("mask", [P, L]), r.sb("cum", [P, L]), r.sb("pos", [P, L])
        posb = r.sb("posb", [P, L], BF16)
        psN, psP = r.ps("psN", [P, L]), r.ps("psP", [P, L])
        s_n, s_pos, s_posb, s_t, s_posT, s_store, s_dve = (
            r.sem(n) for n in ("n", "pos", "posb", "t", "posT", "store", "dve"))
        ctx.callback(r.clear)
        block = ctx.enter_context(nc.Block())

        @block.tensor
        def _(pe):
            for t in range(TPS):
                last = nc.tensor.transpose(psN[:, t * P:(t + 1) * P], c.QN[:, t, :], c.ident)
            last.then_inc(s_n, 1)
            pe.wait_ge(s_pos, 1)
            for t in range(TPS):
                last = nc.tensor.transpose(psP[:, t * P:(t + 1) * P], pos[:, t * P:(t + 1) * P], c.ident)
            last.then_inc(s_t, 1)

        @block.sync
        def _(sp):
            sp.wait_ge(s_posb, 1)
            sp.dma_start(posd, posb[:, :]).then_inc(s_store, 16)
            sp.wait_ge(s_store, 16)

        @block.scalar
        def _(act):
            act.wait_ge(s_pos, 1)
            nc.scalar.activation(posb[:, :], pos[:, :], ACT.Copy).then_inc(s_posb, 1)

        @block.vector
        def _(dve):
            for i in range(8):
                last = nc.vector.memset(w[:, L + i:L + i + 1], -1.0 - i)
            last.then_inc(s_dve, 1)
            dve.wait_ge(s_n, 1)
            nc.vector.tensor_copy(w[:, 0:L], psN[:, :]).then_inc(s_dve, 1)
            for i in range(ROUNDS - 1):
                dve.wait_ge(s_dve, i * 2 + 2)
                nc.vector.max(m8[:, :], w[:, :]).then_inc(s_dve, 1)
                dve.wait_ge(s_dve, i * 2 + 3)
                nc.vector.match_replace(w[:, :], m8[:, :], w[:, :], REPLACED).then_inc(s_dve, 1)
            n = 2 * ROUNDS
            dve.wait_ge(s_dve, n)
            nc.vector.max(m8[:, :], w[:, :]).then_inc(s_dve, 1)
            dve.wait_ge(s_dve, n + 1)
            nc.vector.tensor_copy(m8[:, LAST:8], w[:, L:L + FILL]).then_inc(s_dve, 1)
            dve.wait_ge(s_dve, n + 2)
            nc.vector.match_replace(w[:, :], m8[:, :], w[:, :], REPLACED).then_inc(s_dve, 1)
            dve.wait_ge(s_dve, n + 3)
            nc.vector.tensor_scalar(mask[:, :], w[:, 0:L], REPLACED, None, ALU.is_equal).then_inc(s_dve, 1)
            dve.wait_ge(s_dve, n + 4)
            nc.vector.tensor_tensor_scan(cum[:, :], c.ones[:, 0:1].to_broadcast([P, L]), mask[:, :], 0.0,
                                         ALU.mult, ALU.add).then_inc(s_dve, 1)
            dve.wait_ge(s_dve, n + 5)
            nc.vector.tensor_tensor(pos[:, :], cum[:, :], mask[:, :], ALU.mult).then_inc(s_pos, 1)
            dve.wait_ge(s_t, 1)
            nc.vector.tensor_copy(c.posT[:, :, :].rearrange("p t n -> p (t n)"), psP[:, :]).then_inc(s_posT, 1)
            dve.wait_ge(s_posT, 1)


def attention(nc, c, kd, qd, posd):
    NH = 2 * H
    TURNS = B // 2
    LATER = 20
    WIDE = 32
    with ExitStack() as ctx:
        r = Room(nc, ctx, "a2_")
        q6 = r.sb("q6", [P, 2, TPS * H * KROWS + P], BF16)
        k6T = r.sb("k6T", [KROWS, 2, H, L], BF16)
        posrow = r.sb("posrow", [P, 2, H * L], BF16)
        vcur = r.sb("vcur", [P, 2, L + WIDE - HD])
        pick = r.sb("pick", [P, 2, TPS, P], BF16)
        place = r.sb("place", [P, 2, H, L], BF16)
        qsel = r.sb("qsel", [KROWS, 2, P], BF16)
        nmax = r.sb("nmax", [P, 2])
        rsum = r.sb("rsum", [P, 2, H])
        prob, probT = r.sb("prob", [P, 3, L]), r.sb("probT", [P, 2, L])
        oT = r.sb("oT", [P, L])
        rinv, o, ores = r.sb("rinv", [P, H]), r.sb("o", [P, P]), r.sb("ores", [P, P])
        o3 = r.sb("o3", [P, H, 3, HD], BF16)
        others, omean = r.sb("others", [P, TPS, H]), r.sb("omean", [P, L])
        vmean = r.sb("vmean", [P, 2, P])
        ssum, attn, attnT, xb = (r.sb(n, [P, L]) for n in ("ssum", "attn", "attnT", "xb"))
        psG, psC = r.ps("psG", [P, L]), r.ps("psC", [P, L])
        psS, psE, psO = r.ps("psS", [P, 2, L]), r.ps("psE", [P, 2, L]), r.ps("psO", [P, 2, L])

        k_in, q_in, pos_in, v_in, vm_in = ([r.sig(f"{n}{u}", 16 * m) for u in range(2)] for n, m in
                                           (("kin", NPROD), ("qin", 1), ("pin", 1), ("vin", 1), ("vmin", 1)))
        picked, placed = r.sig("pick", NH), r.sig("place", NH // 4)
        g_done, qsel_ready, s_done, max_ready = r.sig("g", NH), r.sig("qsel", NH), r.sig("s", NH), r.sig("max", NH)
        prob_ready, e_done, probT_ready, o_done = r.sig("prob", NH), r.sig("e", NH), r.sig("probT", NH), r.sig("o", NH)
        oT_ready, ot_done = r.sig("oT", 2), r.sig("ot", 2)
        rinv_ready, o_ready, ohi, ores_ready, omid, olo = (r.sig(n, 2) for n in ("ri", "of", "ohi", "ores", "omid", "olo"))
        c_done, ssum_ready = r.sig("c", 2 * TPS), r.sig("ssum", 2 * TPS)
        others_ready, omean_ready, attn_ready = r.sig("oth", 2), r.sig("om", 2), r.sig("attn", 2)
        a_done, attnT_ready, w_done, xb_ready, x_ready = (r.sig(n, 2) for n in ("a", "attnT", "w", "xb", "x"))
        pad_set = r.sem("pad")
        block = ctx.enter_context(nc.Block())

        @block.sync
        def _(sp):
            with sp.Fori(0, TURNS) as it:
                for u in range(2):
                    b = it * 2 + u
                    sp.wait_ge(s_done.sem, s_done.at(it, (u - 1) * H))
                    for n in range(NPROD):
                        sp.dma_start(k6T[n * HD:(n + 1) * HD, u, :, :],
                                     kd[ds(b, 1), :, KPART[n], :].rearrange("o (h d) t -> (o d) h t", h=H)
                                     ).then_inc(k_in[u].sem, 16)
                    sp.wait_ge(g_done.sem, g_done.at(it, (u - 1) * H))
                    sp.dma_start(q6[:, u, 0:TPS * H * KROWS], qd[ds(b, 1), :, :].rearrange("o p n -> (o p) n")
                                 ).then_inc(q_in[u].sem, 16)
                    sp.wait_ge(placed.sem, placed.at(it, (u - 1) * H // 4))
                    sp.dma_start(posrow[:, u, :], posd[ds(b * H, H), :].rearrange("h t -> (h t)")
                                 .partition_broadcast(P)).then_inc(pos_in[u].sem, 16)
                    sp.wait_ge(o_done.sem, o_done.at(it, (u - 1) * H))
                    sp.dma_start(vcur[:, u, 0:L], one(c.V[:, ds(b, 1), :])).then_inc(v_in[u].sem, 16)
                    sp.wait_ge(omean_ready.sem, omean_ready.at(it, u - 1))
                    sp.dma_start(vmean[:, u, :], one(c.VM[:, ds(b, 1), :])).then_inc(vm_in[u].sem, 16)

        @block.tensor
        def _(pe):
            def gather(it, h):
                u, hh = divmod(h, H)
                if hh == 0:
                    pe.wait_ge(q_in[u].sem, q_in[u].at(it))
                pe.wait_ge(picked.sem, picked.at(it, h + 1))
                pe.wait_ge(qsel_ready.sem, qsel_ready.at(it, h))
                for t in range(TPS):
                    at = t * H * KROWS + hh * KROWS
                    last = nc.tensor.matmul(psG[:, 0:P], q6[:, u, at:at + P], pick[:, h % 2, t, :],
                                            start=(t == 0), stop=(t == TPS - 1))
                last.then_inc(g_done.sem, 1)

            def scores(it, h):
                u, hh = divmod(h, H)
                if hh == 0:
                    pe.wait_ge(k_in[u].sem, k_in[u].at(it))
                pe.wait_ge(qsel_ready.sem, qsel_ready.at(it, h + 1))
                pe.wait_ge(prob_ready.sem, prob_ready.at(it, h - 1))
                nc.tensor.matmul(psS[:, h % 2, :], qsel[:, h % 2, :], k6T[:, u, hh, :],
                                 start=True, stop=True).then_inc(s_done.sem, 1)

            def turn(it, h):
                pe.wait_ge(prob_ready.sem, prob_ready.at(it, h + 1))
                pe.wait_ge(probT_ready.sem, probT_ready.at(it, h - 1))
                for t in range(TPS):
                    last = nc.tensor.transpose(psE[:, h % 2, t * P:(t + 1) * P], prob[:, h % 3, t * P:(t + 1) * P],
                                               c.ident)
                last.then_inc(e_done.sem, 1)

            def weigh(it, h):
                u, hh = divmod(h, H)
                if hh == 0:
                    pe.wait_ge(v_in[u].sem, v_in[u].at(it))
                    pe.wait_ge(oT_ready.sem, oT_ready.at(it, u - 1))
                pe.wait_ge(probT_ready.sem, probT_ready.at(it, h + 1))
                for t in range(TPS):
                    at = t * P + hh * HD
                    last = nc.tensor.matmul(
                        psO[hh % 4 * WIDE:(hh % 4 + 1) * WIDE, u, hh // 4 * P:(hh // 4 + 1) * P],
                        vcur[:, u, at:at + WIDE], probT[:, h % 2, t * P:(t + 1) * P],
                        start=(t == 0), stop=(t == TPS - 1))
                last.then_inc(o_done.sem, 1)

            def turn_slots(it, u):
                pe.wait_ge(oT_ready.sem, oT_ready.at(it, u + 1))
                pe.wait_ge(x_ready.sem, x_ready.at(it, u))
                for t in range(4):
                    last = nc.tensor.transpose(psC[:, t * P:(t + 1) * P], oT[:, t * P:(t + 1) * P], c.ident)
                last.then_inc(ot_done.sem, 1)

            def put_back(it, u, t):
                if t == 0:
                    pe.wait_ge(olo.sem, olo.at(it, u + 1))
                    pe.wait_ge(o_ready.sem, o_ready.at(it, u + 1))
                pe.wait_ge(ssum_ready.sem, ssum_ready.at(it, u * TPS + t))
                for h in range(H):
                    last = nc.tensor.matmul(psC[:, h * 3 * HD:(h + 1) * 3 * HD], place[:, u, h, t * P:(t + 1) * P],
                                            o3[:, h, :, :].rearrange("p s d -> p (s d)"), start=True, stop=True)
                last.then_inc(c_done.sem, 1)

            def turn_outputs(it, u):
                pe.wait_ge(attn_ready.sem, attn_ready.at(it, u + 1))
                for t in range(TPS):
                    last = nc.tensor.transpose(psC[:, t * P:(t + 1) * P], attn[:, t * P:(t + 1) * P], c.ident)
                last.then_inc(a_done.sem, 1)

            def project(it, u):
                pe.wait_ge(attnT_ready.sem, attnT_ready.at(it, u + 1))
                for t in range(TPS):
                    last = nc.tensor.matmul(psC[:, t * P:(t + 1) * P], attnT[:, t * P:(t + 1) * P], c.W[:, 3, :],
                                            start=True, stop=True)
                last.then_inc(w_done.sem, 1)

            warm_up(nc, c, psS[:, 0, :])
            pe.wait_ge(pad_set, 1)

            def finish(it, u, n):
                if n == H + 6:
                    turn_slots(it, u)
                if H + 12 <= n < H + 12 + TPS:
                    put_back(it, u, n - H - 12)
                if n == H + 17:
                    turn_outputs(it, u)
                if n == H + 18:
                    project(it, u)

            def turn_of_two(it, more):
                for h in range(NH + 4):
                    if h < NH:
                        gather(it, h)
                    if 1 <= h < NH + 1:
                        scores(it, h - 1)
                    if 3 <= h < NH + 3:
                        turn(it, h - 3)
                    if 4 <= h:
                        weigh(it, h - 4)
                    finish(it, 0, h)
                    if more and h < LATER:
                        finish(it - 1, 1, h + H)

            turn_of_two(0, False)
            with pe.Fori(1, TURNS) as it:
                turn_of_two(it, True)
            for n in range(H + 4, H + LATER):
                finish(TURNS - 1, 1, n)

        @block.scalar
        def _(act):
            def queries(it, h):
                act.wait_ge(g_done.sem, g_done.at(it, h + 1))
                act.wait_ge(s_done.sem, s_done.at(it, h - 1))
                nc.scalar.activation(qsel[:, h % 2, :], psG[0:KROWS, 0:P], ACT.Copy).then_inc(qsel_ready.sem, 1)

            def exponents(it, h):
                u, hh = divmod(h, H)
                act.wait_ge(max_ready.sem, max_ready.at(it, h + 1))
                act.wait_ge(e_done.sem, e_done.at(it, h - 2 if h > 1 else h - 1))
                if hh == 0:
                    act.wait_ge(rinv_ready.sem, rinv_ready.at(it, u - 1))
                nc.scalar.activation(prob[:, h % 3, :], psS[:, h % 2, :], ACT.Exp, bias=nmax[:, h % 2:h % 2 + 1],
                                     accum_out=rsum[:, u, hh:hh + 1]).then_inc(prob_ready.sem, 1)

            def turned(it, h):
                act.wait_ge(e_done.sem, e_done.at(it, h + 1))
                act.wait_ge(o_done.sem, o_done.at(it, h - 1))
                nc.scalar.activation(probT[:, h % 2, :], psE[:, h % 2, :], ACT.Copy).then_inc(probT_ready.sem, 1)

            def outputs_out(it, u):
                act.wait_ge(o_done.sem, o_done.at(it, (u + 1) * H))
                act.wait_ge(ot_done.sem, ot_done.at(it, u))
                nc.scalar.activation(oT[:, :], psO[:, u, :], ACT.Copy).then_inc(oT_ready.sem, 1)

            def output_high(it, u):
                act.wait_ge(o_ready.sem, o_ready.at(it, u + 1))
                act.wait_ge(c_done.sem, c_done.at(it, u * TPS))
                nc.scalar.activation(o3[:, :, 0, :], o[:, :].rearrange("p (h d) -> p h d", d=HD),
                                     ACT.Copy).then_inc(ohi.sem, 1)

            def output_middle(it, u):
                act.wait_ge(ores_ready.sem, ores_ready.at(it, u + 1))
                nc.scalar.activation(o3[:, :, 1, :], ores[:, :].rearrange("p (h d) -> p h d", d=HD),
                                     ACT.Copy).then_inc(omid.sem, 1)

            def outputs_turned(it, u):
                act.wait_ge(a_done.sem, a_done.at(it, u + 1))
                act.wait_ge(w_done.sem, w_done.at(it, u))
                nc.scalar.activation(attnT[:, :], psC[:, :], ACT.Copy).then_inc(attnT_ready.sem, 1)

            def finish(it, u, n):
                for slot, step in ((4, outputs_out), (8, output_high), (10, output_middle), (17, outputs_turned)):
                    if n == H + slot:
                        step(it, u)

            def turn_of_two(it, more):
                for h in range(NH + 4):
                    if h < NH:
                        queries(it, h)
                    if 1 <= h < NH + 1:
                        exponents(it, h - 1)
                    if 3 <= h < NH + 3:
                        turned(it, h - 3)
                    finish(it, 0, h)
                    if more and h < LATER:
                        finish(it - 1, 1, h + H)

            turn_of_two(0, False)
            with act.Fori(1, TURNS) as it:
                turn_of_two(it, True)
            for n in range(H + 4, H + LATER):
                finish(TURNS - 1, 1, n)

        @block.gpsimd
        def _(pool):
            nc.gpsimd.memset(vcur[:, :, L:], 0.0)
            nc.gpsimd.memset(q6[:, :, TPS * H * KROWS:], 0.0).then_inc(pad_set, 1)
            r.seed(pool)
            with pool.Fori(0, TURNS) as it:
                for u in range(2):
                    b = it * 2 + u
                    pool.wait_ge(x_ready.sem, x_ready.at(it, u))
                    nc.gpsimd.tensor_tensor(xb[:, :].rearrange("p (t c) -> p t c", c=P), c.X[:, ds(b * TPS, TPS), :],
                                            c.rows[:, 2, :].unsqueeze(1).to_broadcast([P, TPS, P]),
                                            ALU.add).then_inc(xb_ready.sem, 1)
                    pool.wait_ge(others_ready.sem, others_ready.at(it, u + 1))
                    pool.wait_ge(vm_in[u].sem, vm_in[u].at(it))
                    pool.wait_ge(attn_ready.sem, attn_ready.at(it, u))
                    nc.gpsimd.tensor_tensor(
                        omean[:, :].rearrange("p (t h d) -> p t h d", h=H, d=HD),
                        others[:, :, :].unsqueeze(3).to_broadcast([P, TPS, H, HD]),
                        vmean[:, u, :].rearrange("p (h d) -> p h d", d=HD).unsqueeze(1).to_broadcast([P, TPS, H, HD]),
                        ALU.mult).then_inc(omean_ready.sem, 1)

        @block.vector
        def _(dve):
            def one_hots(it, h):
                u, hh = divmod(h, H)
                dve.wait_ge(g_done.sem, g_done.at(it, h - 1))
                for t in range(TPS):
                    last = nc.vector.tensor_scalar(pick[:, h % 2, t, :], c.iota1[:, :],
                                                   c.posT[:, t, ds(it * NH + h, 1)], None, ALU.is_equal)
                last.then_inc(picked.sem, 1)
                if hh == 0:
                    dve.wait_ge(pos_in[u].sem, pos_in[u].at(it))
                    dve.wait_ge(c_done.sem, c_done.at(it, (u - 1) * TPS))
                if hh % 4 == 0:
                    nc.vector.tensor_scalar(place[:, u, hh:hh + 4, :].rearrange("p h t -> p (h t)"),
                                            posrow[:, u, hh * L:(hh + 4) * L], c.slot1, None,
                                            ALU.is_equal).then_inc(placed.sem, 1)

            def maximum(it, h):
                dve.wait_ge(s_done.sem, s_done.at(it, h + 1))
                dve.wait_ge(prob_ready.sem, prob_ready.at(it, h - 1))
                nc.vector.tensor_reduce(nmax[:, h % 2:h % 2 + 1], psS[:, h % 2, :], AX.X, ALU.max,
                                        negate=True).then_inc(max_ready.sem, 1)

            def divide(it, u):
                dve.wait_ge(prob_ready.sem, prob_ready.at(it, (u + 1) * H))
                nc.vector.reciprocal(rinv[:, :], rsum[:, u, :]).then_inc(rinv_ready.sem, 1)
                dve.wait_ge(omean_ready.sem, omean_ready.at(it, u))
                nc.vector.tensor_scalar(others[:, :, :], c.posT[:, :, ds((it * 2 + u) * H, H)], 0.0, None,
                                        ALU.is_equal).then_inc(others_ready.sem, 1)
                dve.wait_ge(rinv_ready.sem, rinv_ready.at(it, u + 1))
                dve.wait_ge(ot_done.sem, ot_done.at(it, u + 1))
                nc.vector.tensor_tensor(o[:, :].rearrange("p (h d) -> p h d", d=HD),
                                        psC[:, :].rearrange("p (h d) -> p h d", d=WIDE)[:, :, 0:HD],
                                        rinv[:, :].unsqueeze(2).to_broadcast([P, H, HD]), ALU.mult
                                        ).then_inc(o_ready.sem, 1)

            def output_rest(it, u):
                dve.wait_ge(ohi.sem, ohi.at(it, u + 1))
                nc.vector.tensor_tensor(ores[:, :].rearrange("p (h d) -> p h d", d=HD),
                                        o[:, :].rearrange("p (h d) -> p h d", d=HD), o3[:, :, 0, :],
                                        ALU.subtract).then_inc(ores_ready.sem, 1)

            def output_low(it, u):
                dve.wait_ge(omid.sem, omid.at(it, u + 1))
                nc.vector.tensor_tensor(o3[:, :, 2, :], ores[:, :].rearrange("p (h d) -> p h d", d=HD), o3[:, :, 1, :],
                                        ALU.subtract).then_inc(olo.sem, 1)

            def sum_parts(it, u, t):
                dve.wait_ge(c_done.sem, c_done.at(it, u * TPS + t + 1))
                nc.vector.tensor_reduce(ssum[:, t * P:(t + 1) * P].rearrange("p (h d) -> p h d", d=HD),
                                        psC[:, 0:H * 3 * HD].rearrange("p (h s d) -> p h d s", s=3, d=HD),
                                        AX.X, ALU.add).then_inc(ssum_ready.sem, 1)

            def add_means(it, u):
                dve.wait_ge(ssum_ready.sem, ssum_ready.at(it, (u + 1) * TPS))
                dve.wait_ge(omean_ready.sem, omean_ready.at(it, u + 1))
                dve.wait_ge(a_done.sem, a_done.at(it, u))
                nc.vector.tensor_tensor(attn[:, :], ssum[:, :], omean[:, :], ALU.add).then_inc(attn_ready.sem, 1)

            def residual(it, u):
                b = it * 2 + u
                dve.wait_ge(w_done.sem, w_done.at(it, u + 1))
                dve.wait_ge(xb_ready.sem, xb_ready.at(it, u + 1))
                nc.vector.tensor_tensor(c.X[:, ds(b * TPS, TPS), :], psC[:, :].rearrange("p (t c) -> p t c", c=P),
                                        xb[:, :].rearrange("p (t c) -> p t c", c=P), ALU.add).then_inc(x_ready.sem, 1)

            def finish(it, u, n):
                for slot, step in ((7, divide), (9, output_rest), (11, output_low), (19, residual)):
                    if n == H + slot:
                        step(it, u)
                if H + 13 <= n < H + 13 + TPS:
                    sum_parts(it, u, n - H - 13)
                if n == H + 12 + TPS:
                    add_means(it, u)

            def turn_of_two(it, more):
                for h in range(NH + 4):
                    if more and h < LATER:
                        finish(it - 1, 1, h + H)
                    finish(it, 0, h)
                    if h == 0:
                        one_hots(it, 0)
                    if h + 1 < NH:
                        one_hots(it, h + 1)
                    if 1 <= h < NH + 1:
                        maximum(it, h - 1)

            turn_of_two(0, False)
            with dve.Fori(1, TURNS) as it:
                turn_of_two(it, True)
            for n in range(H + 4, H + LATER):
                finish(TURNS - 1, 1, n)
            dve.wait_ge(x_ready.sem, x_ready.at(TURNS - 1))




def experts(nc, c, a, xnd, yd):
    R32 = 32
    BANKG = 4
    PARTS = 4
    with ExitStack() as ctx:
        r = Room(nc, ctx, "e_")
        stats, mv = r.sb("stats", [P, NT, 6]), r.sb("mv", [P, NT, 2])
        std, rstd = r.sb("std", [P, NT]), r.sb("rstd", [P, NT])
        xn, xnT = r.sb("xn", [P, TPU, P]), r.sb("xnT", [P, STOK])
        xbd = r.sb("xbd", [P, NG, P])
        m8, i8 = r.sb("m8", [P, 8]), r.sb("i8", [P, 8], U32)
        vals, dif = r.sb("vals", [P, 4]), r.sb("dif", [P, 3])
        spread = r.sb("spread", [P, NG, 4])
        chosen = r.sb("chosen", [P, NS + 2, NG * 4])
        idx = r.sb("idx", [P, PARTS, NG * TOPK], U32)
        wts = r.sb("wts", [P, PARTS, NG * TOPK])
        tab = r.sb("tab", [P, NG, TOPK, P])
        tbd = r.sb("tbd", [P, 2, 16, P])
        hbd = r.sb("hbd", [P, 2, 16, P])
        hpre = r.sb("hpre", [P, 2, 16, R32])
        hid = r.sb("hid", [P, 2, NG, P])
        yT = r.sb("yT", [P, 2, P])
        y, ytok = r.sb("y", [P, NG, R32]), r.sb("ytok", [P, TPU, P])
        psT = r.ps("psT", [P, 2, 512])
        psL, psY = r.ps("psL", [P, 512]), r.ps("psY", [P, 512])
        ps1, ps2 = r.ps("ps1", [P, 2, 512]), r.ps("ps2", [P, 2, 512])

        xn_ready, xn_stored = r.sig("xn"), r.sig("xst", 16)
        t_done, xnT_ready = r.sig("t", 2), r.sig("xT", 2)
        s_stats, s_var, s_std, s_rstd, zeroed = (r.sem(n) for n in ("stats", "var", "std", "rstd", "zero"))
        logits, m8_ready, i8_ready, dif_ready, exp_ready, den_ready, inv_ready, vals_ready, spread_ready, spread_done, \
            psL_read = (r.sig(n) for n in ("lg", "m8", "i8", "dif", "exp", "den", "inv", "vals", "spr", "sd", "lr"))
        xbd_loaded = r.sig("xld", 2 * 64)
        idx_up, wts_up, idx_down = r.sig("iu", 2), r.sig("wu", 2), r.sig("id", 2)
        gathered = [r.sig(f"g{q}", PARTS * BANKG * TOPK * 16, given=False) for q in range(NQ)]
        weighted = r.sig("wgt", PARTS * NQ)
        first_done, tbd_act, tbd_dve, second_done = (r.sig(n, PARTS * NQ) for n in ("f", "ta", "td", "s"))
        hpre_ready, hid_ready, ht_done, hbd_act, hbd_dve, yT_ready, yt_done = (
            r.sig(n, 2 * NQ) for n in ("hp", "h", "ht", "ha", "hd", "yT", "yt"))
        y_ready, y_stored, y_loaded, x_ready = r.sig("y", 4), r.sig("yst", 32), r.sig("yld", 32), r.sig("x", 2)
        block = ctx.enter_context(nc.Block())

        def alone(eng):
            eng.sem_inc(c.passed, 1)

        def layout(flat, s):
            return flat[ds(s * (STOK * P), STOK * P)].rearrange("(g p j) -> p g j", p=P, j=R32)

        def tokens(flat, s):
            return flat[ds(s * (STOK * P), STOK * P)].rearrange("(t p c) -> p t c", p=P, c=P)

        @block.sync
        def _(sp):
            with sp.Fori(0, NS) as s:
                sp.wait_ge(xn_ready.sem, xn_ready.at(s))
                alone(sp)
                sp.dma_start(tokens(xnd, s), xn[:, :, :]).then_inc(xn_stored.sem, 16)
            sp.wait_ge(xn_stored.sem, xn_stored.at(NS - 1))
            sp.wait_ge(zeroed, 1)
            with sp.Fori(0, NS // 2) as j:
                for v in range(2):
                    sp.wait_ge(first_done.sem, first_done.at(j, v * NQ if v else 2 * NQ - PARTS * NQ))
                    alone(sp)
                    for g in range(4):
                        sp.dma_start(xbd[R32 * g:R32 * g + R32, :, R32 * g:R32 * g + R32],
                                     layout(xnd, 2 * j + v)[R32 * g:R32 * g + R32, :, :]).then_inc(xbd_loaded.sem, 16)
                for v in range(2):
                    sp.wait_ge(y_ready.sem, y_ready.at(j, 2 * v + 2))
                    alone(sp)
                    sp.dma_start(layout(yd, 2 * j + v), y[:, :, :]).then_inc(y_stored.sem, 16)
                    sp.wait_ge(y_stored.sem, y_stored.at(j, 16 * (v + 1)))
                    alone(sp)
                    sp.wait_ge(x_ready.sem, x_ready.at(j, v))
                    alone(sp)
                    sp.dma_start(ytok[:, :, :], tokens(yd, 2 * j + v)).then_inc(y_loaded.sem, 16)
            sp.wait_ge(y_stored.sem, y_stored.at(NS // 2 - 1))

        @block.gpsimd
        def _(pool):
            r.seed(pool)
            nc.gpsimd.memset(chosen[:, NS:, :], 0.0)
            for buf in (xbd, tbd, hbd):
                last = nc.gpsimd.memset(buf[:, :, :] if buf is xbd else buf[:, :, :, :], 0.0)
            last.then_inc(zeroed, 1)
            with pool.Fori(0, NS // 2) as j:
                for p in range(PARTS):
                    table = a["tab_up"] if p < 2 else a["tab_down"]
                    for q in range(NQ):
                        if q == 0 and p < 2:
                            pool.wait_ge(idx_up.sem, idx_up.at(j, p + 1))
                            alone(pool)
                        if q == 0 and p >= 2:
                            pool.wait_ge(idx_down.sem, idx_down.at(j, p - 1))
                            alone(pool)
                        pool.wait_ge(second_done.sem, second_done.at(j, (p - 1) * NQ + q + 1))
                        alone(pool)
                        for n in range(q * BANKG * TOPK, (q + 1) * BANKG * TOPK):
                            nc.gpsimd.indirect_dma_start(
                                tab[:, n // TOPK, n % TOPK, :], None, table,
                                bass.IndirectOffsetOnAxis(ap=idx[:, p, n:n + 1], axis=0)
                            ).then_inc(gathered[q].sem, 16)

        @block.tensor
        def _(pe):
            def spread_out(n):
                pe.wait_ge(spread_ready.sem, spread_ready.at(n))
                nc.tensor.matmul(psL[:, 0:NG * 4], c.sel4, spread[:, :, :].rearrange("p a b -> p (a b)"),
                                 start=True, stop=True).then_inc(spread_done.sem, 1)

            def choose_up(s):
                pe.wait_ge(xn_ready.sem, xn_ready.at(s))
                pe.wait_ge(xnT_ready.sem, xnT_ready.before(s))
                for i in range(2):
                    for t in range(4):
                        last = nc.tensor.transpose(psT[:, i, t * P:(t + 1) * P], xn[:, i * 4 + t, :], c.ident)
                    last.then_inc(t_done.sem, 1)
                pe.wait_ge(xnT_ready.sem, xnT_ready.at(s))
                pe.wait_ge(psL_read.sem, psL_read.before(s))
                for t in range(ROWTOK):
                    last = nc.tensor.matmul(psL[:, 0:NEXP], xnT[:, :].rearrange("p (n t) -> p t n", t=ROWTOK)[:, t, :],
                                            c.WupR[:, t * NEXP:(t + 1) * NEXP], start=(t == 0), stop=(t == ROWTOK - 1))
                last.then_inc(logits.sem, 1)
                spread_out(s)

            def choose_down(j, v):
                n = 2 * j + (NS + v)
                pe.wait_ge(hid_ready.sem, hid_ready.at(j, (v + 1) * NQ))
                pe.wait_ge(psL_read.sem, psL_read.before(n))
                byrow = hid[:, v, :, :].rearrange("p n (g o) -> p o (n g)", o=R32)
                for o in range(R32):
                    last = nc.tensor.matmul(psL[:, 0:NEXP], byrow[:, o, :], c.WdR[:, o * NEXP:(o + 1) * NEXP],
                                            start=(o == 0), stop=(o == R32 - 1))
                last.then_inc(logits.sem, 1)
                spread_out(n)

            def first(j, p, q):
                u = p * NQ + q
                pe.wait_ge(weighted.sem, weighted.at(j, u + 1))
                pe.wait_ge(tbd_act.sem, tbd_act.at(j, u - 1))
                pe.wait_ge(tbd_dve.sem, tbd_dve.at(j, u - 1))
                if p < 2 and q == 0:
                    pe.wait_ge(xbd_loaded.sem, xbd_loaded.at(j, 64 * (p + 1)))
                if p >= 2:
                    pe.wait_ge(hbd_act.sem, hbd_act.at(j, (p - 2) * NQ + q + 1))
                    pe.wait_ge(hbd_dve.sem, hbd_dve.at(j, (p - 2) * NQ + q + 1))
                for i in range(BANKG):
                    n = q * BANKG + i
                    if p < 2:
                        last = nc.tensor.matmul(ps1[:, u % 2, i * P:(i + 1) * P], xbd[:, n, :],
                                                tab[:, n, :, 0:64], start=True, stop=True)
                    else:
                        for jh in range(2):
                            for ih in range(2):
                                last = nc.tensor.matmul(
                                    ps1[:, u % 2, i * P + jh * 64:i * P + jh * 64 + 64],
                                    hbd[:, q % 2, i * 4 + ih * 2 + jh, :],
                                    tab[:, n, :, ih * R32:(ih + 1) * R32], start=(ih == 0), stop=(ih == 1))
                last.then_inc(first_done.sem, 1)

            def second(j, p, q):
                u = p * NQ + q
                pe.wait_ge(tbd_act.sem, tbd_act.at(j, u + 1))
                pe.wait_ge(tbd_dve.sem, tbd_dve.at(j, u + 1))
                if p < 2:
                    pe.wait_ge(hpre_ready.sem, hpre_ready.at(j, u - 1))
                    if u < 2:
                        pe.wait_ge(yT_ready.sem, yT_ready.before(j))
                else:
                    pe.wait_ge(yT_ready.sem, yT_ready.at(j, u - 2 * NQ - 1))
                    if u < 2 * NQ + 2:
                        pe.wait_ge(hpre_ready.sem, hpre_ready.at(j))
                for i in range(BANKG):
                    n = q * BANKG + i
                    if p < 2:
                        for h in range(2):
                            for k in range(TOPK):
                                last = nc.tensor.matmul(
                                    ps2[64 * h:64 * h + 64, q % 2, i * P:(i + 1) * P], tab[:, n, k, 64:P],
                                    tbd[:, u % 2, i * 4 + k * 2 + h, :], start=(k == 0), stop=(k == TOPK - 1))
                    else:
                        for m in range(4):
                            jh, k = divmod(m, 2)
                            last = nc.tensor.matmul(
                                ps2[R32 * i:R32 * i + R32, q % 2, 0:P],
                                tab[:, n, k, 64 + jh * R32:64 + (jh + 1) * R32],
                                tbd[:, u % 2, i * 4 + jh * 2 + k, :], start=(m == 0), stop=(m == 3))
                last.then_inc(second_done.sem, 1)

            def turn_hidden(j, e):
                v, q = divmod(e, NQ)
                pe.wait_ge(hbd_act.sem, hbd_act.at(j, e - 1))
                pe.wait_ge(hbd_dve.sem, hbd_dve.at(j, e - 1))
                for i in range(BANKG):
                    last = nc.tensor.transpose(psT[:, e % 2, i * P:(i + 1) * P], hid[:, v, q * BANKG + i, :], c.ident)
                last.then_inc(ht_done.sem, 1)

            def turn_outputs(j, e):
                pe.wait_ge(yT_ready.sem, yT_ready.at(j, e + 1))
                if e % 4 == 0:
                    pe.wait_ge(y_ready.sem, y_ready.at(j, e // 4))
                nc.tensor.transpose(psY[:, e % 4 * P:(e % 4 + 1) * P], yT[:, e % 2, :], c.ident
                                    ).then_inc(yt_done.sem, 1)

            choose_up(0)
            with pe.Fori(1, NS) as s:
                choose_up(s)
            pe.wait_ge(zeroed, 1)
            warm_up(nc, c, ps1[:, 0, :])
            with pe.Fori(0, NS // 2) as j:
                for v in range(2):
                    for q in range(NQ + 1):
                        if q < NQ:
                            first(j, v, q)
                        if q >= 1:
                            second(j, v, q - 1)
                    choose_down(j, v)
                turn_hidden(j, 0)
                for e in range(2 * NQ + 2):
                    if e + 1 < 2 * NQ:
                        turn_hidden(j, e + 1)
                    if e < 2 * NQ:
                        first(j, 2 + e // NQ, e % NQ)
                    if 1 <= e < 2 * NQ + 1:
                        second(j, 2 + (e - 1) // NQ, (e - 1) % NQ)
                    if e >= 2:
                        turn_outputs(j, e - 2)

        def diagonal(copy, dst, src, g):
            return copy(dst[R32 * g:R32 * g + R32, :, R32 * g:R32 * g + R32],
                        src[R32 * g:R32 * g + R32, :].rearrange("p (a b) -> p a b", b=R32))

        @block.scalar
        def _(act):
            def copy(dst, src):
                return nc.scalar.activation(dst, src, ACT.Copy)

            def exponent(n):
                act.wait_ge(dif_ready.sem, dif_ready.at(n))
                act.wait_ge(vals_ready.sem, vals_ready.before(n))
                nc.scalar.activation(dif[:, 1:2], dif[:, 0:1], ACT.Exp).then_inc(exp_ready.sem, 1)

            def choose_up(s):
                act.wait_ge(logits.sem, logits.before(s))
                for i in range(2):
                    act.wait_ge(t_done.sem, t_done.at(s, i + 1))
                    nc.scalar.activation(xnT[:, i * 512:(i + 1) * 512], psT[:, i, :], ACT.Copy).then_inc(xnT_ready.sem, 1)
                exponent(s)

            def first_to_diagonal(j, p, q):
                u = p * NQ + q
                act.wait_ge(first_done.sem, first_done.at(j, u + 1))
                act.wait_ge(second_done.sem, second_done.at(j, u - 1))
                for g in (0, 1):
                    last = diagonal(copy, tbd[:, u % 2, :, :], ps1[:, u % 2, :], g)
                last.then_inc(tbd_act.sem, 1)

            def hidden_to_diagonal(j, e):
                act.wait_ge(first_done.sem, first_done.at(j, 2 * NQ + e - 1))
                act.wait_ge(ht_done.sem, ht_done.at(j, e + 1))
                for g in (0, 1):
                    last = diagonal(copy, hbd[:, e % 2, :, :], psT[:, e % 2, :], g)
                last.then_inc(hbd_act.sem, 1)

            act.wait_ge(s_var, 1)
            nc.scalar.activation(std[:, :], mv[:, :, 1], ACT.Sqrt, bias=c.eps[:, :], scale=1.0).then_inc(s_std, 1)
            choose_up(0)
            with act.Fori(1, NS) as s:
                choose_up(s)
            act.wait_ge(zeroed, 1)
            with act.Fori(0, NS // 2) as j:
                for v in range(2):
                    for q in range(NQ + 1):
                        if q < NQ:
                            first_to_diagonal(j, v, q)
                        if q >= 1:
                            e = v * NQ + q - 1
                            act.wait_ge(hpre_ready.sem, hpre_ready.at(j, e + 1))
                            act.wait_ge(ht_done.sem, ht_done.before(j, e + 1))
                            nc.scalar.activation(hid[:, v, (q - 1) * BANKG:q * BANKG, :].rearrange("p a b -> p (a b)"),
                                                 hpre[:, (q - 1) % 2, :, :].rearrange("p a b -> p (a b)"),
                                                 ACT.Gelu).then_inc(hid_ready.sem, 1)
                    exponent(2 * j + (NS + v))
                hidden_to_diagonal(j, 0)
                for e in range(2 * NQ + 1):
                    if e + 1 < 2 * NQ:
                        hidden_to_diagonal(j, e + 1)
                    if e < 2 * NQ:
                        first_to_diagonal(j, 2 + e // NQ, e % NQ)
                    if e >= 1:
                        act.wait_ge(second_done.sem, second_done.at(j, 2 * NQ + e))
                        act.wait_ge(yt_done.sem, yt_done.at(j, e - 2))
                        nc.scalar.activation(yT[:, (e - 1) % 2, :], ps2[:, (e - 1) % 2, 0:P], ACT.Copy
                                             ).then_inc(yT_ready.sem, 1)

        @block.vector
        def _(dve):
            def route(n):
                dve.wait_ge(logits.sem, logits.at(n))
                dve.wait_ge(vals_ready.sem, vals_ready.before(n))
                alone(dve)
                nc.vector.max(m8[:, :], psL[:, 0:NEXP]).then_inc(m8_ready.sem, 1)
                dve.wait_ge(m8_ready.sem, m8_ready.at(n))
                nc.vector.tensor_tensor(dif[:, 0:1], m8[:, 1:2], m8[:, 0:1], ALU.subtract).then_inc(dif_ready.sem, 1)
                nc.vector.max_index(i8[:, :], m8[:, :], psL[:, 0:NEXP]).then_inc(i8_ready.sem, 1)
                dve.wait_ge(exp_ready.sem, exp_ready.at(n))
                nc.vector.tensor_scalar(dif[:, 2:3], dif[:, 1:2], 1.0, None, ALU.add).then_inc(den_ready.sem, 1)
                dve.wait_ge(den_ready.sem, den_ready.at(n))
                dve.wait_ge(spread_ready.sem, spread_ready.before(n))
                nc.vector.reciprocal(vals[:, 2:3], dif[:, 2:3]).then_inc(inv_ready.sem, 1)
                dve.wait_ge(i8_ready.sem, i8_ready.at(n))
                nc.vector.tensor_copy(vals[:, 0:2], i8[:, 0:2])
                dve.wait_ge(inv_ready.sem, inv_ready.at(n))
                nc.vector.tensor_tensor(vals[:, 3:4], dif[:, 1:2], vals[:, 2:3], ALU.mult).then_inc(vals_ready.sem, 1)
                dve.wait_ge(vals_ready.sem, vals_ready.at(n))
                dve.wait_ge(spread_done.sem, spread_done.before(n))
                nc.vector.tensor_tensor(spread[:, :, :], c.grp.unsqueeze(2).to_broadcast([P, NG, 4]),
                                        vals[:, :].unsqueeze(1).to_broadcast([P, NG, 4]), ALU.mult
                                        ).then_inc(spread_ready.sem, 1)
                dve.wait_ge(spread_done.sem, spread_done.at(n))

            def settle(p, source, idx_done, wts_done):
                both = source.rearrange("p (n v) -> p n v", v=4)
                nc.vector.tensor_scalar(idx[:, p, :].rearrange("p (n k) -> p n k", k=TOPK), both[:, :, 0:2], float(R32),
                                        c.row32, ALU.mult, ALU.add).then_inc(idx_done.sem, 1)
                nc.vector.tensor_copy(wts[:, p, :].rearrange("p (n k) -> p n k", k=TOPK), both[:, :, 2:4]
                                      ).then_inc(wts_done.sem, 1)

            def choose_up(s):
                dve.wait_ge(xn_stored.sem, xn_stored.before(s))
                dve.wait_ge(t_done.sem, t_done.before(s))
                for t in range(TPU):
                    j = s * TPU + t
                    last = nc.vector.tensor_scalar(xn[:, t, :], one(c.X[:, ds(j, 1), :]), one(mv[:, ds(j, 1), 0:1]),
                                                   rstd[:, ds(j, 1)], ALU.subtract, ALU.mult)
                last.then_inc(xn_ready.sem, 1)
                route(s)
                alone(dve)
                nc.vector.tensor_copy(one(chosen[:, ds(s, 1), :]), psL[:, 0:NG * 4]).then_inc(psL_read.sem, 1)

            def weigh(j, p, q):
                if q == 0 and p < 2:
                    dve.wait_ge(wts_up.sem, wts_up.at(j, p + 1))
                if q == 0 and p >= 2:
                    dve.wait_ge(psL_read.sem, psL_read.at(2 * j + (NS + p - 2)))
                dve.wait_ge(gathered[q].sem, gathered[q].at(j, (p + 1) * BANKG * TOPK * 16))
                part = tab[:, q * BANKG:(q + 1) * BANKG, :, 0:64].rearrange("p n k o -> p (n k) o")
                wt = wts[:, p, q * BANKG * TOPK:(q + 1) * BANKG * TOPK].unsqueeze(2).to_broadcast([P, BANKG * TOPK, 64])
                nc.vector.tensor_tensor(part, part, wt, ALU.mult).then_inc(weighted.sem, 1)

            def first_to_diagonal(j, p, q):
                u = p * NQ + q
                dve.wait_ge(first_done.sem, first_done.at(j, u + 1))
                dve.wait_ge(second_done.sem, second_done.at(j, u - 1))
                for g in (2, 3):
                    last = diagonal(nc.vector.tensor_copy, tbd[:, u % 2, :, :], ps1[:, u % 2, :], g)
                last.then_inc(tbd_dve.sem, 1)

            def hidden_to_diagonal(j, e):
                dve.wait_ge(first_done.sem, first_done.at(j, 2 * NQ + e - 1))
                dve.wait_ge(ht_done.sem, ht_done.at(j, e + 1))
                for g in (2, 3):
                    last = diagonal(nc.vector.tensor_copy, hbd[:, e % 2, :, :], psT[:, e % 2, :], g)
                last.then_inc(hbd_dve.sem, 1)

            def add(j, v):
                dve.wait_ge(y_loaded.sem, y_loaded.at(j, 16 * (v + 1)))
                tiles = ds((2 * j + v) * TPU, TPU)
                nc.vector.tensor_tensor(c.X[:, tiles, :], c.X[:, tiles, :], ytok[:, :, :], ALU.add
                                        ).then_inc(x_ready.sem, 1)

            for t in range(NT):
                last = nc.vector.bn_stats(stats[:, t, :], c.X[:, t, :])
            last.then_inc(s_stats, 1)
            dve.wait_ge(s_stats, 1)
            for t in range(NT):
                last = nc.vector.bn_aggr(mv[:, t, :], stats[:, t, :])
            last.then_inc(s_var, 1)
            dve.wait_ge(s_std, 1)
            nc.vector.reciprocal(rstd[:, :], std[:, :]).then_inc(s_rstd, 1)
            dve.wait_ge(s_rstd, 1)
            choose_up(0)
            dve.wait_ge(psL_read.sem, psL_read.at(0))
            settle(0, chosen[:, 0, :], idx_up, wts_up)
            with dve.Fori(1, NS) as s:
                choose_up(s)
            dve.wait_ge(psL_read.sem, psL_read.at(NS - 1))
            settle(1, chosen[:, 1, :], idx_up, wts_up)
            dve.wait_ge(zeroed, 1)
            with dve.Fori(0, NS // 2) as j:
                for v in range(2):
                    weigh(j, v, 0)
                    for q in range(NQ + 1):
                        if q < NQ:
                            first_to_diagonal(j, v, q)
                        if q + 1 < NQ:
                            weigh(j, v, q + 1)
                        if q >= 1:
                            n = q - 1
                            dve.wait_ge(second_done.sem, second_done.at(j, v * NQ + n + 1))
                            dve.wait_ge(hid_ready.sem, hid_ready.at(j, v * NQ + n - 1))
                            nc.vector.scalar_tensor_tensor(
                                hpre[:, n % 2, :, :], ps2[:, n % 2, :].rearrange("p (a b) -> p a b", b=R32),
                                c.scales[:, 0:1], c.bup[:, :].unsqueeze(1).to_broadcast([P, 16, R32]),
                                ALU.mult, ALU.add).then_inc(hpre_ready.sem, 1)
                    settle(v, one(chosen[:, ds(2 * j + (2 + v), 1), :]), idx_up, wts_up)
                    route(2 * j + (NS + v))
                    settle(2 + v, psL[:, 0:NG * 4], idx_down, psL_read)
                hidden_to_diagonal(j, 0)
                for e in range(2 * NQ + 2):
                    p, q = 2 + e // NQ, e % NQ
                    if e == 0:
                        weigh(j, p, q)
                    if e + 1 < 2 * NQ:
                        hidden_to_diagonal(j, e + 1)
                    if e < 2 * NQ:
                        first_to_diagonal(j, p, q)
                    if e + 1 < 2 * NQ:
                        weigh(j, 2 + (e + 1) // NQ, (e + 1) % NQ)
                    if e % 4 == 1 and e > 4:
                        n = e // 4 - 1
                        dve.wait_ge(yt_done.sem, yt_done.at(j, 4 * (n + 1)))
                        dve.wait_ge(y_stored.sem, y_stored.at(j, n // 2 * 16))
                        nc.vector.scalar_tensor_tensor(
                            y[:, n % 2 * 16:(n % 2 + 1) * 16, :], psY[:, :].rearrange("p (a b) -> p a b", b=R32),
                            c.scales[:, 1:2], c.bdn[:, :].unsqueeze(1).to_broadcast([P, 16, R32]),
                            ALU.mult, ALU.add).then_inc(y_ready.sem, 1)
                    if e == NQ + 4:
                        add(j, 0)
                add(j, 1)
            dve.wait_ge(x_ready.sem, x_ready.at(NS // 2 - 1))


class Norm:

    def __init__(self, nc, c, r):
        self.nc, self.c = nc, c
        self.stats, self.mv = r.sb("stats", [P, TPS, 6]), r.sb("mv", [P, TPS, 2])
        self.std, self.rstd = r.sb("std", [P, TPS]), r.sb("rstd", [P, TPS])
        self.xn, self.xnT, self.psT = r.sb("xn", [P, TPS, P]), r.sb("xnT", [P, L]), r.ps("psT", [P, L])
        self.stat_ready, self.var_ready, self.std_ready, self.rstd_ready, self.xn_ready, self.t_done, self.ready = (
            r.sig(n) for n in ("stat", "var", "std", "rstd", "xn", "t", "xnT"))


    def statistics(self, dve, b):
        for t in range(TPS):
            last = self.nc.vector.bn_stats(self.stats[:, t, :], one(self.c.X[:, ds(b * TPS + t, 1), :]))
        last.then_inc(self.stat_ready.sem, 1)
        dve.wait_ge(self.stat_ready.sem, self.stat_ready.at(b))
        dve.sem_inc(self.c.passed, 1)
        for t in range(TPS):
            last = self.nc.vector.bn_aggr(self.mv[:, t, :], self.stats[:, t, :])
        last.then_inc(self.var_ready.sem, 1)

    def root(self, act, b):
        act.wait_ge(self.var_ready.sem, self.var_ready.at(b))
        self.nc.scalar.activation(self.std[:, :], self.mv[:, :, 1], ACT.Sqrt, bias=self.c.eps[:, :],
                                  scale=1.0).then_inc(self.std_ready.sem, 1)

    def apply(self, dve, b):
        dve.wait_ge(self.std_ready.sem, self.std_ready.at(b))
        self.nc.vector.reciprocal(self.rstd[:, :], self.std[:, :]).then_inc(self.rstd_ready.sem, 1)
        dve.wait_ge(self.t_done.sem, self.t_done.before(b))
        dve.wait_ge(self.rstd_ready.sem, self.rstd_ready.at(b))
        for t in range(TPS):
            last = self.nc.vector.tensor_scalar(self.xn[:, t, :], one(self.c.X[:, ds(b * TPS + t, 1), :]),
                                                self.mv[:, t, 0:1], self.rstd[:, t:t + 1], ALU.subtract, ALU.mult)
        last.then_inc(self.xn_ready.sem, 1)

    def turn(self, pe, b):
        pe.wait_ge(self.xn_ready.sem, self.xn_ready.at(b))
        pe.wait_ge(self.ready.sem, self.ready.before(b))
        for t in range(TPS):
            last = self.nc.tensor.transpose(self.psT[:, t * P:(t + 1) * P], self.xn[:, t, :], self.c.ident)
        last.then_inc(self.t_done.sem, 1)

    def turned(self, act, b, used):
        act.wait_ge(self.t_done.sem, self.t_done.at(b))
        act.wait_ge(used.sem, used.before(b))
        self.nc.scalar.activation(self.xnT[:, :], self.psT[:, :], ACT.Copy).then_inc(self.ready.sem, 1)


def plastic_attention(nc, c):
    with ExitStack() as ctx:
        r = Room(nc, ctx, "s_")
        norm = Norm(nc, c, r)
        wq, wk = r.sb("wq", [P, HD, P]), r.sb("wk", [P, HD, P])
        keep, gain = r.sb("keep", [P, HD]), r.sb("gain", [P, HD])
        v = r.sb("v", [P, L])
        heb, state, syn, z = (r.sb(n, [P, 2, L]) for n in ("heb", "state", "syn", "z"))
        xb = r.sb("xb", [P, TPS, P])
        psV, psO = r.ps("psV", [P, L]), r.ps("psO", [P, L])
        psK, psQ = r.ps("psK", [P, 2, L]), r.ps("psQ", [P, 2, L])
        v_done, v_ready, k_done, q_done = r.sig("vd"), r.sig("v"), r.sig("kd", HD), r.sig("qd", HD)
        heb_ready, state_ready, syn_ready, z_ready, o_done = (r.sig(n, HD) for n in ("heb", "st", "syn", "z", "o"))
        used, xb_ready, x_ready = r.sig("used"), r.sig("xb"), r.sig("x")
        w_ready, sig_ready, set_up = r.sem("w"), r.sem("sg"), r.sem("setup")
        static, lam, gamma = (c.stp[:, n * HD:(n + 1) * HD] for n in range(3))
        block = ctx.enter_context(nc.Block())

        @block.tensor
        def _(pe):
            pe.wait_ge(w_ready, 2)
            norm.turn(pe, 0)

            def sequence(b, more):
                pe.wait_ge(norm.ready.sem, norm.ready.at(b))
                pe.wait_ge(v_ready.sem, v_ready.before(b))
                nc.tensor.matmul(psV[:, :], c.Wqkv[:, 2 * P:3 * P], norm.xnT[:, :], start=True, stop=True
                                 ).then_inc(v_done.sem, 1)
                for j in range(HD + 2):
                    if j < HD:
                        pe.wait_ge(heb_ready.sem, heb_ready.at(b, j - 1))
                        nc.tensor.matmul(psK[:, j % 2, :], wk[:, j, :], norm.xnT[:, :], start=True, stop=True
                                         ).then_inc(k_done.sem, 1)
                        pe.wait_ge(z_ready.sem, z_ready.at(b, j - 1))
                        last = nc.tensor.matmul(psQ[:, j % 2, :], wq[:, j, :], norm.xnT[:, :], start=True, stop=True)
                        last.then_inc(q_done.sem, 1)
                    if j == HD - 1:
                        pe.drain().then_inc(used.sem, 1)
                    if j == HD and more:
                        norm.turn(pe, b + 1)
                    if j >= 2:
                        n = j - 2
                        pe.wait_ge(z_ready.sem, z_ready.at(b, n + 1))
                        if n == 0:
                            pe.wait_ge(x_ready.sem, x_ready.before(b))
                        for t in range(TPS):
                            last = nc.tensor.matmul(psO[:, t * P:(t + 1) * P], z[:, n % 2, t * P:(t + 1) * P],
                                                    c.outW[:, :], start=(n == 0 and t == 0), stop=(n == HD - 1),
                                                    skip_group_check=True)
                        last.then_inc(o_done.sem, 1)

            with pe.Fori(0, B - 1) as b:
                sequence(b, True)
            sequence(B - 1, False)

        @block.scalar
        def _(act):
            nc.scalar.activation(keep[:, :], lam, ACT.Sigmoid).then_inc(sig_ready, 1)
            norm.root(act, 0)
            norm.turned(act, 0, used)

            def sequence(b, more):
                act.wait_ge(v_done.sem, v_done.at(b))
                act.wait_ge(heb_ready.sem, heb_ready.before(b))
                nc.scalar.activation(v[:, :], psV[:, :], ACT.Identity, bias=c.bqkv[:, 0:1]).then_inc(v_ready.sem, 1)
                for j in range(HD):
                    act.wait_ge(state_ready.sem, state_ready.at(b, j + 1))
                    act.wait_ge(z_ready.sem, z_ready.at(b, j - 1))
                    nc.scalar.activation(syn[:, j % 2, :], state[:, j % 2, :], ACT.Identity, bias=static[:, j:j + 1],
                                         scale=gain[:, j:j + 1]).then_inc(syn_ready.sem, 1)
                    if j == 4 and more:
                        norm.root(act, b + 1)
                if more:
                    norm.turned(act, b + 1, used)

            act.wait_ge(set_up, 2)
            with act.Fori(0, B - 1) as b:
                sequence(b, True)
            sequence(B - 1, False)

        @block.gpsimd
        def _(pool):
            r.seed(pool)

            def sequence(b):
                pool.wait_ge(x_ready.sem, x_ready.before(b))
                nc.gpsimd.tensor_tensor(xb[:, :, :], c.X[:, ds(b * TPS, TPS), :],
                                        c.rows[:, 3, :].unsqueeze(1).to_broadcast([P, TPS, P]),
                                        ALU.add).then_inc(xb_ready.sem, 1)

            with pool.Fori(0, B) as b:
                sequence(b)

        @block.vector
        def _(dve):
            for dst, at in ((wq, 0), (wk, P)):
                nc.vector.tensor_copy(
                    dst[:, :, :].rearrange("p j (h i) -> p j h i", h=H),
                    c.Wqkv[:, at:at + P].rearrange("p (h j) -> p j h", h=H).unsqueeze(3).to_broadcast([P, HD, H, HD])
                ).then_inc(w_ready, 1)
            nc.vector.tensor_scalar(gain[:, :], gamma, QSCALE, None, ALU.mult).then_inc(set_up, 1)
            dve.wait_ge(sig_ready, 1)
            nc.vector.tensor_scalar(keep[:, :], keep[:, :], -1.0, 1.0, ALU.mult, ALU.add).then_inc(set_up, 1)
            dve.wait_ge(set_up, 2)
            norm.statistics(dve, 0)
            norm.apply(dve, 0)

            def sequence(b, more):
                for j in range(HD + 2):
                    if j >= 2:
                        n = j - 2
                        dve.wait_ge(syn_ready.sem, syn_ready.at(b, n + 1))
                        dve.wait_ge(q_done.sem, q_done.at(b, n + 1))
                        dve.wait_ge(o_done.sem, o_done.at(b, n - 1))
                        nc.vector.scalar_tensor_tensor(z[:, n % 2, :], psQ[:, n % 2, :], c.bqkv[:, 2 + n:3 + n],
                                                       syn[:, n % 2, :], ALU.add, ALU.mult).then_inc(z_ready.sem, 1)
                    if j < HD:
                        dve.wait_ge(k_done.sem, k_done.at(b, j + 1))
                        if j == 0:
                            dve.wait_ge(v_ready.sem, v_ready.at(b))
                        dve.wait_ge(state_ready.sem, state_ready.at(b, j - 1))
                        nc.vector.scalar_tensor_tensor(heb[:, j % 2, :], psK[:, j % 2, :],
                                                       c.bqkv[:, 2 + HD + j:3 + HD + j], v[:, :], ALU.add, ALU.mult
                                                       ).then_inc(heb_ready.sem, 1)
                    if j < HD:
                        dve.wait_ge(heb_ready.sem, heb_ready.at(b, j + 1))
                        dve.wait_ge(syn_ready.sem, syn_ready.at(b, j - 1))
                        nc.vector.tensor_tensor_scan(state[:, j % 2, :], keep[:, j:j + 1].to_broadcast([P, L]),
                                                     heb[:, j % 2, :], 0.0, ALU.mult, ALU.add
                                                     ).then_inc(state_ready.sem, 1)
                    if j == 3 and more:
                        norm.statistics(dve, b + 1)
                    if j == 6 and more:
                        norm.apply(dve, b + 1)
                dve.wait_ge(o_done.sem, o_done.at(b))
                dve.wait_ge(xb_ready.sem, xb_ready.at(b))
                nc.vector.tensor_tensor(c.X[:, ds(b * TPS, TPS), :], psO[:, :].rearrange("p (t c) -> p t c", c=P),
                                        xb[:, :, :], ALU.add).then_inc(x_ready.sem, 1)

            with dve.Fori(0, B - 1) as b:
                sequence(b, True)
            sequence(B - 1, False)
            dve.wait_ge(x_ready.sem, x_ready.at(B - 1))


def gated_feed_forward(nc, c, out):
    with ExitStack() as ctx:
        r = Room(nc, ctx, "f_")
        norm = Norm(nc, c, r)
        gated, hidden = r.sb("gated", [P, 2, L]), r.sb("hidden", [P, HM, L])
        res = r.sb("res", [P, 2, L])
        psG, psU, psO = r.ps("psG", [P, 2, L]), r.ps("psU", [P, 2, L]), r.ps("psO", [P, L])
        g_done, u_done, gated_ready, hidden_ready = (r.sig(n, HM) for n in ("g", "u", "gt", "h"))
        used, o_done, x_ready, stored = r.sig("used"), r.sig("o"), r.sig("x"), r.sig("out", 16)

        block = ctx.enter_context(nc.Block())

        @block.sync
        def _(sp):
            with sp.Fori(0, B) as b:
                sp.wait_ge(x_ready.sem, x_ready.at(b))
                sp.sem_inc(c.passed, 1)
                sp.dma_start(out[ds(b * L, L), :].rearrange("(t p) c -> p t c", p=P),
                             c.X[:, ds(b * TPS, TPS), :]).then_inc(stored.sem, 16)
            sp.wait_ge(stored.sem, stored.at(B - 1))

        @block.tensor
        def _(pe):
            norm.turn(pe, 0)

            def sequence(b, more):
                pe.wait_ge(norm.ready.sem, norm.ready.at(b))
                for m in range(HM):
                    pe.wait_ge(gated_ready.sem, gated_ready.at(b, m - 1))
                    nc.tensor.matmul(psG[:, m % 2, :], c.Wint[:, m * P:(m + 1) * P], norm.xnT[:, :],
                                     start=True, stop=True).then_inc(g_done.sem, 1)
                    pe.wait_ge(hidden_ready.sem, hidden_ready.at(b, m - 1))
                    last = nc.tensor.matmul(psU[:, m % 2, :], c.Wint[:, (HM + m) * P:(HM + m + 1) * P],
                                            norm.xnT[:, :], start=True, stop=True)
                    last.then_inc(u_done.sem, 1)
                pe.drain().then_inc(used.sem, 1)
                if more:
                    norm.turn(pe, b + 1)
                pe.wait_ge(hidden_ready.sem, hidden_ready.at(b))
                pe.wait_ge(x_ready.sem, x_ready.before(b))
                for t in range(TPS):
                    for m in range(HM):
                        last = nc.tensor.matmul(psO[:, t * P:(t + 1) * P], hidden[:, m, t * P:(t + 1) * P],
                                                c.Wint[:, (2 * HM + m) * P:(2 * HM + m + 1) * P],
                                                start=(m == 0), stop=(m == HM - 1))
                last.then_inc(o_done.sem, 1)

            with pe.Fori(0, B - 1) as b:
                sequence(b, True)
            sequence(B - 1, False)

        @block.scalar
        def _(act):
            norm.root(act, 0)
            norm.turned(act, 0, used)

            def sequence(b, more):
                if more:
                    norm.root(act, b + 1)
                for m in range(HM):
                    act.wait_ge(g_done.sem, g_done.at(b, m + 1))
                    act.wait_ge(hidden_ready.sem, hidden_ready.at(b, m - 1))
                    nc.scalar.activation(gated[:, m % 2, :], psG[:, m % 2, :], ACT.Silu).then_inc(gated_ready.sem, 1)
                if more:
                    norm.turned(act, b + 1, used)

            with act.Fori(0, B - 1) as b:
                sequence(b, True)
            sequence(B - 1, False)

        @block.gpsimd
        def _(pool):
            r.seed(pool)

        @block.vector
        def _(dve):
            norm.statistics(dve, 0)
            norm.apply(dve, 0)

            def sequence(b, more):
                if more:
                    norm.statistics(dve, b + 1)
                    norm.apply(dve, b + 1)
                for m in range(HM):
                    dve.wait_ge(gated_ready.sem, gated_ready.at(b, m + 1))
                    dve.wait_ge(u_done.sem, u_done.at(b, m + 1))
                    dve.wait_ge(o_done.sem, o_done.before(b))
                    nc.vector.tensor_tensor(hidden[:, m, :], psU[:, m % 2, :], gated[:, m % 2, :], ALU.mult
                                            ).then_inc(hidden_ready.sem, 1)
                dve.wait_ge(o_done.sem, o_done.at(b))
                nc.vector.tensor_tensor(c.X[:, ds(b * TPS, TPS), :], psO[:, :].rearrange("p (t c) -> p t c", c=P),
                                        c.X[:, ds(b * TPS, TPS), :], ALU.add).then_inc(x_ready.sem, 1)

            with dve.Fori(0, B - 1) as b:
                sequence(b, True)
            sequence(B - 1, False)


def build(nc, a, out):
    scratch = {
        "kd": ((B, P, 3, L), BF16),
        "qd": ((B, P, TPS * H * KROWS), BF16),
        "posd": ((P, L), BF16),
        "xnd": ((N * P,), F32),
        "yd": ((N * P,), F32),
    }
    kd, qd, posd, xnd, yd = (nc.dram_tensor(n, s, d).ap() for n, (s, d) in scratch.items())
    with ExitStack() as ctx:
        c = Room(nc, ctx, "c_")
        c.passed = c.sem("passed")
        c.X = c.sb("X", [P, NT, P])
        c.consts = c.sb("consts", [P, 3 * P + NG + 2])
        c.ident = c.consts[:, 0:P]
        c.sel4 = c.consts[:, 2 * P:3 * P]
        c.grp = c.consts[:, 3 * P:3 * P + NG]
        c.slot1 = c.consts[:, 3 * P + NG:3 * P + NG + 1]
        c.row32 = c.consts[:, 3 * P + NG + 1:3 * P + NG + 2]
        c.iota1 = c.sb("iota1", [P, P], BF16)
        c.ones, c.eps, c.mean_ones = c.sb("ones", [P, 1]), c.sb("eps", [P, 1]), c.sb("mean_ones", [P, P])
        c.W, c.rows, c.cols = c.sb("W", [P, 4, P]), c.sb("rows", [P, 4, P]), c.sb("cols", [P, 1])
        c.Wint = c.sb("Wint", [P, 3 * HM * P])
        c.WupR, c.WdR = c.sb("WupR", [P, ROWTOK * NEXP]), c.sb("WdR", [P, 32 * NEXP])
        c.scales, c.bup, c.bdn = c.sb("scales", [P, 2]), c.sb("bup", [P, 32]), c.sb("bdn", [P, 32])
        c.Wqkv, c.outW, c.bqkv, c.stp = (c.sb("Wqkv", [P, 3 * P]), c.sb("outW", [P, P]),
                                         c.sb("bqkv", [P, 2 + 2 * HD]), c.sb("stp", [P, 3 * HD]))
        load(nc, c, a)
        with ExitStack() as att:
            t = Room(nc, att, "c0_")
            c.V, c.VM, c.QN, c.posT = (t.sb("V", [P, B, L]), t.sb("VM", [P, B, P]), t.sb("QN", [P, TPS, P]),
                                       t.sb("posT", [P, TPS, P]))
            attention_projections(nc, c, kd, qd)
            top_queries(nc, c, posd)
            attention(nc, c, kd, qd, posd)
        experts(nc, c, a, xnd, yd)
        plastic_attention(nc, c)
        gated_feed_forward(nc, c, out)


def kernel(**inputs):
    import numpy as _np
    import concourse.bacc as _bacc
    from concourse import mybir as _mybir
    from concourse.bass_utils import run_bass_kernel_spmd as _run

    def turned(name):
        return inputs[name].T

    i = {k: _np.asarray(v) for k, v in inputs.items()}
    n = _np.arange(P)
    consts = _np.concatenate([
        _np.eye(P), _np.tile(n + 1.0, (P, 1)), n[:, None] % G4 == n[None, :] // 32,
        n[:, None] // G4 == _np.arange(NG)[None, :], n[:, None] + 1.0, n[:, None] % 32,
    ], axis=1).astype(_np.float32)
    arrays = {
        "x": i["L0_attn_x"].reshape(N, P), "consts": consts,
        "WqT": i["L0_attn_Wq"].T, "WkT": i["L0_attn_Wk"].T, "WvT": i["L0_attn_Wv"].T, "WoT": i["L0_attn_Wo"].T,
        "bq": i["L0_attn_bq"], "bk": i["L0_attn_bk"].reshape(P, 1), "bv": i["L0_attn_bv"], "bo": i["L0_attn_bo"],
        "WupR": i["L0_ffn_W_up"].reshape(NEXP, ROWTOK, P).transpose(2, 1, 0).reshape(P, -1),
        "tab_up": _np.concatenate([i["L0_ffn_A_up"].transpose(0, 2, 1), i["L0_ffn_B_up"].transpose(0, 2, 1)],
                                  axis=2).reshape(NEXP * 32, P),
        "tab_down": _np.concatenate([
            i[f"L0_ffn_{m}_down"].transpose(0, 2, 1).reshape(NEXP, 2, 32, 32).transpose(0, 2, 1, 3).reshape(NEXP, 32, 64)
            for m in "AB"], axis=2).reshape(NEXP * 32, P),
        "bias_up": i["L0_ffn_bias_up"].reshape(2, 32, 64).transpose(0, 2, 1).reshape(P, 32),
        "bias_down": i["L0_ffn_bias_down"].reshape(32, 32),
        "scale_up": i["L0_ffn_scale_up"], "scale_down": i["L0_ffn_scale_down"],
        "WdR": i["L0_ffn_W_down"].reshape(NEXP, 2, 32, 64).transpose(1, 3, 2, 0).reshape(P, -1),
        "WqkvT": i["L1_attn_Wqkv_w"].T, "out_wT": i["L1_attn_out_w"].T, "out_b": i["L1_attn_out_b"],
        "bqkv": _np.concatenate([
            i["L1_attn_Wqkv_b"][2 * P:].reshape(P, 1), i["L1_attn_Wqkv_b"][2 * P:].reshape(P, 1),
            _np.repeat(i["L1_attn_Wqkv_b"][:P].reshape(H, HD), HD, axis=0),
            _np.repeat(i["L1_attn_Wqkv_b"][P:2 * P].reshape(H, HD), HD, axis=0)], axis=1),
        "stp": _np.concatenate([i[f"L1_attn_{m}"].reshape(P, HD) for m in ("W_static", "Lambda_raw", "Gamma")], axis=1),
        "w_gateT": i["L1_ffn_w_gate"].T, "w_upT": i["L1_ffn_w_up"].T, "w_downT": i["L1_ffn_w_down"].T,
    }
    arrays = {f"in_{k}": _np.ascontiguousarray(v) for k, v in arrays.items()}
    nc = _bacc.Bacc("TRN2", target_bir_lowering=False, num_devices=1)
    a = {k[3:]: nc.dram_tensor(k, v.shape, _mybir.dt.from_np(v.dtype), kind="ExternalInput").ap()
         for k, v in arrays.items()}
    out = nc.dram_tensor("out_x", (N, P), F32, kind="ExternalOutput").ap()
    build(nc, a, out)
    r = _run(nc, [arrays], core_ids=[0])
    return r.results[0]["out_x"].reshape(B, L, P)
```

```python
import concourse.bass as bass
from concourse import mybir
from concourse.bass import ds
from contextlib import ExitStack

P = 128
B, L = 8, 512
N = B * L
TPS = L // P
NT = N // P
H, HD = 16, 8
KTOP = int(L * 0.2)
ROUNDS = -(-KTOP // 8)
LAST = KTOP - 8 * (ROUNDS - 1)
QPART = [0, 0, 0, 1, 1, 2]
KPART = [0, 1, 2, 0, 1, 0]
NPROD = len(QPART)
KROWS = NPROD * HD
QSCALE = float(HD) ** -0.5
NEXP, TOPK = 64, 2
ROWTOK = 8
SROWS = 128
STOK = SROWS * ROWTOK
TPU = STOK // P
NS = N // STOK
G4 = 4
NG = SROWS // G4
NQ = NG // 4
HM = 3
EPS = 1e-5
WARM = 5

F32 = mybir.dt.float32
BF16 = mybir.dt.bfloat16
I32 = mybir.dt.int32
U32 = mybir.dt.uint32
ALU = mybir.AluOpType
ACT = mybir.ActivationFunctionType
AX = mybir.AxisListType


class Sig:

    def __init__(self, sem, per=1, given=True):
        self.sem, self.per, self.given = sem, per, given

    def seed(self, eng):
        if self.given:
            eng.sem_inc(self.sem, self.per)

    def at(self, turn, k=None):
        return (turn + self.given) * self.per + (self.per if k is None else k)

    def before(self, turn, k=None):
        assert self.given
        return turn * self.per + (self.per if k is None else k)


class Room:

    def __init__(self, nc, ctx, name):
        self.nc, self.ctx, self.name = nc, ctx, name
        self.sigs, self.sems = [], []

    def sb(self, name, shape, dt=F32):
        return self.ctx.enter_context(self.nc.sbuf_tensor(self.name + name, shape, dt))

    def ps(self, name, shape, dt=F32):
        return self.ctx.enter_context(self.nc.psum_tensor(self.name + name, shape, dt))

    def sem(self, name):
        self.sems.append(self.ctx.enter_context(self.nc.semaphore(self.name + name)))
        return self.sems[-1]

    def clear(self):
        self.nc.gpsimd.drain()
        for s in self.sems:
            self.nc.gpsimd.sem_clear(s)
        self.nc.all_engine_barrier()

    def sig(self, name, per=1, given=True):
        self.sigs.append(Sig(self.sem(name), per, given))
        return self.sigs[-1]

    def seed(self, eng):
        for s in self.sigs:
            s.seed(eng)


def one(ap):
    if len(ap.shape) == 3:
        return ap.rearrange("p o c -> p (o c)")
    return ap.rearrange("p o t c -> p (o t) c")


def warm_up(nc, c, ps):
    for _ in range(WARM):
        nc.tensor.matmul(ps, c.ident, c.Wint[:, 0:512], start=True, stop=True)


def load(nc, c, a):
    with ExitStack() as ctx:
        r = Room(nc, ctx, "ld_")
        s_in, s_int = r.sem("in"), r.sem("int")
        ints = r.sb("ints", [P, 3 * HM * P], I32)
        ctx.callback(r.clear)
        block = ctx.enter_context(nc.Block())
        loads = [
            (c.X[:, :, :], a["x"].rearrange("(t p) c -> p t c", p=P)),
            (c.consts[:, :], a["consts"]),
            (c.W[:, 0, :], a["WqT"]), (c.W[:, 1, :], a["WkT"]), (c.W[:, 2, :], a["WvT"]), (c.W[:, 3, :], a["WoT"]),
            (c.rows[:, 0, :], a["bq"].partition_broadcast(P)), (c.rows[:, 1, :], a["bv"].partition_broadcast(P)),
            (c.rows[:, 2, :], a["bo"].partition_broadcast(P)), (c.rows[:, 3, :], a["out_b"].partition_broadcast(P)),
            (c.cols[:, 0:1], a["bk"]),
            (ints[:, 0:HM * P], a["w_gateT"]), (ints[:, HM * P:2 * HM * P], a["w_upT"]),
            (ints[:, 2 * HM * P:].rearrange("p (m c) -> p m c", m=HM), a["w_downT"].rearrange("(m p) c -> p m c", p=P)),
            (c.WupR[:, :], a["WupR"]), (c.WdR[:, :], a["WdR"]),
            (c.scales[:, 0:1], a["scale_up"].partition_broadcast(P)),
            (c.scales[:, 1:2], a["scale_down"].partition_broadcast(P)),
            (c.Wqkv[:, :], a["WqkvT"]), (c.outW[:, :], a["out_wT"]), (c.bqkv[:, :], a["bqkv"]),
            (c.stp[:, :], a["stp"]),
            (c.bup[:, :], a["bias_up"]),
        ] + [(c.bdn[32 * i:32 * i + 32, :], a["bias_down"]) for i in range(4)]

        @block.sync
        def _(sp):
            for dst, src in loads:
                sp.dma_start(dst, src).then_inc(s_in, 16)

        @block.vector
        def _(dve):
            nc.vector.memset(c.mean_ones[:, :], 1.0 / L)
            nc.vector.memset(c.ones[:, :], 1.0)
            nc.vector.memset(c.eps[:, :], EPS)
            dve.wait_ge(s_in, 16 * len(loads))
            nc.vector.tensor_copy(c.Wint[:, :], ints[:, :]).then_inc(s_int, 1)
            nc.vector.tensor_copy(c.iota1[:, :], c.consts[:, P:2 * P])
            dve.wait_ge(s_int, 1)
            nc.vector.tensor_scalar(c.Wint[:, :], c.Wint[:, :], 1.0 / 127.0, None, ALU.mult).then_inc(s_int, 1)
            dve.wait_ge(s_int, 2)


def attention_projections(nc, c, kd, qd):
    with ExitStack() as ctx:
        r = Room(nc, ctx, "a1_")
        stats, mv = r.sb("stats", [P, NT, 6]), r.sb("mv", [P, NT, 2])
        std, rstd = r.sb("std", [P, NT]), r.sb("rstd", [P, NT])
        xn = r.sb("xn", [P, TPS, P])
        xnT = r.sb("xnT", [P, L])
        q, q2, qs = r.sb("q", [P, L]), r.sb("q2", [P, L]), r.sb("qs", [P, L])
        qres = r.sb("qres", [P, L])
        kres = r.sb("kres", [P, L])
        k3 = r.sb("k3", [P, 3, L], BF16)
        vcur = r.sb("vcur", [P, L])
        q6 = r.sb("q6", [P, TPS * H * KROWS], BF16)
        parts = q6[:, :].rearrange("p (a c d) -> p a c d", c=NPROD, d=HD)
        q_stored = r.sig("q6st", 16)
        psT, psK, psQ, psV = (r.ps(n, [P, L]) for n in ("psT", "psK", "psQ", "psV"))
        psM = r.ps("psM", [P, 512])
        s_stats, s_var, s_std, s_rstd = (r.sem(n) for n in ("stats", "var", "std", "rstd"))
        xn_ready, t_done, xnT_ready = r.sig("xn"), r.sig("t"), r.sig("xnT")
        k_done, q_done, v_done, m_done = r.sig("k"), r.sig("q"), r.sig("v"), r.sig("m")
        khi, kres_ready, kmid, klo = r.sig("khi"), r.sig("kres"), r.sig("kmid"), r.sig("klo")
        k_stored = r.sig("kst", 16)
        q_ready, q2_ready, qs_ready, qn_ready = r.sig("qf"), r.sig("q2"), r.sig("qs"), r.sig("qn")
        qhi, qres_ready, qmid, qlo = r.sig("qhi"), r.sig("qres"), r.sig("qmid"), r.sig("qlo")
        v_ready, v_stored, mean_ready = r.sig("vf"), r.sig("vst", 16), r.sig("mean")
        bq_row = c.rows[:, 0, :].unsqueeze(1).to_broadcast([P, TPS, P])
        bv_row = c.rows[:, 1, :].unsqueeze(1).to_broadcast([P, TPS, P])
        ctx.callback(r.clear)
        block = ctx.enter_context(nc.Block())

        def tiles(ap):
            return ap.rearrange("p (t c) -> p t c", c=P)

        def heads(buf):
            return buf[:, :].rearrange("p (a d) -> p a d", d=HD)

        @block.sync
        def _(sp):
            with sp.Fori(0, B) as b:
                sp.wait_ge(klo.sem, klo.at(b))
                sp.dma_start(kd[ds(b, 1), :, :, :].rearrange("o p c t -> (o p) c t"),
                             k3[:, :, :]).then_inc(k_stored.sem, 16)
                sp.wait_ge(v_ready.sem, v_ready.at(b))
                sp.dma_start(one(c.V[:, ds(b, 1), :]), vcur[:, :]).then_inc(v_stored.sem, 16)
                sp.wait_ge(qlo.sem, qlo.at(b))
                sp.dma_start(one(qd[ds(b, 1), :, :].rearrange("o p n -> p o n")), q6[:, :]).then_inc(q_stored.sem, 16)
            sp.wait_ge(k_stored.sem, k_stored.at(B - 1))
            sp.wait_ge(q_stored.sem, q_stored.at(B - 1))
            sp.wait_ge(v_stored.sem, v_stored.at(B - 1))

        @block.tensor
        def _(pe):
            def turn(b):
                pe.wait_ge(xn_ready.sem, xn_ready.at(b))
                pe.wait_ge(xnT_ready.sem, xnT_ready.before(b))
                for t in range(TPS):
                    last = nc.tensor.transpose(psT[:, t * P:(t + 1) * P], xn[:, t, :], c.ident)
                last.then_inc(t_done.sem, 1)

            def sequence(b, more):
                pe.wait_ge(xnT_ready.sem, xnT_ready.at(b))
                pe.wait_ge(kres_ready.sem, kres_ready.before(b))
                nc.tensor.matmul(psK[:, :], c.W[:, 1, :], xnT[:, :], start=True, stop=True).then_inc(k_done.sem, 1)
                pe.wait_ge(q_ready.sem, q_ready.before(b))
                for t in range(TPS):
                    last = nc.tensor.matmul(psQ[:, t * P:(t + 1) * P], xnT[:, t * P:(t + 1) * P], c.W[:, 0, :],
                                            start=True, stop=True)
                last.then_inc(q_done.sem, 1)
                pe.wait_ge(v_ready.sem, v_ready.before(b))
                for t in range(TPS):
                    last = nc.tensor.matmul(psV[:, t * P:(t + 1) * P], xnT[:, t * P:(t + 1) * P], c.W[:, 2, :],
                                            start=True, stop=True)
                last.then_inc(v_done.sem, 1)
                if more:
                    turn(b + 1)
                pe.wait_ge(v_ready.sem, v_ready.at(b))
                pe.wait_ge(mean_ready.sem, mean_ready.before(b))
                for t in range(TPS):
                    last = nc.tensor.matmul(psM[:, 0:P], c.mean_ones[:, :], vcur[:, t * P:(t + 1) * P],
                                            start=(t == 0), stop=(t == TPS - 1))
                last.then_inc(m_done.sem, 1)

            turn(0)
            with pe.Fori(0, B - 1) as b:
                sequence(b, True)
            sequence(B - 1, False)

        @block.scalar
        def _(act):
            act.wait_ge(s_var, 1)
            nc.scalar.activation(std[:, :], mv[:, :, 1], ACT.Sqrt, bias=c.eps[:, :], scale=1.0).then_inc(s_std, 1)

            def turned(b):
                act.wait_ge(t_done.sem, t_done.at(b))
                act.wait_ge(v_done.sem, v_done.before(b))
                nc.scalar.activation(xnT[:, :], psT[:, :], ACT.Copy).then_inc(xnT_ready.sem, 1)

            def sequence(b, more):
                act.wait_ge(k_done.sem, k_done.at(b))
                act.wait_ge(k_stored.sem, k_stored.before(b))
                nc.scalar.activation(k3[:, 0, :], psK[:, :], ACT.Identity, bias=c.cols[:, 0:1]).then_inc(khi.sem, 1)
                act.wait_ge(q_ready.sem, q_ready.at(b))
                act.wait_ge(qn_ready.sem, qn_ready.before(b))
                nc.scalar.activation(q2[:, :], q[:, :], ACT.Square).then_inc(q2_ready.sem, 1)
                act.wait_ge(kres_ready.sem, kres_ready.at(b))
                nc.scalar.activation(k3[:, 1, :], kres[:, :], ACT.Copy).then_inc(kmid.sem, 1)
                if more:
                    turned(b + 1)
                act.wait_ge(qs_ready.sem, qs_ready.at(b))
                act.wait_ge(q_stored.sem, q_stored.before(b))
                nc.scalar.activation(parts[:, :, 0:3, :], heads(qs).unsqueeze(2).to_broadcast([P, TPS * H, 3, HD]),
                                     ACT.Copy).then_inc(qhi.sem, 1)
                act.wait_ge(qres_ready.sem, qres_ready.at(b))
                nc.scalar.activation(parts[:, :, 3:5, :], heads(qres).unsqueeze(2).to_broadcast([P, TPS * H, 2, HD]),
                                     ACT.Copy).then_inc(qmid.sem, 1)
                act.wait_ge(m_done.sem, m_done.at(b))
                nc.scalar.activation(one(c.VM[:, ds(b, 1), :]), psM[:, 0:P], ACT.Copy).then_inc(mean_ready.sem, 1)

            turned(0)
            with act.Fori(0, B - 1) as b:
                sequence(b, True)
            sequence(B - 1, False)

        @block.gpsimd
        def _(pool):
            r.seed(pool)
            with pool.Fori(0, B) as b:
                pool.wait_ge(kmid.sem, kmid.at(b))
                nc.gpsimd.tensor_tensor(k3[:, 2, :], kres[:, :], k3[:, 1, :], ALU.subtract).then_inc(klo.sem, 1)

        @block.vector
        def _(dve):
            for t in range(NT):
                last = nc.vector.bn_stats(stats[:, t, :], c.X[:, t, :])
            last.then_inc(s_stats, 1)
            dve.wait_ge(s_stats, 1)
            for t in range(NT):
                last = nc.vector.bn_aggr(mv[:, t, :], stats[:, t, :])
            last.then_inc(s_var, 1)
            dve.wait_ge(s_std, 1)
            nc.vector.reciprocal(rstd[:, :], std[:, :]).then_inc(s_rstd, 1)
            dve.wait_ge(s_rstd, 1)

            def normalise(b):
                dve.wait_ge(t_done.sem, t_done.before(b))
                for t in range(TPS):
                    j = b * TPS + t
                    last = nc.vector.tensor_scalar(xn[:, t, :], one(c.X[:, ds(j, 1), :]), one(mv[:, ds(j, 1), 0:1]),
                                                   rstd[:, ds(j, 1)], ALU.subtract, ALU.mult)
                last.then_inc(xn_ready.sem, 1)

            def sequence(b, more):
                dve.wait_ge(khi.sem, khi.at(b))
                dve.wait_ge(klo.sem, klo.before(b))
                nc.vector.scalar_tensor_tensor(kres[:, :], psK[:, :], c.cols[:, 0:1], k3[:, 0, :],
                                               ALU.add, ALU.subtract).then_inc(kres_ready.sem, 1)
                dve.wait_ge(q_done.sem, q_done.at(b))
                dve.wait_ge(q2_ready.sem, q2_ready.before(b))
                nc.vector.tensor_tensor(tiles(q[:, :]), tiles(psQ[:, :]), bq_row, ALU.add).then_inc(q_ready.sem, 1)
                dve.wait_ge(v_done.sem, v_done.at(b))
                dve.wait_ge(v_stored.sem, v_stored.before(b))
                dve.wait_ge(m_done.sem, m_done.before(b))
                nc.vector.tensor_tensor(tiles(vcur[:, :]), tiles(psV[:, :]), bv_row, ALU.add).then_inc(v_ready.sem, 1)
                if more:
                    normalise(b + 1)
                dve.wait_ge(q_ready.sem, q_ready.at(b))
                dve.wait_ge(qres_ready.sem, qres_ready.before(b))
                nc.vector.tensor_scalar(qs[:, :], q[:, :], QSCALE, None, ALU.mult).then_inc(qs_ready.sem, 1)
                dve.wait_ge(q2_ready.sem, q2_ready.at(b))
                nc.vector.tensor_reduce(c.QN[:, :, ds(b * H, H)], q2[:, :].rearrange("p (t h d) -> p t h d", h=H, d=HD),
                                        AX.X, ALU.add).then_inc(qn_ready.sem, 1)
                dve.wait_ge(qhi.sem, qhi.at(b))
                dve.wait_ge(qlo.sem, qlo.before(b))
                nc.vector.tensor_tensor(heads(qres), heads(qs), parts[:, :, 0, :], ALU.subtract
                                        ).then_inc(qres_ready.sem, 1)
                dve.wait_ge(qmid.sem, qmid.at(b))
                nc.vector.tensor_tensor(parts[:, :, 5, :], heads(qres), parts[:, :, 3, :], ALU.subtract
                                        ).then_inc(qlo.sem, 1)

            normalise(0)
            with dve.Fori(0, B - 1) as b:
                sequence(b, True)
            sequence(B - 1, False)


class TopQueries:
    REPLACED = -1000.0
    FILL = 8 - LAST

    def __init__(self, nc, c, r, psN, psP, mask, cum, pos):
        self.nc, self.c, self.psN, self.psP = nc, c, psN, psP
        self.mask, self.cum, self.pos = mask, cum, pos
        self.w, self.m8 = r.sb("w", [P, L + 8]), r.sb("m8", [P, 8])
        self.posb = r.sb("posb", [P, L], BF16)
        self.s_n, self.s_pos, self.s_posb, self.s_t, self.s_posT, self.stored, self.s_dve = (
            r.sem(n) for n in ("n", "pos", "posb", "t", "posT", "store", "dve"))

    def turn(self, pe):
        nc, c = self.nc, self.c
        for t in range(TPS):
            last = nc.tensor.transpose(self.psN[:, t * P:(t + 1) * P], c.QN[:, t, :], c.ident)
        last.then_inc(self.s_n, 1)
        pe.wait_ge(self.s_pos, 1)
        for t in range(TPS):
            last = nc.tensor.transpose(self.psP[:, t * P:(t + 1) * P], self.pos[:, t * P:(t + 1) * P], c.ident)
        last.then_inc(self.s_t, 1)

    def store(self, act, posd):
        act.wait_ge(self.s_pos, 1)
        self.nc.scalar.activation(self.posb[:, :], self.pos[:, :], ACT.Copy).then_inc(self.s_posb, 1)
        act.wait_ge(self.s_posb, 1)
        act.dma_start(posd, self.posb[:, :]).then_inc(self.stored, 16)

    def search(self, dve):
        nc, c, w, m8, s_dve = self.nc, self.c, self.w, self.m8, self.s_dve
        for i in range(8):
            last = nc.vector.memset(w[:, L + i:L + i + 1], -1.0 - i)
        last.then_inc(s_dve, 1)
        dve.wait_ge(self.s_n, 1)
        nc.vector.tensor_copy(w[:, 0:L], self.psN[:, :]).then_inc(s_dve, 1)
        for i in range(ROUNDS - 1):
            dve.wait_ge(s_dve, i * 2 + 2)
            nc.vector.max(m8[:, :], w[:, :]).then_inc(s_dve, 1)
            dve.wait_ge(s_dve, i * 2 + 3)
            nc.vector.match_replace(w[:, :], m8[:, :], w[:, :], self.REPLACED).then_inc(s_dve, 1)
        n = 2 * ROUNDS
        dve.wait_ge(s_dve, n)
        nc.vector.max(m8[:, :], w[:, :]).then_inc(s_dve, 1)
        dve.wait_ge(s_dve, n + 1)
        nc.vector.tensor_copy(m8[:, LAST:8], w[:, L:L + self.FILL]).then_inc(s_dve, 1)
        dve.wait_ge(s_dve, n + 2)
        nc.vector.match_replace(w[:, :], m8[:, :], w[:, :], self.REPLACED).then_inc(s_dve, 1)
        dve.wait_ge(s_dve, n + 3)
        nc.vector.tensor_scalar(self.mask[:, :], w[:, 0:L], self.REPLACED, None, ALU.is_equal).then_inc(s_dve, 1)
        dve.wait_ge(s_dve, n + 4)
        nc.vector.tensor_tensor_scan(self.cum[:, :], c.ones[:, 0:1].to_broadcast([P, L]), self.mask[:, :], 0.0,
                                     ALU.mult, ALU.add).then_inc(s_dve, 1)
        dve.wait_ge(s_dve, n + 5)
        nc.vector.tensor_tensor(self.pos[:, :], self.cum[:, :], self.mask[:, :], ALU.mult).then_inc(self.s_pos, 1)
        dve.wait_ge(self.s_t, 1)
        nc.vector.tensor_copy(c.posT[:, :, :].rearrange("p t n -> p (t n)"), self.psP[:, :]).then_inc(self.s_posT, 1)
        dve.wait_ge(self.s_posT, 1)


def attention(nc, c, kd, qd, posd):
    NH = 2 * H
    TURNS = B // 2
    LATER = 20
    WIDE = 32
    with ExitStack() as ctx:
        r = Room(nc, ctx, "a2_")
        q6 = r.sb("q6", [P, 2, TPS * H * KROWS], BF16)
        k6T = r.sb("k6T", [KROWS, 2, H, L], BF16)
        posrow = r.sb("posrow", [KTOP, 2, H * L], BF16)
        vcur = r.sb("vcur", [P, 2, L + WIDE - HD])
        pick = r.sb("pick", [P, 2, TPS, KTOP], BF16)
        place = r.sb("place", [KTOP, 2, H, L], BF16)
        qsel = r.sb("qsel", [KROWS, 2, KTOP], BF16)
        nmax = r.sb("nmax", [KTOP, 2])
        rsum = r.sb("rsum", [KTOP, 2, H])
        prob, probT = r.sb("prob", [KTOP, 3, L]), r.sb("probT", [P, 2, TPS * KTOP])
        oT = r.sb("oT", [P, 4 * KTOP])
        rinv, o, ores = r.sb("rinv", [KTOP, H]), r.sb("o", [KTOP, P]), r.sb("ores", [KTOP, P])
        o3 = r.sb("o3", [KTOP, H, 3, HD], BF16)
        others, omean = r.sb("others", [P, TPS, H]), r.sb("omean", [P, L])
        vmean = r.sb("vmean", [P, 2, P])
        ssum, attn, attnT, xb = (r.sb(n, [P, L]) for n in ("ssum", "attn", "attnT", "xb"))
        psG, psC = r.ps("psG", [P, L]), r.ps("psC", [P, L])
        psS, psE, psO = r.ps("psS", [P, 2, L]), r.ps("psE", [P, 2, L]), r.ps("psO", [P, 2, L])

        k_in, q_in, pos_in, v_in, vm_in = ([r.sig(f"{n}{u}", 16 * m) for u in range(2)] for n, m in
                                           (("kin", NPROD), ("qin", 1), ("pin", 1), ("vin", 1), ("vmin", 1)))
        picked, placed = r.sig("pick", NH), r.sig("place", NH // 4)
        g_done, qsel_ready, s_done, max_ready = r.sig("g", NH), r.sig("qsel", NH), r.sig("s", NH), r.sig("max", NH)
        prob_ready, e_done, probT_ready, o_done = r.sig("prob", NH), r.sig("e", NH), r.sig("probT", NH), r.sig("o", NH)
        oT_ready, ot_done = r.sig("oT", 2), r.sig("ot", 2)
        rinv_ready, o_ready, ohi, ores_ready, omid, olo = (
            r.sig(n, 2) for n in ("ri", "of", "ohi", "ores", "omid", "olo"))
        c_done, ssum_ready = r.sig("c", 2 * TPS), r.sig("ssum", 2 * TPS)
        others_ready, omean_ready, attn_ready = r.sig("oth", 2), r.sig("om", 2), r.sig("attn", 2)
        a_done, attnT_ready, w_done, xb_ready, x_ready = (r.sig(n, 2) for n in ("a", "attnT", "w", "xb", "x"))
        pad_set = r.sem("pad")
        top = TopQueries(nc, c, r, psS[:, 0, :], psS[:, 1, :], ssum, attn, attnT)
        block = ctx.enter_context(nc.Block())

        def placed_in(u, t):
            return psO[:, u, :] if t % 2 else psC[:, :]

        def lagging(stage, lag, it, h, prior, own):
            if h >= lag and own:
                stage(it, h - lag)
            elif h < lag and prior:
                stage(it - 1, NH + h - lag)

        def finishing(finish, it, h, prior, own):
            if prior and h + NH < H + LATER:
                finish(it - 1, 0, h + NH)
            if prior and h < LATER:
                finish(it - 1, 1, h + H)
            if own:
                finish(it, 0, h)

        @block.sync
        def _(sp):
            with sp.Fori(0, TURNS) as it:
                for u in range(2):
                    b = it * 2 + u
                    sp.wait_ge(s_done.sem, s_done.at(it, (u - 1) * H))
                    for n in range(NPROD):
                        sp.dma_start(k6T[n * HD:(n + 1) * HD, u, :, :],
                                     kd[ds(b, 1), :, KPART[n], :].rearrange("o (h d) t -> (o d) h t", h=H)
                                     ).then_inc(k_in[u].sem, 16)
                    sp.wait_ge(g_done.sem, g_done.at(it, (u - 1) * H))
                    sp.dma_start(q6[:, u, :], qd[ds(b, 1), :, :].rearrange("o p n -> (o p) n")
                                 ).then_inc(q_in[u].sem, 16)
                    sp.wait_ge(o_done.sem, o_done.at(it, (u - 1) * H))
                    sp.dma_start(vcur[:, u, 0:L], one(c.V[:, ds(b, 1), :])).then_inc(v_in[u].sem, 16)
                    sp.wait_ge(omean_ready.sem, omean_ready.at(it, u - 1))
                    sp.dma_start(vmean[:, u, :], one(c.VM[:, ds(b, 1), :])).then_inc(vm_in[u].sem, 16)
                    sp.wait_ge(top.stored, 16)
                    sp.wait_ge(placed.sem, placed.at(it, (u - 1) * H // 4))
                    sp.dma_start(posrow[:, u, :], posd[ds(b * H, H), :].rearrange("h t -> (h t)")
                                 .partition_broadcast(KTOP)).then_inc(pos_in[u].sem, 16)

        @block.tensor
        def _(pe):
            def gather(it, h):
                u, hh = divmod(h, H)
                if hh == 0:
                    pe.wait_ge(q_in[u].sem, q_in[u].at(it))
                pe.wait_ge(picked.sem, picked.at(it, h + 1))
                pe.wait_ge(qsel_ready.sem, qsel_ready.at(it, h))
                for t in range(TPS):
                    at = t * H * KROWS + hh * KROWS
                    last = nc.tensor.matmul(psG[0:KROWS, 0:KTOP], q6[:, u, at:at + KROWS], pick[:, h % 2, t, :],
                                            start=(t == 0), stop=(t == TPS - 1))
                last.then_inc(g_done.sem, 1)

            def scores(it, h):
                u, hh = divmod(h, H)
                if hh == 0:
                    pe.wait_ge(k_in[u].sem, k_in[u].at(it))
                pe.wait_ge(qsel_ready.sem, qsel_ready.at(it, h + 1))
                pe.wait_ge(prob_ready.sem, prob_ready.at(it, h - 1))
                nc.tensor.matmul(psS[0:KTOP, h % 2, :], qsel[:, h % 2, :], k6T[:, u, hh, :],
                                 start=True, stop=True).then_inc(s_done.sem, 1)

            def turn(it, h):
                pe.wait_ge(prob_ready.sem, prob_ready.at(it, h + 1))
                pe.wait_ge(probT_ready.sem, probT_ready.at(it, h - 1))
                for t in range(TPS):
                    last = nc.tensor.transpose(psE[:, h % 2, t * KTOP:(t + 1) * KTOP],
                                               prob[:, h % 3, t * P:(t + 1) * P], c.ident[0:KTOP, 0:KTOP])
                last.then_inc(e_done.sem, 1)

            def weigh(it, h):
                u, hh = divmod(h, H)
                if hh == 0:
                    pe.wait_ge(v_in[u].sem, v_in[u].at(it))
                    pe.wait_ge(oT_ready.sem, oT_ready.at(it, u - 1))
                    pe.wait_ge(ssum_ready.sem, ssum_ready.at(it, (u - 1) * TPS))
                pe.wait_ge(probT_ready.sem, probT_ready.at(it, h + 1))
                for t in range(TPS):
                    at = t * P + hh * HD
                    last = nc.tensor.matmul(
                        psO[hh % 4 * WIDE:(hh % 4 + 1) * WIDE, u, hh // 4 * KTOP:(hh // 4 + 1) * KTOP],
                        vcur[:, u, at:at + WIDE], probT[:, h % 2, t * KTOP:(t + 1) * KTOP],
                        start=(t == 0), stop=(t == TPS - 1))
                last.then_inc(o_done.sem, 1)

            def turn_slots(it, u):
                pe.wait_ge(oT_ready.sem, oT_ready.at(it, u + 1))
                pe.wait_ge(x_ready.sem, x_ready.at(it, u))
                for t in range(4):
                    last = nc.tensor.transpose(psC[0:KTOP, t * P:(t + 1) * P], oT[:, t * KTOP:(t + 1) * KTOP], c.ident)
                last.then_inc(ot_done.sem, 1)

            def put_back(it, u, t):
                if t == 0:
                    pe.wait_ge(olo.sem, olo.at(it, u + 1))
                    pe.wait_ge(o_ready.sem, o_ready.at(it, u + 1))
                pe.wait_ge(ssum_ready.sem, ssum_ready.at(it, u * TPS + t - 1))
                for h in range(H):
                    last = nc.tensor.matmul(placed_in(u, t)[:, h * 3 * HD:(h + 1) * 3 * HD],
                                            place[:, u, h, t * P:(t + 1) * P],
                                            o3[:, h, :, :].rearrange("p s d -> p (s d)"), start=True, stop=True)
                last.then_inc(c_done.sem, 1)

            def turn_outputs(it, u):
                pe.wait_ge(attn_ready.sem, attn_ready.at(it, u + 1))
                for t in range(TPS):
                    last = nc.tensor.transpose(psC[:, t * P:(t + 1) * P], attn[:, t * P:(t + 1) * P], c.ident)
                last.then_inc(a_done.sem, 1)

            def project(it, u):
                pe.wait_ge(attnT_ready.sem, attnT_ready.at(it, u + 1))
                for t in range(TPS):
                    last = nc.tensor.matmul(psC[:, t * P:(t + 1) * P], attnT[:, t * P:(t + 1) * P], c.W[:, 3, :],
                                            start=True, stop=True)
                last.then_inc(w_done.sem, 1)

            def finish(it, u, n):
                if n == H + 6:
                    turn_slots(it, u)
                if H + 12 <= n < H + 12 + TPS:
                    put_back(it, u, n - H - 12)
                if n == H + 17:
                    turn_outputs(it, u)
                if n == H + 18:
                    project(it, u)

            def step(it, h, prior, own=True):
                if own:
                    gather(it, h)
                lagging(scores, 1, it, h, prior, own)
                lagging(turn, 3, it, h, prior, own)
                lagging(weigh, 4, it, h, prior, own)
                finishing(finish, it, h, prior, own)

            top.turn(pe)
            warm_up(nc, c, psO[:, 0, :])
            pe.wait_ge(pad_set, 1)
            for h in range(NH):
                step(0, h, False)
            with pe.Fori(1, TURNS) as it:
                for h in range(NH):
                    step(it, h, True)
            for h in range(LATER):
                step(TURNS, h, True, own=False)

        @block.scalar
        def _(act):
            def queries(it, h):
                act.wait_ge(g_done.sem, g_done.at(it, h + 1))
                act.wait_ge(s_done.sem, s_done.at(it, h - 1))
                nc.scalar.activation(qsel[:, h % 2, :], psG[0:KROWS, 0:KTOP], ACT.Copy).then_inc(qsel_ready.sem, 1)

            def exponents(it, h):
                u, hh = divmod(h, H)
                act.wait_ge(max_ready.sem, max_ready.at(it, h + 1))
                act.wait_ge(e_done.sem, e_done.at(it, h - 2 if h > 1 else h - 1))
                if hh == 0:
                    act.wait_ge(rinv_ready.sem, rinv_ready.at(it, u - 1))
                nc.scalar.activation(prob[:, h % 3, :], psS[0:KTOP, h % 2, :], ACT.Exp, bias=nmax[:, h % 2:h % 2 + 1],
                                     accum_out=rsum[:, u, hh:hh + 1]).then_inc(prob_ready.sem, 1)

            def turned(it, h):
                act.wait_ge(e_done.sem, e_done.at(it, h + 1))
                act.wait_ge(o_done.sem, o_done.at(it, h - 1))
                nc.scalar.activation(probT[:, h % 2, :], psE[:, h % 2, 0:TPS * KTOP], ACT.Copy
                                     ).then_inc(probT_ready.sem, 1)

            def outputs_out(it, u):
                act.wait_ge(o_done.sem, o_done.at(it, (u + 1) * H))
                act.wait_ge(ot_done.sem, ot_done.at(it, u))
                nc.scalar.activation(oT[:, :], psO[:, u, 0:4 * KTOP], ACT.Copy).then_inc(oT_ready.sem, 1)

            def output_high(it, u):
                act.wait_ge(o_ready.sem, o_ready.at(it, u + 1))
                act.wait_ge(c_done.sem, c_done.at(it, u * TPS))
                nc.scalar.activation(o3[:, :, 0, :], o[:, :].rearrange("p (h d) -> p h d", d=HD),
                                     ACT.Copy).then_inc(ohi.sem, 1)

            def output_middle(it, u):
                act.wait_ge(ores_ready.sem, ores_ready.at(it, u + 1))
                nc.scalar.activation(o3[:, :, 1, :], ores[:, :].rearrange("p (h d) -> p h d", d=HD),
                                     ACT.Copy).then_inc(omid.sem, 1)

            def outputs_turned(it, u):
                act.wait_ge(a_done.sem, a_done.at(it, u + 1))
                act.wait_ge(w_done.sem, w_done.at(it, u))
                nc.scalar.activation(attnT[:, :], psC[:, :], ACT.Copy).then_inc(attnT_ready.sem, 1)

            def finish(it, u, n):
                for slot, step in ((4, outputs_out), (8, output_high), (10, output_middle), (17, outputs_turned)):
                    if n == H + slot:
                        step(it, u)

            def step(it, h, prior, own=True):
                if own:
                    queries(it, h)
                lagging(exponents, 1, it, h, prior, own)
                lagging(turned, 3, it, h, prior, own)
                finishing(finish, it, h, prior, own)

            top.store(act, posd)
            for h in range(NH):
                step(0, h, False)
            with act.Fori(1, TURNS) as it:
                for h in range(NH):
                    step(it, h, True)
            for h in range(LATER):
                step(TURNS, h, True, own=False)

        @block.gpsimd
        def _(pool):
            nc.gpsimd.memset(vcur[:, :, L:], 0.0).then_inc(pad_set, 1)
            r.seed(pool)
            with pool.Fori(0, TURNS) as it:
                for u in range(2):
                    b = it * 2 + u
                    pool.wait_ge(x_ready.sem, x_ready.at(it, u))
                    nc.gpsimd.tensor_tensor(xb[:, :].rearrange("p (t c) -> p t c", c=P), c.X[:, ds(b * TPS, TPS), :],
                                            c.rows[:, 2, :].unsqueeze(1).to_broadcast([P, TPS, P]),
                                            ALU.add).then_inc(xb_ready.sem, 1)
                    pool.wait_ge(others_ready.sem, others_ready.at(it, u + 1))
                    pool.wait_ge(vm_in[u].sem, vm_in[u].at(it))
                    pool.wait_ge(attn_ready.sem, attn_ready.at(it, u))
                    nc.gpsimd.tensor_tensor(
                        omean[:, :].rearrange("p (t h d) -> p t h d", h=H, d=HD),
                        others[:, :, :].unsqueeze(3).to_broadcast([P, TPS, H, HD]),
                        vmean[:, u, :].rearrange("p (h d) -> p h d", d=HD).unsqueeze(1).to_broadcast([P, TPS, H, HD]),
                        ALU.mult).then_inc(omean_ready.sem, 1)

        @block.vector
        def _(dve):
            def one_hots(it, h):
                u, hh = divmod(h, H)
                dve.wait_ge(g_done.sem, g_done.at(it, h - 1))
                for t in range(TPS):
                    last = nc.vector.tensor_scalar(pick[:, h % 2, t, :], c.iota1[:, 0:KTOP],
                                                   c.posT[:, t, ds(it * NH + h, 1)], None, ALU.is_equal)
                last.then_inc(picked.sem, 1)
                if hh == 3:
                    dve.wait_ge(pos_in[u].sem, pos_in[u].at(it))
                    dve.wait_ge(c_done.sem, c_done.at(it, (u - 1) * TPS))
                if hh % 4 == 3:
                    nc.vector.tensor_scalar(place[:, u, hh - 3:hh + 1, :].rearrange("p h t -> p (h t)"),
                                            posrow[:, u, (hh - 3) * L:(hh + 1) * L], c.slot1[0:KTOP, :], None,
                                            ALU.is_equal).then_inc(placed.sem, 1)

            def maximum(it, h):
                dve.wait_ge(s_done.sem, s_done.at(it, h + 1))
                dve.wait_ge(prob_ready.sem, prob_ready.at(it, h - 1))
                nc.vector.tensor_reduce(nmax[:, h % 2:h % 2 + 1], psS[0:KTOP, h % 2, :], AX.X, ALU.max,
                                        negate=True).then_inc(max_ready.sem, 1)

            def divide(it, u):
                dve.wait_ge(prob_ready.sem, prob_ready.at(it, (u + 1) * H))
                nc.vector.reciprocal(rinv[:, :], rsum[:, u, :]).then_inc(rinv_ready.sem, 1)
                dve.wait_ge(omean_ready.sem, omean_ready.at(it, u))
                nc.vector.tensor_scalar(others[:, :, :], c.posT[:, :, ds((it * 2 + u) * H, H)], 0.0, None,
                                        ALU.is_equal).then_inc(others_ready.sem, 1)
                dve.wait_ge(rinv_ready.sem, rinv_ready.at(it, u + 1))
                dve.wait_ge(ot_done.sem, ot_done.at(it, u + 1))
                nc.vector.tensor_tensor(o[:, :].rearrange("p (h d) -> p h d", d=HD),
                                        psC[0:KTOP, :].rearrange("p (h d) -> p h d", d=WIDE)[:, :, 0:HD],
                                        rinv[:, :].unsqueeze(2).to_broadcast([KTOP, H, HD]), ALU.mult
                                        ).then_inc(o_ready.sem, 1)

            def output_rest(it, u):
                dve.wait_ge(ohi.sem, ohi.at(it, u + 1))
                nc.vector.tensor_tensor(ores[:, :].rearrange("p (h d) -> p h d", d=HD),
                                        o[:, :].rearrange("p (h d) -> p h d", d=HD), o3[:, :, 0, :],
                                        ALU.subtract).then_inc(ores_ready.sem, 1)

            def output_low(it, u):
                dve.wait_ge(omid.sem, omid.at(it, u + 1))
                nc.vector.tensor_tensor(o3[:, :, 2, :], ores[:, :].rearrange("p (h d) -> p h d", d=HD), o3[:, :, 1, :],
                                        ALU.subtract).then_inc(olo.sem, 1)

            def sum_parts(it, u, t):
                dve.wait_ge(c_done.sem, c_done.at(it, u * TPS + t + 1))
                nc.vector.tensor_reduce(ssum[:, t * P:(t + 1) * P].rearrange("p (h d) -> p h d", d=HD),
                                        placed_in(u, t)[:, 0:H * 3 * HD].rearrange("p (h s d) -> p h d s", s=3, d=HD),
                                        AX.X, ALU.add).then_inc(ssum_ready.sem, 1)

            def add_means(it, u):
                dve.wait_ge(ssum_ready.sem, ssum_ready.at(it, (u + 1) * TPS))
                dve.wait_ge(omean_ready.sem, omean_ready.at(it, u + 1))
                dve.wait_ge(a_done.sem, a_done.at(it, u))
                nc.vector.tensor_tensor(attn[:, :], ssum[:, :], omean[:, :], ALU.add).then_inc(attn_ready.sem, 1)

            def residual(it, u):
                b = it * 2 + u
                dve.wait_ge(w_done.sem, w_done.at(it, u + 1))
                dve.wait_ge(xb_ready.sem, xb_ready.at(it, u + 1))
                nc.vector.tensor_tensor(c.X[:, ds(b * TPS, TPS), :], psC[:, :].rearrange("p (t c) -> p t c", c=P),
                                        xb[:, :].rearrange("p (t c) -> p t c", c=P), ALU.add).then_inc(x_ready.sem, 1)

            def finish(it, u, n):
                for slot, step in ((7, divide), (9, output_rest), (11, output_low), (19, residual)):
                    if n == H + slot:
                        step(it, u)
                if H + 13 <= n < H + 13 + TPS:
                    sum_parts(it, u, n - H - 13)
                if n == H + 12 + TPS:
                    add_means(it, u)

            def step(it, h, prior, own=True):
                if own and h == 0:
                    one_hots(it, 0)
                if own and h + 1 < NH:
                    one_hots(it, h + 1)
                lagging(maximum, 1, it, h, prior, own)
                finishing(finish, it, h, prior, own)

            top.search(dve)
            for h in range(NH):
                step(0, h, False)
            with dve.Fori(1, TURNS) as it:
                for h in range(NH):
                    step(it, h, True)
            for h in range(LATER):
                step(TURNS, h, True, own=False)
            dve.wait_ge(x_ready.sem, x_ready.at(TURNS - 1))




def experts(nc, c, a, xnd, yd):
    R32 = 32
    BANKG = 4
    WARM_AT = ((2, 0), (3, 4))
    PARTS = 4
    with ExitStack() as ctx:
        r = Room(nc, ctx, "e_")
        stats, mv = r.sb("stats", [P, NT, 6]), r.sb("mv", [P, NT, 2])
        std, rstd = r.sb("std", [P, NT]), r.sb("rstd", [P, NT])
        xn, xnT = r.sb("xn", [P, TPU, P]), r.sb("xnT", [P, STOK])
        xbd = r.sb("xbd", [P, NG, P])
        m8, i8 = r.sb("m8", [P, 8]), r.sb("i8", [P, 8], U32)
        vals, dif = r.sb("vals", [P, 4]), r.sb("dif", [P, 3])
        spread = r.sb("spread", [P, NG, 4])
        chosen = r.sb("chosen", [P, NS + 2, NG * 4])
        idx = r.sb("idx", [P, PARTS, NG * TOPK], U32)
        wts = r.sb("wts", [P, PARTS, NG * TOPK])
        tab = r.sb("tab", [P, NG, TOPK, P])
        tbd = r.sb("tbd", [P, 2, 16, P])
        hbd = r.sb("hbd", [P, 2, 16, P])
        halves, fold = r.sb("halves", [P, P]), r.sb("fold", [P, NEXP])
        hpre = r.sb("hpre", [P, 2, 16, R32])
        hid = r.sb("hid", [P, 2, NG, P])
        yT = r.sb("yT", [P, 2, P])
        y, ytok = r.sb("y", [P, NG, R32]), r.sb("ytok", [P, TPU, P])
        psT = r.ps("psT", [P, 2, 512])
        psL, psY = r.ps("psL", [P, 512]), r.ps("psY", [P, 512])
        ps1, ps2 = r.ps("ps1", [P, 2, 512]), r.ps("ps2", [P, 2, 512])

        xn_ready, xn_stored = r.sig("xn"), r.sig("xst", 16)
        t_done, xnT_ready = r.sig("t", 2), r.sig("xT", 2)
        s_stats, s_var, s_std, s_rstd, zeroed, folded = (
            r.sem(n) for n in ("stats", "var", "std", "rstd", "zero", "fold"))
        logits, m8_ready, i8_ready, dif_ready, exp_ready, den_ready, inv_ready, vals_ready, spread_ready, spread_done, \
            psL_read = (r.sig(n) for n in ("lg", "m8", "i8", "dif", "exp", "den", "inv", "vals", "spr", "sd", "lr"))
        xbd_loaded = r.sig("xld", 2 * 64)
        halves_done, halves_ready = r.sig("hfd", 2), r.sig("hfr", 2)
        idx_up, wts_up, idx_down = r.sig("iu", 2), r.sig("wu", 2), r.sig("id", 2)
        gathered = [r.sig(f"g{q}", PARTS * BANKG * TOPK * 16, given=False) for q in range(NQ)]
        weighted = r.sig("wgt", PARTS * NQ)
        first_done, tbd_act, tbd_dve, second_done = (r.sig(n, PARTS * NQ) for n in ("f", "ta", "td", "s"))
        hpre_ready, hid_ready, ht_done, hbd_act, hbd_dve, yT_ready, yt_done = (
            r.sig(n, 2 * NQ) for n in ("hp", "h", "ht", "ha", "hd", "yT", "yt"))
        y_ready, y_stored, y_loaded, x_ready = r.sig("y", 4), r.sig("yst", 32), r.sig("yld", 32), r.sig("x", 2)
        block = ctx.enter_context(nc.Block())

        def alone(eng):
            eng.sem_inc(c.passed, 1)

        def layout(flat, s):
            return flat[ds(s * (STOK * P), STOK * P)].rearrange("(g p j) -> p g j", p=P, j=R32)

        def tokens(flat, s):
            return flat[ds(s * (STOK * P), STOK * P)].rearrange("(t p c) -> p t c", p=P, c=P)

        @block.sync
        def _(sp):
            with sp.Fori(0, NS) as s:
                sp.wait_ge(xn_ready.sem, xn_ready.at(s))
                alone(sp)
                sp.dma_start(tokens(xnd, s), xn[:, :, :]).then_inc(xn_stored.sem, 16)
            sp.wait_ge(xn_stored.sem, xn_stored.at(NS - 1))
            sp.wait_ge(zeroed, 1)
            with sp.Fori(0, NS // 2) as j:
                for v in range(2):
                    sp.wait_ge(first_done.sem, first_done.at(j, v * NQ if v else 2 * NQ - PARTS * NQ))
                    alone(sp)
                    for g in range(4):
                        sp.dma_start(xbd[R32 * g:R32 * g + R32, :, R32 * g:R32 * g + R32],
                                     layout(xnd, 2 * j + v)[R32 * g:R32 * g + R32, :, :]).then_inc(xbd_loaded.sem, 16)
                for v in range(2):
                    sp.wait_ge(y_ready.sem, y_ready.at(j, 2 * v + 2))
                    alone(sp)
                    sp.dma_start(layout(yd, 2 * j + v), y[:, :, :]).then_inc(y_stored.sem, 16)
                    sp.wait_ge(y_stored.sem, y_stored.at(j, 16 * (v + 1)))
                    alone(sp)
                    sp.wait_ge(x_ready.sem, x_ready.at(j, v))
                    alone(sp)
                    sp.dma_start(ytok[:, :, :], tokens(yd, 2 * j + v)).then_inc(y_loaded.sem, 16)
            sp.wait_ge(y_stored.sem, y_stored.at(NS // 2 - 1))

        @block.gpsimd
        def _(pool):
            r.seed(pool)
            nc.gpsimd.memset(chosen[:, NS:, :], 0.0)
            for buf in (xbd, tbd, hbd):
                last = nc.gpsimd.memset(buf[:, :, :] if buf is xbd else buf[:, :, :, :], 0.0)
            last.then_inc(zeroed, 1)
            with pool.Fori(0, NS // 2) as j:
                for p in range(PARTS):
                    table = a["tab_up"] if p < 2 else a["tab_down"]
                    for q in range(NQ):
                        if q == 0 and p < 2:
                            pool.wait_ge(idx_up.sem, idx_up.at(j, p + 1))
                            alone(pool)
                        if q == 0 and p >= 2:
                            pool.wait_ge(idx_down.sem, idx_down.at(j, p - 1))
                            alone(pool)
                        pool.wait_ge(second_done.sem, second_done.at(j, (p - 1) * NQ + q + 1))
                        alone(pool)
                        for n in range(q * BANKG * TOPK, (q + 1) * BANKG * TOPK):
                            nc.gpsimd.indirect_dma_start(
                                tab[:, n // TOPK, n % TOPK, :], None, table,
                                bass.IndirectOffsetOnAxis(ap=idx[:, p, n:n + 1], axis=0)
                            ).then_inc(gathered[q].sem, 16)

        @block.tensor
        def _(pe):
            def spread_out(n):
                pe.wait_ge(spread_ready.sem, spread_ready.at(n))
                nc.tensor.matmul(psL[:, 0:NG * 4], c.sel4, spread[:, :, :].rearrange("p a b -> p (a b)"),
                                 start=True, stop=True).then_inc(spread_done.sem, 1)

            def choose_up(s):
                pe.wait_ge(xn_ready.sem, xn_ready.at(s))
                pe.wait_ge(xnT_ready.sem, xnT_ready.before(s))
                for i in range(2):
                    for t in range(4):
                        last = nc.tensor.transpose(psT[:, i, t * P:(t + 1) * P], xn[:, i * 4 + t, :], c.ident)
                    last.then_inc(t_done.sem, 1)
                pe.wait_ge(xnT_ready.sem, xnT_ready.at(s))
                pe.wait_ge(psL_read.sem, psL_read.before(s))
                for t in range(ROWTOK):
                    last = nc.tensor.matmul(psL[:, 0:NEXP], xnT[:, :].rearrange("p (n t) -> p t n", t=ROWTOK)[:, t, :],
                                            c.WupR[:, t * NEXP:(t + 1) * NEXP], start=(t == 0), stop=(t == ROWTOK - 1))
                last.then_inc(logits.sem, 1)
                spread_out(s)

            def choose_down(j, v):
                n = 2 * j + (NS + v)
                pe.wait_ge(hid_ready.sem, hid_ready.at(j, (v + 1) * NQ))
                pe.wait_ge(psL_read.sem, psL_read.before(n))
                byrow = hid[:, v, :, :].rearrange("p n (g o) -> p o (n g)", o=R32)
                for o in range(R32):
                    at = o % 2 * NEXP
                    last = nc.tensor.matmul(psL[at:at + NEXP, P:2 * P], c.WdR[:, o * NEXP:(o + 1) * NEXP],
                                            byrow[:, o, :], start=(o < 2), stop=(o >= R32 - 2),
                                            skip_group_check=True)
                last.then_inc(halves_done.sem, 1)
                pe.wait_ge(halves_ready.sem, halves_ready.at(j, v + 1))
                nc.tensor.matmul(psL[:, 0:NEXP], halves[:, :], fold[:, :], start=True, stop=True
                                 ).then_inc(logits.sem, 1)
                spread_out(n)

            def first(j, p, q):
                u = p * NQ + q
                pe.wait_ge(weighted.sem, weighted.at(j, u + 1))
                pe.wait_ge(tbd_act.sem, tbd_act.at(j, u - 1))
                pe.wait_ge(tbd_dve.sem, tbd_dve.at(j, u - 1))
                if p < 2 and q == 0:
                    pe.wait_ge(xbd_loaded.sem, xbd_loaded.at(j, 64 * (p + 1)))
                if p >= 2:
                    pe.wait_ge(hbd_act.sem, hbd_act.at(j, (p - 2) * NQ + q + 1))
                    pe.wait_ge(hbd_dve.sem, hbd_dve.at(j, (p - 2) * NQ + q + 1))
                if (p, q) in WARM_AT:
                    warm_up(nc, c, ps1[:, u % 2, :])
                for i in range(BANKG):
                    n = q * BANKG + i
                    if p < 2:
                        last = nc.tensor.matmul(ps1[:, u % 2, i * P:(i + 1) * P], xbd[:, n, :],
                                                tab[:, n, :, 0:64], start=True, stop=True)
                    else:
                        for jh in range(2):
                            for ih in range(2):
                                last = nc.tensor.matmul(
                                    ps1[:, u % 2, i * P + jh * 64:i * P + jh * 64 + 64],
                                    hbd[:, q % 2, i * 4 + ih * 2 + jh, :],
                                    tab[:, n, :, ih * R32:(ih + 1) * R32], start=(ih == 0), stop=(ih == 1))
                last.then_inc(first_done.sem, 1)

            def second(j, p, q):
                u = p * NQ + q
                pe.wait_ge(tbd_act.sem, tbd_act.at(j, u + 1))
                pe.wait_ge(tbd_dve.sem, tbd_dve.at(j, u + 1))
                if p < 2:
                    pe.wait_ge(hpre_ready.sem, hpre_ready.at(j, u - 1))
                    if u < 2:
                        pe.wait_ge(yT_ready.sem, yT_ready.before(j))
                else:
                    pe.wait_ge(yT_ready.sem, yT_ready.at(j, u - 2 * NQ - 1))
                    if u < 2 * NQ + 2:
                        pe.wait_ge(hpre_ready.sem, hpre_ready.at(j))
                if p < 2:
                    for i in range(BANKG):
                        for k in range(TOPK):
                            for h in range(2):
                                last = nc.tensor.matmul(
                                    ps2[64 * h:64 * h + 64, q % 2, i * P:(i + 1) * P],
                                    tab[:, q * BANKG + i, k, 64:P], tbd[:, u % 2, i * 4 + k * 2 + h, :],
                                    start=(k == 0), stop=(k == TOPK - 1), skip_group_check=True)
                else:
                    for m in range(4):
                        jh, k = divmod(m, 2)
                        for i in range(BANKG):
                            last = nc.tensor.matmul(
                                ps2[R32 * i:R32 * i + R32, q % 2, 0:P],
                                tab[:, q * BANKG + i, k, 64 + jh * R32:64 + (jh + 1) * R32],
                                tbd[:, u % 2, i * 4 + jh * 2 + k, :], start=(m == 0), stop=(m == 3),
                                skip_group_check=True)
                last.then_inc(second_done.sem, 1)

            def turn_hidden(j, e):
                v, q = divmod(e, NQ)
                pe.wait_ge(hbd_act.sem, hbd_act.at(j, e - 1))
                pe.wait_ge(hbd_dve.sem, hbd_dve.at(j, e - 1))
                for i in range(BANKG):
                    last = nc.tensor.transpose(psT[:, e % 2, i * P:(i + 1) * P], hid[:, v, q * BANKG + i, :], c.ident)
                last.then_inc(ht_done.sem, 1)

            def turn_outputs(j, e):
                pe.wait_ge(yT_ready.sem, yT_ready.at(j, e + 1))
                if e % 4 == 0:
                    pe.wait_ge(y_ready.sem, y_ready.at(j, e // 4))
                nc.tensor.transpose(psY[:, e % 4 * P:(e % 4 + 1) * P], yT[:, e % 2, :], c.ident
                                    ).then_inc(yt_done.sem, 1)

            choose_up(0)
            with pe.Fori(1, NS) as s:
                choose_up(s)
            pe.wait_ge(zeroed, 1)
            pe.wait_ge(folded, 1)
            warm_up(nc, c, ps1[:, 0, :])
            with pe.Fori(0, NS // 2) as j:
                for v in range(2):
                    for q in range(NQ + 1):
                        if q < NQ:
                            first(j, v, q)
                        if q >= 1:
                            second(j, v, q - 1)
                    choose_down(j, v)
                turn_hidden(j, 0)
                for e in range(2 * NQ + 2):
                    if e + 1 < 2 * NQ:
                        turn_hidden(j, e + 1)
                    if e < 2 * NQ:
                        first(j, 2 + e // NQ, e % NQ)
                    if 1 <= e < 2 * NQ + 1:
                        second(j, 2 + (e - 1) // NQ, (e - 1) % NQ)
                    if e >= 2:
                        turn_outputs(j, e - 2)

        def diagonal(copy, dst, src, g):
            return copy(dst[R32 * g:R32 * g + R32, :, R32 * g:R32 * g + R32],
                        src[R32 * g:R32 * g + R32, :].rearrange("p (a b) -> p a b", b=R32))

        @block.scalar
        def _(act):
            def copy(dst, src):
                return nc.scalar.activation(dst, src, ACT.Copy)

            def exponent(n):
                act.wait_ge(dif_ready.sem, dif_ready.at(n))
                act.wait_ge(vals_ready.sem, vals_ready.before(n))
                nc.scalar.activation(dif[:, 1:2], dif[:, 0:1], ACT.Exp).then_inc(exp_ready.sem, 1)

            def choose_up(s):
                act.wait_ge(logits.sem, logits.before(s))
                for i in range(2):
                    act.wait_ge(t_done.sem, t_done.at(s, i + 1))
                    nc.scalar.activation(xnT[:, i * 512:(i + 1) * 512], psT[:, i, :], ACT.Copy
                                         ).then_inc(xnT_ready.sem, 1)
                exponent(s)

            def first_to_diagonal(j, p, q):
                u = p * NQ + q
                act.wait_ge(first_done.sem, first_done.at(j, u + 1))
                act.wait_ge(second_done.sem, second_done.at(j, u - 1))
                for g in (0, 1):
                    last = diagonal(copy, tbd[:, u % 2, :, :], ps1[:, u % 2, :], g)
                last.then_inc(tbd_act.sem, 1)

            def hidden_to_diagonal(j, e):
                act.wait_ge(first_done.sem, first_done.at(j, 2 * NQ + e - 1))
                act.wait_ge(ht_done.sem, ht_done.at(j, e + 1))
                for g in (0, 1):
                    last = diagonal(copy, hbd[:, e % 2, :, :], psT[:, e % 2, :], g)
                last.then_inc(hbd_act.sem, 1)

            def root(part, tiles):
                act.wait_ge(s_var, part)
                nc.scalar.activation(std[:, tiles], mv[:, tiles, 1], ACT.Sqrt, bias=c.eps[:, :], scale=1.0
                                     ).then_inc(s_std, 1)

            root(1, slice(0, TPU))
            choose_up(0)
            root(2, slice(TPU, NT))
            with act.Fori(1, NS) as s:
                choose_up(s)
            act.wait_ge(zeroed, 1)
            with act.Fori(0, NS // 2) as j:
                for v in range(2):
                    for q in range(NQ + 1):
                        if q < NQ:
                            first_to_diagonal(j, v, q)
                        if q >= 1:
                            e = v * NQ + q - 1
                            act.wait_ge(hpre_ready.sem, hpre_ready.at(j, e + 1))
                            act.wait_ge(ht_done.sem, ht_done.before(j, e + 1))
                            nc.scalar.activation(hid[:, v, (q - 1) * BANKG:q * BANKG, :].rearrange("p a b -> p (a b)"),
                                                 hpre[:, (q - 1) % 2, :, :].rearrange("p a b -> p (a b)"),
                                                 ACT.Gelu).then_inc(hid_ready.sem, 1)
                    act.wait_ge(halves_done.sem, halves_done.at(j, v + 1))
                    act.wait_ge(logits.sem, logits.at(2 * j + (NS + v - 1)))
                    nc.scalar.activation(halves[:, :], psL[:, P:2 * P], ACT.Copy).then_inc(halves_ready.sem, 1)
                    exponent(2 * j + (NS + v))
                hidden_to_diagonal(j, 0)
                for e in range(2 * NQ + 1):
                    if e + 1 < 2 * NQ:
                        hidden_to_diagonal(j, e + 1)
                    if e < 2 * NQ:
                        first_to_diagonal(j, 2 + e // NQ, e % NQ)
                    if e >= 1:
                        act.wait_ge(second_done.sem, second_done.at(j, 2 * NQ + e))
                        act.wait_ge(yt_done.sem, yt_done.at(j, e - 2))
                        nc.scalar.activation(yT[:, (e - 1) % 2, :], ps2[:, (e - 1) % 2, 0:P], ACT.Copy
                                             ).then_inc(yT_ready.sem, 1)

        @block.vector
        def _(dve):
            def route(n):
                dve.wait_ge(logits.sem, logits.at(n))
                dve.wait_ge(vals_ready.sem, vals_ready.before(n))
                alone(dve)
                nc.vector.max(m8[:, :], psL[:, 0:NEXP]).then_inc(m8_ready.sem, 1)
                dve.wait_ge(m8_ready.sem, m8_ready.at(n))
                nc.vector.tensor_tensor(dif[:, 0:1], m8[:, 1:2], m8[:, 0:1], ALU.subtract).then_inc(dif_ready.sem, 1)
                nc.vector.max_index(i8[:, :], m8[:, :], psL[:, 0:NEXP]).then_inc(i8_ready.sem, 1)
                dve.wait_ge(exp_ready.sem, exp_ready.at(n))
                nc.vector.tensor_scalar(dif[:, 2:3], dif[:, 1:2], 1.0, None, ALU.add).then_inc(den_ready.sem, 1)
                dve.wait_ge(den_ready.sem, den_ready.at(n))
                dve.wait_ge(spread_ready.sem, spread_ready.before(n))
                nc.vector.reciprocal(vals[:, 2:3], dif[:, 2:3]).then_inc(inv_ready.sem, 1)
                dve.wait_ge(i8_ready.sem, i8_ready.at(n))
                nc.vector.tensor_copy(vals[:, 0:2], i8[:, 0:2])
                dve.wait_ge(inv_ready.sem, inv_ready.at(n))
                nc.vector.tensor_tensor(vals[:, 3:4], dif[:, 1:2], vals[:, 2:3], ALU.mult).then_inc(vals_ready.sem, 1)
                dve.wait_ge(vals_ready.sem, vals_ready.at(n))
                dve.wait_ge(spread_done.sem, spread_done.before(n))
                nc.vector.tensor_tensor(spread[:, :, :], c.grp.unsqueeze(2).to_broadcast([P, NG, 4]),
                                        vals[:, :].unsqueeze(1).to_broadcast([P, NG, 4]), ALU.mult
                                        ).then_inc(spread_ready.sem, 1)
                dve.wait_ge(spread_done.sem, spread_done.at(n))

            def settle(p, source, idx_done, wts_done):
                both = source.rearrange("p (n v) -> p n v", v=4)
                nc.vector.tensor_scalar(idx[:, p, :].rearrange("p (n k) -> p n k", k=TOPK), both[:, :, 0:2], float(R32),
                                        c.row32, ALU.mult, ALU.add).then_inc(idx_done.sem, 1)
                nc.vector.tensor_copy(wts[:, p, :].rearrange("p (n k) -> p n k", k=TOPK), both[:, :, 2:4]
                                      ).then_inc(wts_done.sem, 1)

            def choose_up(s):
                dve.wait_ge(xn_stored.sem, xn_stored.before(s))
                dve.wait_ge(t_done.sem, t_done.before(s))
                for t in range(TPU):
                    j = s * TPU + t
                    last = nc.vector.tensor_scalar(xn[:, t, :], one(c.X[:, ds(j, 1), :]), one(mv[:, ds(j, 1), 0:1]),
                                                   rstd[:, ds(j, 1)], ALU.subtract, ALU.mult)
                last.then_inc(xn_ready.sem, 1)
                route(s)
                alone(dve)
                nc.vector.tensor_copy(one(chosen[:, ds(s, 1), :]), psL[:, 0:NG * 4]).then_inc(psL_read.sem, 1)

            def weigh(j, p, q):
                if q == 0 and p < 2:
                    dve.wait_ge(wts_up.sem, wts_up.at(j, p + 1))
                if q == 0 and p >= 2:
                    dve.wait_ge(psL_read.sem, psL_read.at(2 * j + (NS + p - 2)))
                dve.wait_ge(gathered[q].sem, gathered[q].at(j, (p + 1) * BANKG * TOPK * 16))
                part = tab[:, q * BANKG:(q + 1) * BANKG, :, 0:64].rearrange("p n k o -> p (n k) o")
                wt = wts[:, p, q * BANKG * TOPK:(q + 1) * BANKG * TOPK].unsqueeze(2).to_broadcast([P, BANKG * TOPK, 64])
                nc.vector.tensor_tensor(part, part, wt, ALU.mult).then_inc(weighted.sem, 1)

            def first_to_diagonal(j, p, q):
                u = p * NQ + q
                dve.wait_ge(first_done.sem, first_done.at(j, u + 1))
                dve.wait_ge(second_done.sem, second_done.at(j, u - 1))
                for g in (2, 3):
                    last = diagonal(nc.vector.tensor_copy, tbd[:, u % 2, :, :], ps1[:, u % 2, :], g)
                last.then_inc(tbd_dve.sem, 1)

            def hidden_to_diagonal(j, e):
                dve.wait_ge(first_done.sem, first_done.at(j, 2 * NQ + e - 1))
                dve.wait_ge(ht_done.sem, ht_done.at(j, e + 1))
                for g in (2, 3):
                    last = diagonal(nc.vector.tensor_copy, hbd[:, e % 2, :, :], psT[:, e % 2, :], g)
                last.then_inc(hbd_dve.sem, 1)

            def add(j, v):
                dve.wait_ge(y_loaded.sem, y_loaded.at(j, 16 * (v + 1)))
                tiles = ds((2 * j + v) * TPU, TPU)
                nc.vector.tensor_tensor(c.X[:, tiles, :], c.X[:, tiles, :], ytok[:, :, :], ALU.add
                                        ).then_inc(x_ready.sem, 1)

            def statistics(part, tiles):
                for t in range(NT)[tiles]:
                    last = nc.vector.bn_stats(stats[:, t, :], c.X[:, t, :])
                last.then_inc(s_stats, 1)
                dve.wait_ge(s_stats, part)
                for t in range(NT)[tiles]:
                    last = nc.vector.bn_aggr(mv[:, t, :], stats[:, t, :])
                last.then_inc(s_var, 1)
                dve.wait_ge(s_std, part)
                nc.vector.reciprocal(rstd[:, tiles], std[:, tiles]).then_inc(s_rstd, 1)
                dve.wait_ge(s_rstd, part)

            statistics(1, slice(0, TPU))
            choose_up(0)
            dve.wait_ge(psL_read.sem, psL_read.at(0))
            settle(0, chosen[:, 0, :], idx_up, wts_up)
            nc.vector.tensor_tensor(fold[:, :], c.ident[:, 0:NEXP], c.ident[:, NEXP:], ALU.add).then_inc(folded, 1)
            statistics(2, slice(TPU, NT))
            with dve.Fori(1, NS) as s:
                choose_up(s)
            dve.wait_ge(psL_read.sem, psL_read.at(NS - 1))
            settle(1, chosen[:, 1, :], idx_up, wts_up)
            dve.wait_ge(zeroed, 1)
            with dve.Fori(0, NS // 2) as j:
                for v in range(2):
                    weigh(j, v, 0)
                    for q in range(NQ + 1):
                        if q + 1 < NQ:
                            weigh(j, v, q + 1)
                        if q < NQ:
                            first_to_diagonal(j, v, q)
                        if q >= 1:
                            n = q - 1
                            dve.wait_ge(second_done.sem, second_done.at(j, v * NQ + n + 1))
                            dve.wait_ge(hid_ready.sem, hid_ready.at(j, v * NQ + n - 1))
                            nc.vector.scalar_tensor_tensor(
                                hpre[:, n % 2, :, :], ps2[:, n % 2, :].rearrange("p (a b) -> p a b", b=R32),
                                c.scales[:, 0:1], c.bup[:, :].unsqueeze(1).to_broadcast([P, 16, R32]),
                                ALU.mult, ALU.add).then_inc(hpre_ready.sem, 1)
                    settle(v, one(chosen[:, ds(2 * j + (2 + v), 1), :]), idx_up, wts_up)
                    route(2 * j + (NS + v))
                    settle(2 + v, psL[:, 0:NG * 4], idx_down, psL_read)
                hidden_to_diagonal(j, 0)
                for e in range(2 * NQ + 2):
                    p, q = 2 + e // NQ, e % NQ
                    if e == 0:
                        weigh(j, p, q)
                    if e + 1 < 2 * NQ:
                        hidden_to_diagonal(j, e + 1)
                    if e + 1 < 2 * NQ:
                        weigh(j, 2 + (e + 1) // NQ, (e + 1) % NQ)
                    if e < 2 * NQ:
                        first_to_diagonal(j, p, q)
                    if e % 4 == 1 and e > 4:
                        n = e // 4 - 1
                        dve.wait_ge(yt_done.sem, yt_done.at(j, 4 * (n + 1)))
                        dve.wait_ge(y_stored.sem, y_stored.at(j, n // 2 * 16))
                        nc.vector.scalar_tensor_tensor(
                            y[:, n % 2 * 16:(n % 2 + 1) * 16, :], psY[:, :].rearrange("p (a b) -> p a b", b=R32),
                            c.scales[:, 1:2], c.bdn[:, :].unsqueeze(1).to_broadcast([P, 16, R32]),
                            ALU.mult, ALU.add).then_inc(y_ready.sem, 1)
                    if e == NQ + 4:
                        add(j, 0)
                add(j, 1)
            dve.wait_ge(x_ready.sem, x_ready.at(NS // 2 - 1))


class Norm:

    def __init__(self, nc, c, r):
        self.nc, self.c = nc, c
        self.stats, self.mv = r.sb("stats", [P, TPS, 6]), r.sb("mv", [P, TPS, 2])
        self.std, self.rstd = r.sb("std", [P, TPS]), r.sb("rstd", [P, TPS])
        self.xn, self.xnT, self.psT = r.sb("xn", [P, TPS, P]), r.sb("xnT", [P, L]), r.ps("psT", [P, L])
        self.stat_ready, self.var_ready, self.std_ready, self.rstd_ready, self.xn_ready, self.t_done, self.ready = (
            r.sig(n) for n in ("stat", "var", "std", "rstd", "xn", "t", "xnT"))


    def statistics(self, dve, b):
        for t in range(TPS):
            last = self.nc.vector.bn_stats(self.stats[:, t, :], one(self.c.X[:, ds(b * TPS + t, 1), :]))
        last.then_inc(self.stat_ready.sem, 1)
        dve.wait_ge(self.stat_ready.sem, self.stat_ready.at(b))
        dve.sem_inc(self.c.passed, 1)
        for t in range(TPS):
            last = self.nc.vector.bn_aggr(self.mv[:, t, :], self.stats[:, t, :])
        last.then_inc(self.var_ready.sem, 1)

    def root(self, act, b):
        act.wait_ge(self.var_ready.sem, self.var_ready.at(b))
        self.nc.scalar.activation(self.std[:, :], self.mv[:, :, 1], ACT.Sqrt, bias=self.c.eps[:, :],
                                  scale=1.0).then_inc(self.std_ready.sem, 1)

    def apply(self, dve, b):
        dve.wait_ge(self.std_ready.sem, self.std_ready.at(b))
        self.nc.vector.reciprocal(self.rstd[:, :], self.std[:, :]).then_inc(self.rstd_ready.sem, 1)
        dve.wait_ge(self.t_done.sem, self.t_done.before(b))
        dve.wait_ge(self.rstd_ready.sem, self.rstd_ready.at(b))
        for t in range(TPS):
            last = self.nc.vector.tensor_scalar(self.xn[:, t, :], one(self.c.X[:, ds(b * TPS + t, 1), :]),
                                                self.mv[:, t, 0:1], self.rstd[:, t:t + 1], ALU.subtract, ALU.mult)
        last.then_inc(self.xn_ready.sem, 1)

    def turn(self, pe, b):
        pe.wait_ge(self.xn_ready.sem, self.xn_ready.at(b))
        pe.wait_ge(self.ready.sem, self.ready.before(b))
        for t in range(TPS):
            last = self.nc.tensor.transpose(self.psT[:, t * P:(t + 1) * P], self.xn[:, t, :], self.c.ident)
        last.then_inc(self.t_done.sem, 1)

    def turned(self, act, b, used):
        act.wait_ge(self.t_done.sem, self.t_done.at(b))
        act.wait_ge(used.sem, used.before(b))
        self.nc.scalar.activation(self.xnT[:, :], self.psT[:, :], ACT.Copy).then_inc(self.ready.sem, 1)


def plastic_attention(nc, c):
    with ExitStack() as ctx:
        r = Room(nc, ctx, "s_")
        norm = Norm(nc, c, r)
        wq, wk = r.sb("wq", [P, HD, P]), r.sb("wk", [P, HD, P])
        keep, gain = r.sb("keep", [P, HD]), r.sb("gain", [P, HD])
        v = r.sb("v", [P, L])
        heb, state, syn = (r.sb(n, [P, 2, L]) for n in ("heb", "state", "syn"))
        z, y = r.sb("z", [P, 4, L]), r.sb("y", [P, L])
        xb = r.sb("xb", [P, TPS, P])
        psV, psO = r.ps("psV", [P, L]), r.ps("psO", [P, L])
        psK, psQ = r.ps("psK", [P, 2, L]), r.ps("psQ", [P, 2, L])
        v_done, v_ready, k_done, q_done = r.sig("vd"), r.sig("v"), r.sig("kd", HD), r.sig("qd", HD)
        heb_ready, state_ready, syn_ready, z_ready = (r.sig(n, HD) for n in ("heb", "st", "syn", "z"))
        y_added, o_done = r.sig("y", HD - 1), r.sig("o")
        used, xb_ready, x_ready = r.sig("used"), r.sig("xb"), r.sig("x")
        w_ready, sig_ready, set_up = r.sem("w"), r.sem("sg"), r.sem("setup")
        static, lam, gamma = (c.stp[:, n * HD:(n + 1) * HD] for n in range(3))
        block = ctx.enter_context(nc.Block())

        @block.tensor
        def _(pe):
            def keys(b, j):
                pe.wait_ge(heb_ready.sem, heb_ready.at(b, j - 1))
                nc.tensor.matmul(psK[:, j % 2, :], wk[:, j, :], norm.xnT[:, :], start=True, stop=True
                                 ).then_inc(k_done.sem, 1)

            def begin(b):
                pe.wait_ge(norm.ready.sem, norm.ready.at(b))
                pe.wait_ge(v_ready.sem, v_ready.before(b))
                nc.tensor.matmul(psV[:, :], c.Wqkv[:, 2 * P:3 * P], norm.xnT[:, :], start=True, stop=True
                                 ).then_inc(v_done.sem, 1)
                keys(b, 0)

            def sequence(b, prior, more):
                for j in range(HD + 2):
                    if j < HD:
                        if j > 0:
                            keys(b, j)
                        pe.wait_ge(z_ready.sem, z_ready.at(b, j - 1))
                        last = nc.tensor.matmul(psQ[:, j % 2, :], wq[:, j, :], norm.xnT[:, :], start=True, stop=True)
                        last.then_inc(q_done.sem, 1)
                    if j == HD - 1:
                        pe.drain().then_inc(used.sem, 1)
                    if j == HD and more:
                        norm.turn(pe, b + 1)
                    if j == HD + 1 and more:
                        begin(b + 1)
                    if j == 1 and prior:
                        project(b - 1)

            def project(b):
                pe.wait_ge(y_added.sem, y_added.at(b))
                pe.wait_ge(x_ready.sem, x_ready.before(b))
                for t in range(TPS):
                    last = nc.tensor.matmul(psO[:, t * P:(t + 1) * P], y[:, t * P:(t + 1) * P], c.outW[:, :],
                                            start=True, stop=True)
                last.then_inc(o_done.sem, 1)

            pe.wait_ge(w_ready, 2)
            norm.turn(pe, 0)
            begin(0)
            sequence(0, False, True)
            with pe.Fori(1, B - 1) as b:
                sequence(b, True, True)
            sequence(B - 1, True, False)
            project(B - 1)

        @block.scalar
        def _(act):
            nc.scalar.activation(keep[:, :], lam, ACT.Sigmoid).then_inc(sig_ready, 1)
            norm.root(act, 0)
            norm.turned(act, 0, used)

            def sequence(b, more):
                act.wait_ge(v_done.sem, v_done.at(b))
                act.wait_ge(heb_ready.sem, heb_ready.before(b))
                nc.scalar.activation(v[:, :], psV[:, :], ACT.Identity, bias=c.bqkv[:, 0:1]).then_inc(v_ready.sem, 1)
                for j in range(HD):
                    act.wait_ge(state_ready.sem, state_ready.at(b, j + 1))
                    act.wait_ge(z_ready.sem, z_ready.at(b, j - 1))
                    nc.scalar.activation(syn[:, j % 2, :], state[:, j % 2, :], ACT.Identity, bias=static[:, j:j + 1],
                                         scale=gain[:, j:j + 1]).then_inc(syn_ready.sem, 1)
                    if j == 4 and more:
                        norm.root(act, b + 1)
                if more:
                    norm.turned(act, b + 1, used)

            act.wait_ge(set_up, 2)
            with act.Fori(0, B - 1) as b:
                sequence(b, True)
            sequence(B - 1, False)

        @block.gpsimd
        def _(pool):
            r.seed(pool)

            def sequence(b):
                for j in range(1, HD):
                    pool.wait_ge(z_ready.sem, z_ready.at(b, j + 1))
                    if j == 1:
                        pool.wait_ge(o_done.sem, o_done.before(b))
                    else:
                        pool.wait_ge(y_added.sem, y_added.at(b, j - 1))
                    nc.gpsimd.tensor_tensor(y[:, :], z[:, 0, :] if j == 1 else y[:, :], z[:, j % 4, :], ALU.add
                                            ).then_inc(y_added.sem, 1)
                pool.wait_ge(x_ready.sem, x_ready.before(b))
                nc.gpsimd.tensor_tensor(xb[:, :, :], c.X[:, ds(b * TPS, TPS), :],
                                        c.rows[:, 3, :].unsqueeze(1).to_broadcast([P, TPS, P]),
                                        ALU.add).then_inc(xb_ready.sem, 1)

            with pool.Fori(0, B) as b:
                sequence(b)

        @block.vector
        def _(dve):
            for dst, at in ((wq, 0), (wk, P)):
                nc.vector.tensor_copy(
                    dst[:, :, :].rearrange("p j (h i) -> p j h i", h=H),
                    c.Wqkv[:, at:at + P].rearrange("p (h j) -> p j h", h=H).unsqueeze(3).to_broadcast([P, HD, H, HD])
                ).then_inc(w_ready, 1)
            nc.vector.tensor_scalar(gain[:, :], gamma, QSCALE, None, ALU.mult).then_inc(set_up, 1)
            dve.wait_ge(sig_ready, 1)
            nc.vector.tensor_scalar(keep[:, :], keep[:, :], -1.0, 1.0, ALU.mult, ALU.add).then_inc(set_up, 1)
            dve.wait_ge(set_up, 2)
            norm.statistics(dve, 0)
            norm.apply(dve, 0)

            def residual(b):
                dve.wait_ge(o_done.sem, o_done.at(b))
                dve.wait_ge(xb_ready.sem, xb_ready.at(b))
                nc.vector.tensor_tensor(c.X[:, ds(b * TPS, TPS), :], psO[:, :].rearrange("p (t c) -> p t c", c=P),
                                        xb[:, :, :], ALU.add).then_inc(x_ready.sem, 1)

            def sequence(b, prior, more):
                for j in range(HD + 2):
                    if j >= 2:
                        n = j - 2
                        dve.wait_ge(syn_ready.sem, syn_ready.at(b, n + 1))
                        dve.wait_ge(q_done.sem, q_done.at(b, n + 1))
                        dve.wait_ge(y_added.sem, y_added.at(b, max(n - 4, 1)) if n >= 4 else y_added.before(b, n + 4))
                        nc.vector.scalar_tensor_tensor(z[:, n % 4, :], psQ[:, n % 2, :], c.bqkv[:, 2 + n:3 + n],
                                                       syn[:, n % 2, :], ALU.add, ALU.mult).then_inc(z_ready.sem, 1)
                    if j < HD:
                        dve.wait_ge(k_done.sem, k_done.at(b, j + 1))
                        if j == 0:
                            dve.wait_ge(v_ready.sem, v_ready.at(b))
                        dve.wait_ge(state_ready.sem, state_ready.at(b, j - 1))
                        nc.vector.scalar_tensor_tensor(heb[:, j % 2, :], psK[:, j % 2, :],
                                                       c.bqkv[:, 2 + HD + j:3 + HD + j], v[:, :], ALU.add, ALU.mult
                                                       ).then_inc(heb_ready.sem, 1)
                    if j < HD:
                        dve.wait_ge(heb_ready.sem, heb_ready.at(b, j + 1))
                        dve.wait_ge(syn_ready.sem, syn_ready.at(b, j - 1))
                        nc.vector.tensor_tensor_scan(state[:, j % 2, :], keep[:, j:j + 1].to_broadcast([P, L]),
                                                     heb[:, j % 2, :], 0.0, ALU.mult, ALU.add
                                                     ).then_inc(state_ready.sem, 1)
                    if j == 3 and more:
                        norm.statistics(dve, b + 1)
                    if j == 6 and more:
                        norm.apply(dve, b + 1)
                    if j == 2 and prior:
                        residual(b - 1)

            sequence(0, False, True)
            with dve.Fori(1, B - 1) as b:
                sequence(b, True, True)
            sequence(B - 1, True, False)
            residual(B - 1)
            dve.wait_ge(x_ready.sem, x_ready.at(B - 1))


def gated_feed_forward(nc, c, out):
    with ExitStack() as ctx:
        r = Room(nc, ctx, "f_")
        norm = Norm(nc, c, r)
        gated, hidden = r.sb("gated", [P, 2, L]), r.sb("hidden", [P, HM, L])
        res = r.sb("res", [P, 2, L])
        psG, psU, psO = r.ps("psG", [P, 2, L]), r.ps("psU", [P, 2, L]), r.ps("psO", [P, L])
        g_done, u_done, gated_ready, hidden_ready = (r.sig(n, HM) for n in ("g", "u", "gt", "h"))
        used, o_done, x_ready, stored = r.sig("used"), r.sig("o"), r.sig("x"), r.sig("out", 16)

        block = ctx.enter_context(nc.Block())

        @block.sync
        def _(sp):
            with sp.Fori(0, B) as b:
                sp.wait_ge(x_ready.sem, x_ready.at(b))
                sp.sem_inc(c.passed, 1)
                sp.dma_start(out[ds(b * L, L), :].rearrange("(t p) c -> p t c", p=P),
                             c.X[:, ds(b * TPS, TPS), :]).then_inc(stored.sem, 16)
            sp.wait_ge(stored.sem, stored.at(B - 1))

        @block.tensor
        def _(pe):
            norm.turn(pe, 0)

            def sequence(b, more):
                pe.wait_ge(norm.ready.sem, norm.ready.at(b))
                for m in range(HM):
                    pe.wait_ge(gated_ready.sem, gated_ready.at(b, m - 1))
                    nc.tensor.matmul(psG[:, m % 2, :], c.Wint[:, m * P:(m + 1) * P], norm.xnT[:, :],
                                     start=True, stop=True).then_inc(g_done.sem, 1)
                    pe.wait_ge(hidden_ready.sem, hidden_ready.at(b, m - 1))
                    last = nc.tensor.matmul(psU[:, m % 2, :], c.Wint[:, (HM + m) * P:(HM + m + 1) * P],
                                            norm.xnT[:, :], start=True, stop=True)
                    last.then_inc(u_done.sem, 1)
                pe.drain().then_inc(used.sem, 1)
                if more:
                    norm.turn(pe, b + 1)
                pe.wait_ge(hidden_ready.sem, hidden_ready.at(b))
                pe.wait_ge(x_ready.sem, x_ready.before(b))
                for t in range(TPS):
                    for m in range(HM):
                        last = nc.tensor.matmul(psO[:, t * P:(t + 1) * P], hidden[:, m, t * P:(t + 1) * P],
                                                c.Wint[:, (2 * HM + m) * P:(2 * HM + m + 1) * P],
                                                start=(m == 0), stop=(m == HM - 1))
                last.then_inc(o_done.sem, 1)

            with pe.Fori(0, B - 1) as b:
                sequence(b, True)
            sequence(B - 1, False)

        @block.scalar
        def _(act):
            norm.root(act, 0)
            norm.turned(act, 0, used)

            def sequence(b, more):
                if more:
                    norm.root(act, b + 1)
                for m in range(HM):
                    act.wait_ge(g_done.sem, g_done.at(b, m + 1))
                    act.wait_ge(hidden_ready.sem, hidden_ready.at(b, m - 1))
                    nc.scalar.activation(gated[:, m % 2, :], psG[:, m % 2, :], ACT.Silu).then_inc(gated_ready.sem, 1)
                if more:
                    norm.turned(act, b + 1, used)

            with act.Fori(0, B - 1) as b:
                sequence(b, True)
            sequence(B - 1, False)

        @block.gpsimd
        def _(pool):
            r.seed(pool)

        @block.vector
        def _(dve):
            norm.statistics(dve, 0)
            norm.apply(dve, 0)

            def sequence(b, more):
                if more:
                    norm.statistics(dve, b + 1)
                    norm.apply(dve, b + 1)
                for m in range(HM):
                    dve.wait_ge(gated_ready.sem, gated_ready.at(b, m + 1))
                    dve.wait_ge(u_done.sem, u_done.at(b, m + 1))
                    dve.wait_ge(o_done.sem, o_done.before(b))
                    nc.vector.tensor_tensor(hidden[:, m, :], psU[:, m % 2, :], gated[:, m % 2, :], ALU.mult
                                            ).then_inc(hidden_ready.sem, 1)
                dve.wait_ge(o_done.sem, o_done.at(b))
                nc.vector.tensor_tensor(c.X[:, ds(b * TPS, TPS), :], psO[:, :].rearrange("p (t c) -> p t c", c=P),
                                        c.X[:, ds(b * TPS, TPS), :], ALU.add).then_inc(x_ready.sem, 1)

            with dve.Fori(0, B - 1) as b:
                sequence(b, True)
            sequence(B - 1, False)


def build(nc, a, out):
    scratch = {
        "kd": ((B, P, 3, L), BF16),
        "qd": ((B, P, TPS * H * KROWS), BF16),
        "posd": ((P, L), BF16),
        "xnd": ((N * P,), F32),
        "yd": ((N * P,), F32),
    }
    kd, qd, posd, xnd, yd = (nc.dram_tensor(n, s, d).ap() for n, (s, d) in scratch.items())
    with ExitStack() as ctx:
        c = Room(nc, ctx, "c_")
        c.passed = c.sem("passed")
        c.X = c.sb("X", [P, NT, P])
        c.consts = c.sb("consts", [P, 3 * P + NG + 2])
        c.ident = c.consts[:, 0:P]
        c.sel4 = c.consts[:, 2 * P:3 * P]
        c.grp = c.consts[:, 3 * P:3 * P + NG]
        c.slot1 = c.consts[:, 3 * P + NG:3 * P + NG + 1]
        c.row32 = c.consts[:, 3 * P + NG + 1:3 * P + NG + 2]
        c.iota1 = c.sb("iota1", [P, P], BF16)
        c.ones, c.eps, c.mean_ones = c.sb("ones", [P, 1]), c.sb("eps", [P, 1]), c.sb("mean_ones", [P, P])
        c.W, c.rows, c.cols = c.sb("W", [P, 4, P]), c.sb("rows", [P, 4, P]), c.sb("cols", [P, 1])
        c.Wint = c.sb("Wint", [P, 3 * HM * P])
        c.WupR, c.WdR = c.sb("WupR", [P, ROWTOK * NEXP]), c.sb("WdR", [P, 32 * NEXP])
        c.scales, c.bup, c.bdn = c.sb("scales", [P, 2]), c.sb("bup", [P, 32]), c.sb("bdn", [P, 32])
        c.Wqkv, c.outW, c.bqkv, c.stp = (c.sb("Wqkv", [P, 3 * P]), c.sb("outW", [P, P]),
                                         c.sb("bqkv", [P, 2 + 2 * HD]), c.sb("stp", [P, 3 * HD]))
        load(nc, c, a)
        with ExitStack() as att:
            t = Room(nc, att, "c0_")
            c.V, c.VM, c.QN, c.posT = (t.sb("V", [P, B, L]), t.sb("VM", [P, B, P]), t.sb("QN", [P, TPS, P]),
                                       t.sb("posT", [P, TPS, P]))
            attention_projections(nc, c, kd, qd)
            attention(nc, c, kd, qd, posd)
        experts(nc, c, a, xnd, yd)
        plastic_attention(nc, c)
        gated_feed_forward(nc, c, out)


def kernel(**inputs):
    import numpy as _np
    import concourse.bacc as _bacc
    from concourse import mybir as _mybir
    from concourse.bass_utils import run_bass_kernel_spmd as _run

    def turned(name):
        return inputs[name].T

    i = {k: _np.asarray(v) for k, v in inputs.items()}
    n = _np.arange(P)
    consts = _np.concatenate([
        _np.eye(P), _np.tile(n + 1.0, (P, 1)), n[:, None] % G4 == n[None, :] // 32,
        n[:, None] // G4 == _np.arange(NG)[None, :], n[:, None] + 1.0, n[:, None] % 32,
    ], axis=1).astype(_np.float32)
    arrays = {
        "x": i["L0_attn_x"].reshape(N, P), "consts": consts,
        "WqT": i["L0_attn_Wq"].T, "WkT": i["L0_attn_Wk"].T, "WvT": i["L0_attn_Wv"].T, "WoT": i["L0_attn_Wo"].T,
        "bq": i["L0_attn_bq"], "bk": i["L0_attn_bk"].reshape(P, 1), "bv": i["L0_attn_bv"], "bo": i["L0_attn_bo"],
        "WupR": i["L0_ffn_W_up"].reshape(NEXP, ROWTOK, P).transpose(2, 1, 0).reshape(P, -1),
        "tab_up": _np.concatenate([i["L0_ffn_A_up"].transpose(0, 2, 1), i["L0_ffn_B_up"].transpose(0, 2, 1)],
                                  axis=2).reshape(NEXP * 32, P),
        "tab_down": _np.concatenate([
            i[f"L0_ffn_{m}_down"].transpose(0, 2, 1).reshape(NEXP, 2, 32, 32).transpose(0, 2, 1, 3)
            .reshape(NEXP, 32, 64)
            for m in "AB"], axis=2).reshape(NEXP * 32, P),
        "bias_up": i["L0_ffn_bias_up"].reshape(2, 32, 64).transpose(0, 2, 1).reshape(P, 32),
        "bias_down": i["L0_ffn_bias_down"].reshape(32, 32),
        "scale_up": i["L0_ffn_scale_up"], "scale_down": i["L0_ffn_scale_down"],
        "WdR": i["L0_ffn_W_down"].reshape(NEXP, 2, 32, 64).transpose(1, 3, 2, 0).reshape(P, -1),
        "WqkvT": i["L1_attn_Wqkv_w"].T, "out_wT": i["L1_attn_out_w"].T, "out_b": i["L1_attn_out_b"],
        "bqkv": _np.concatenate([
            i["L1_attn_Wqkv_b"][2 * P:].reshape(P, 1), i["L1_attn_Wqkv_b"][2 * P:].reshape(P, 1),
            _np.repeat(i["L1_attn_Wqkv_b"][:P].reshape(H, HD), HD, axis=0),
            _np.repeat(i["L1_attn_Wqkv_b"][P:2 * P].reshape(H, HD), HD, axis=0)], axis=1),
        "stp": _np.concatenate([i[f"L1_attn_{m}"].reshape(P, HD) for m in ("W_static", "Lambda_raw", "Gamma")], axis=1),
        "w_gateT": i["L1_ffn_w_gate"].T, "w_upT": i["L1_ffn_w_up"].T, "w_downT": i["L1_ffn_w_down"].T,
    }
    arrays = {f"in_{k}": _np.ascontiguousarray(v) for k, v in arrays.items()}
    nc = _bacc.Bacc("TRN2", target_bir_lowering=False, num_devices=1)
    a = {k[3:]: nc.dram_tensor(k, v.shape, _mybir.dt.from_np(v.dtype), kind="ExternalInput").ap()
         for k, v in arrays.items()}
    out = nc.dram_tensor("out_x", (N, P), F32, kind="ExternalOutput").ap()
    build(nc, a, out)
    r = _run(nc, [arrays], core_ids=[0])
    return r.results[0]["out_x"].reshape(B, L, P)
```
